# Optimizing a Trainium2 kernel written in Bass

```python
import numpy as np
import jax
import jax.numpy as jnp

def _softmax(x, axis=-1):
    return jax.nn.softmax(x, axis=axis)

def _gelu(x):
    return jax.nn.gelu(x, approximate=True)

def _silu(x):
    return jax.nn.silu(x)

def _sigmoid(x):
    return jax.nn.sigmoid(x)

def _layernorm(x, axis=-1, eps=1e-05):
    m = jnp.mean(x, axis=axis, keepdims=True)
    v = jnp.var(x, axis=axis, keepdims=True)
    return (x - m) / jnp.sqrt(v + eps)

def _scatter_add(tgt, idx, src, axis=0):
    return tgt.at[idx].add(src)

def _segment_sum(src, seg, n):
    return jax.ops.segment_sum(src, seg, n)
kernel_name = 'mk_adj_ffn_d4_adj_r2_01db31'

def setup_inputs(seed: int=0):
    np.random.seed(seed)
    _w = jnp.asarray

    def _rec_inputs():
        import jax
        import jax.numpy as jnp
        _gk = jax.random.key(seed)
        x = -0.0005207 + 1.001 * jax.random.normal(jax.random.fold_in(_gk, 1), (2048, 128), jnp.float32)
        _w = (1.0 + jnp.arange(2048, dtype=jnp.float32)) ** (-0.5)
        _w = _w / _w.mean()
        _pij = jnp.clip(0.0078125 * _w[:, None] * _w[None, :], 0.0, 1.0)
        _a = jax.random.uniform(jax.random.fold_in(_gk, 2), (2048, 2048)) < _pij
        adj = _a.astype(jnp.int32)
        return (x, adj)
    x, adj = _rec_inputs()

    def _L0_gnn_setup():
        import jax, jax.numpy as jnp
        import numpy as np
        ALPHA = 0.2
        NEG_FILL = -9000000000000000.0
        key = jax.random.key(seed)
        k_h, k_adj, k_W, k_a = jax.random.split(key, 4)
        N, D_IN, D_OUT = (4096, 128, 128)
        h = jax.random.normal(k_h, (N, D_IN), dtype=jnp.float32)
        adj = jax.random.randint(k_adj, (N, N), 0, 2, dtype=jnp.int32)
        W = jax.random.normal(k_W, (D_IN, D_OUT), dtype=jnp.float32) * (1.414 * np.sqrt(2.0 / (D_IN + D_OUT)))
        a = jax.random.normal(k_a, (2 * D_OUT, 1), dtype=jnp.float32) * (1.414 * np.sqrt(2.0 / (2 * D_OUT + 1)))
        return {'h': h, 'adj': adj, 'W': W, 'a': a}
    _L0_gnn_all = _L0_gnn_setup()
    _L0_gnn_in = {k: v for k, v in _L0_gnn_all.items() if k in ('W', 'a')}
    del _L0_gnn_all

    def _L0_ffn_setup():
        import jax, jax.numpy as jnp
        import numpy as np
        B, S, D, E, H, K = (4, 2048, 128, 8, 256, 2)
        key = jax.random.key(seed)
        ks = jax.random.split(key, 6)
        x = jax.random.normal(ks[0], (B, S, D), jnp.float32)
        Wg = jax.random.normal(ks[1], (D, E), jnp.float32) * 0.02
        bg = jnp.zeros((E,), jnp.float32)
        W1 = jax.random.normal(ks[2], (E, D, H), jnp.float32) * 0.02
        b1 = jnp.zeros((E, H), jnp.float32)
        W2 = jax.random.normal(ks[3], (E, H, D), jnp.float32) * 0.02
        b2 = jnp.zeros((E, D), jnp.float32)
        return {'x': x, 'Wg': Wg, 'bg': bg, 'W1': W1, 'b1': b1, 'W2': W2, 'b2': b2}
    _L0_ffn_all = _L0_ffn_setup()
    _L0_ffn_in = {k: v for k, v in _L0_ffn_all.items() if k in ('Wg', 'bg', 'W1', 'b1', 'W2', 'b2')}
    del _L0_ffn_all

    def _L1_gnn_setup():
        import jax, jax.numpy as jnp
        import numpy as np
        NEG = -9000000000000000.0
        key = jax.random.key(seed)
        k1, k2, k3, k4 = jax.random.split(key, 4)
        N, F_IN, F_OUT = (4096, 128, 128)
        h = jax.random.normal(k1, (N, F_IN), dtype=jnp.float32)
        adj = jax.random.randint(k2, (N, N), 0, 2, dtype=jnp.int32)
        W = jax.random.normal(k3, (F_IN, F_OUT), dtype=jnp.float32) * (1.0 / np.sqrt(F_IN))
        a = jax.random.normal(k4, (2 * F_OUT,), dtype=jnp.float32) * (1.0 / np.sqrt(2 * F_OUT))
        return {'h': h, 'adj': adj, 'W': W, 'a': a}
    _L1_gnn_all = _L1_gnn_setup()
    _L1_gnn_in = {k: v for k, v in _L1_gnn_all.items() if k in ('W', 'a')}
    del _L1_gnn_all

    def _L1_ffn_setup():
        import jax, jax.numpy as jnp
        import numpy as np
        D_MODEL = 128
        D_STATE = 64
        D_CONV = 4
        EXPAND = 2
        HEADDIM = 64
        D_INNER = EXPAND * D_MODEL
        NHEADS = D_INNER // HEADDIM
        CONV_DIM = D_INNER + 2 * D_STATE
        D_IN_PROJ = 2 * D_INNER + 2 * D_STATE + NHEADS
        CHUNK = 128
        EPS = 1e-05

        def segsum(a):
            T = a.shape[-1]
            cs = jnp.cumsum(a, axis=-1)
            ss = cs[..., :, None] - cs[..., None, :]
            mask = jnp.tril(jnp.ones((T, T), dtype=bool))
            return jnp.where(mask, ss, -jnp.inf)

        def mamba2_block(x, W_in, conv_w, conv_b, dt_bias, A_log, D, norm_w, W_out, W_lin, b_lin):
            Bsz, L, _ = x.shape
            zxbcdt = x @ W_in
            z, xBC, dt = jnp.split(zxbcdt, [D_INNER, D_INNER + CONV_DIM], axis=-1)
            xp = jnp.pad(xBC, ((0, 0), (D_CONV - 1, 0), (0, 0)))
            conv = conv_b + sum((xp[:, k:k + L, :] * conv_w[:, k] for k in range(D_CONV)))
            xBC = jax.nn.silu(conv)
            xh, Bmat, Cmat = jnp.split(xBC, [D_INNER, D_INNER + D_STATE], axis=-1)
            dt = jax.nn.softplus(dt + dt_bias)
            A = -jnp.exp(A_log)
            nc = L // CHUNK
            xh = xh.reshape(Bsz, nc, CHUNK, NHEADS, HEADDIM)
            Bc = Bmat.reshape(Bsz, nc, CHUNK, D_STATE)
            Cc = Cmat.reshape(Bsz, nc, CHUNK, D_STATE)
            dtc = dt.reshape(Bsz, nc, CHUNK, NHEADS)
            dA = jnp.einsum('bclh,h->bhcl', dtc, A)
            A_cum = jnp.cumsum(dA, axis=-1)
            Lmat = jnp.exp(segsum(dA))
            xdt = xh * dtc[..., None]
            Y_diag = jnp.einsum('bcln,bcsn,bhcls,bcshp->bclhp', Cc, Bc, Lmat, xdt)
            decay_states = jnp.exp(A_cum[..., -1:] - A_cum)
            states = jnp.einsum('bcln,bhcl,bclhp->bchpn', Bc, decay_states, xdt)
            chunk_decay = jnp.exp(A_cum[..., -1])

            def step(h, inp):
                s, d = inp
                return (h * d[..., None, None] + s, h)
            _, prevs = jax.lax.scan(step, jnp.zeros_like(states[:, 0]), (jnp.moveaxis(states, 1, 0), jnp.moveaxis(chunk_decay, 2, 0)))
            prevs = jnp.moveaxis(prevs, 0, 1)
            Y_off = jnp.einsum('bcln,bchpn,bhcl->bclhp', Cc, prevs, jnp.exp(A_cum))
            Y = (Y_diag + Y_off + xh * D[:, None]).reshape(Bsz, L, D_INNER)
            Y = Y * jax.nn.silu(z)
            Y = Y * jax.lax.rsqrt(jnp.mean(Y * Y, axis=-1, keepdims=True) + EPS) * norm_w
            out = Y @ W_out
            return out @ W_lin + b_lin
        key = jax.random.key(seed)
        ks = jax.random.split(key, 12)
        B, L = (8, 2048)

        def gauss(k, shape, scale):
            return jax.random.normal(k, shape, dtype=jnp.float32) * scale
        return {'x': gauss(ks[0], (B, L, D_MODEL), 1.0), 'W_in': gauss(ks[1], (D_MODEL, D_IN_PROJ), D_MODEL ** (-0.5)), 'conv_w': gauss(ks[2], (CONV_DIM, D_CONV), 0.3), 'conv_b': gauss(ks[3], (CONV_DIM,), 0.1), 'dt_bias': jax.random.uniform(ks[4], (NHEADS,), minval=-4.0, maxval=-1.0), 'A_log': jnp.log(jax.random.uniform(ks[5], (NHEADS,), minval=1.0, maxval=16.0)), 'D': jnp.ones((NHEADS,), jnp.float32), 'norm_w': jnp.ones((D_INNER,), jnp.float32), 'W_out': gauss(ks[6], (D_INNER, D_MODEL), D_INNER ** (-0.5)), 'W_lin': gauss(ks[7], (D_MODEL, D_MODEL), D_MODEL ** (-0.5)), 'b_lin': jnp.zeros((D_MODEL,), jnp.float32)}
    _L1_ffn_all = _L1_ffn_setup()
    _L1_ffn_in = {k: v for k, v in _L1_ffn_all.items() if k in ('W_in', 'conv_w', 'conv_b', 'dt_bias', 'A_log', 'D', 'norm_w', 'W_out', 'W_lin', 'b_lin')}
    del _L1_ffn_all

    def _L2_gnn_setup():
        import jax, jax.numpy as jnp
        import numpy as np
        N = 8192
        F_IN = 128
        F_OUT = 128
        key = jax.random.key(seed)
        k1, k2, k3 = jax.random.split(key, 3)
        x = jax.random.normal(k1, (N, F_IN), dtype=jnp.float32)
        adj = jax.random.randint(k2, (N, N), 0, 2, dtype=jnp.int32)
        stdv = np.sqrt(6.0 / (2 * F_IN + F_OUT)).astype(np.float32)
        weight = jax.random.uniform(k3, (2 * F_IN, F_OUT), dtype=jnp.float32, minval=-stdv, maxval=stdv)
        bias = jnp.zeros((F_OUT,), dtype=jnp.float32)
        return {'x': x, 'adj': adj, 'weight': weight, 'bias': bias}
    _L2_gnn_all = _L2_gnn_setup()
    _L2_gnn_in = {k: v for k, v in _L2_gnn_all.items() if k in ('weight', 'bias')}
    del _L2_gnn_all

    def _L2_ffn_setup():
        import jax, jax.numpy as jnp
        import numpy as np
        B, S, D, H, E, K = (8, 4096, 128, 512, 8, 2)
        key = jax.random.key(seed)
        ks = jax.random.split(key, 7)
        s_in = 1.0 / np.sqrt(D)
        s_hid = 1.0 / np.sqrt(H)
        return {'x': jax.random.normal(ks[0], (B, S, D), dtype=jnp.float32), 'Wg': jax.random.uniform(ks[1], (E, D), jnp.float32, -s_in, s_in), 'bg': jax.random.uniform(ks[2], (E,), jnp.float32, -s_in, s_in), 'W1': jax.random.uniform(ks[3], (E, H, D), jnp.float32, -s_in, s_in), 'b1': jax.random.uniform(ks[4], (E, H), jnp.float32, -s_in, s_in), 'W2': jax.random.uniform(ks[5], (E, D, H), jnp.float32, -s_hid, s_hid), 'b2': jax.random.uniform(ks[6], (E, D), jnp.float32, -s_hid, s_hid)}
    _L2_ffn_all = _L2_ffn_setup()
    _L2_ffn_in = {k: v for k, v in _L2_ffn_all.items() if k in ('Wg', 'bg', 'W1', 'b1', 'W2', 'b2')}
    del _L2_ffn_all

    def _L3_gnn_setup():
        import jax, jax.numpy as jnp
        import numpy as np
        N, FEAT = (4096, 128)
        ALPHA = 0.2
        NEG_INF = jnp.float32(-1000000000000.0)
        key = jax.random.key(seed)
        k0, k1, k2, k3, k4 = jax.random.split(key, 5)
        inp = jax.random.normal(k0, (N, FEAT), dtype=jnp.float32)
        adj = jax.random.randint(k1, (N, N), 0, 2, dtype=jnp.int32)
        W = jax.random.normal(k2, (FEAT, FEAT), dtype=jnp.float32) * 0.05
        a = jax.random.normal(k3, (2 * FEAT, 1), dtype=jnp.float32) * 0.05
        wtrans = jax.random.normal(k4, (2 * FEAT, FEAT), dtype=jnp.float32) * 0.05
        return {'inp': inp, 'adj': adj, 'W': W, 'a': a, 'wtrans': wtrans}
    _L3_gnn_all = _L3_gnn_setup()
    _L3_gnn_in = {k: v for k, v in _L3_gnn_all.items() if k in ('W', 'a', 'wtrans')}
    del _L3_gnn_all

    def _L3_ffn_setup():
        import jax, jax.numpy as jnp
        import numpy as np
        H, P, G, NS, K = (8, 64, 64, 64, 3)
        D_INNER = H * P
        CONV_DIM = D_INNER + 2 * NS
        D_IN_PROJ = 2 * D_INNER + 2 * NS + 2 * H

        def _hydra(u, in_w, conv_w, conv_b, dt_bias, A_log, Dp, fcD_w, norm_w, out_w):
            Bt, L, _ = u.shape
            zxbcdt = u @ in_w.T
            z = zxbcdt[..., :D_INNER]
            xBC = zxbcdt[..., D_INNER:D_INNER + CONV_DIM]
            dt = zxbcdt[..., -2 * H:]
            dt = jnp.concatenate([dt[..., :H], jnp.flip(dt[..., H:], axis=1)], axis=0)
            dt = jax.nn.softplus(dt + dt_bias)
            xp = jnp.pad(xBC, ((0, 0), (K - 1, 0), (0, 0)))
            xBC = sum((xp[:, k:k + L, :] * conv_w[:, k] for k in range(K))) + conv_b
            xBC = jax.nn.silu(xBC)
            x = xBC[..., :D_INNER]
            Bm = xBC[..., D_INNER:D_INNER + NS]
            Cm = xBC[..., D_INNER + NS:]
            x_og = x
            x2 = jnp.concatenate([x, jnp.flip(x, 1)], 0).reshape(2 * Bt, L, H, P)
            B2 = jnp.concatenate([Bm, jnp.flip(Bm, 1)], 0)
            C2 = jnp.concatenate([Cm, jnp.flip(Cm, 1)], 0)
            dA = jnp.exp(dt * -jnp.exp(A_log))
            dBx = jnp.einsum('blh,bln,blhp->blhpn', dt, B2, x2)

            def step(h, inp):
                dA_t, dBx_t, C_t = inp
                h = h * dA_t[:, :, None, None] + dBx_t
                return (h, jnp.einsum('bhpn,bn->bhp', h, C_t))
            h0 = jnp.zeros((2 * Bt, H, P, NS), u.dtype)
            _, ys = jax.lax.scan(step, h0, (dA.transpose(1, 0, 2), dBx.transpose(1, 0, 2, 3, 4), C2.transpose(1, 0, 2)))
            y = ys.transpose(1, 0, 2, 3).reshape(2 * Bt, L, D_INNER)
            y_fw, y_bw = (y[:Bt], jnp.flip(y[Bt:], 1))
            y = jnp.pad(y_fw[:, :-1], ((0, 0), (1, 0), (0, 0))) + jnp.pad(y_bw[:, 1:], ((0, 0), (0, 1), (0, 0)))
            y = y + x_og * jnp.repeat(x_og @ fcD_w.T + Dp, P, axis=-1)
            yg = y * jax.nn.silu(z)
            yg = yg * jax.lax.rsqrt(jnp.mean(jnp.square(yg), -1, keepdims=True) + 1e-05) * norm_w
            return yg @ out_w.T
        key = jax.random.key(seed)
        ks = jax.random.split(key, 10)
        dim, Bsz, N = (128, 4, 4096)
        s = 0.02
        return {'x': jax.random.normal(ks[0], (Bsz, N, dim), jnp.float32), 'W_fx': jax.random.normal(ks[1], (D_INNER, dim), jnp.float32) * s, 'b_fx': jnp.zeros((D_INNER,), jnp.float32), 'W_x': jax.random.normal(ks[2], (D_INNER, dim), jnp.float32) * s, 'b_x': jnp.zeros((D_INNER,), jnp.float32), 'W_slice': jax.random.normal(ks[3], (G, P), jnp.float32) * s, 'b_slice': jnp.zeros((G,), jnp.float32), 'temperature': jnp.full((1, H, 1, 1), 0.5, jnp.float32), 'hy_in_w': jax.random.normal(ks[4], (D_IN_PROJ, D_INNER), jnp.float32) * s, 'hy_conv_w': jax.random.normal(ks[5], (CONV_DIM, K), jnp.float32) * s, 'hy_conv_b': jnp.zeros((CONV_DIM,), jnp.float32), 'hy_dt_bias': jnp.log(jnp.expm1(jnp.full((H,), 0.01, jnp.float32))), 'hy_A_log': jnp.log(jnp.linspace(1.0, 16.0, H)).astype(jnp.float32), 'hy_D': jnp.ones((H,), jnp.float32), 'hy_fcD_w': jax.random.normal(ks[6], (H, D_INNER), jnp.float32) * s, 'hy_norm_w': jnp.ones((D_INNER,), jnp.float32), 'hy_out_w': jax.random.normal(ks[7], (D_INNER, D_INNER), jnp.float32) * s, 'out_w': jax.random.normal(ks[8], (dim, D_INNER), jnp.float32) * s, 'out_b': jnp.zeros((dim,), jnp.float32)}
    _L3_ffn_all = _L3_ffn_setup()
    _L3_ffn_in = {k: v for k, v in _L3_ffn_all.items() if k in ('W_fx', 'b_fx', 'W_x', 'b_x', 'W_slice', 'b_slice', 'temperature', 'hy_in_w', 'hy_conv_w', 'hy_conv_b', 'hy_dt_bias', 'hy_A_log', 'hy_D', 'hy_fcD_w', 'hy_norm_w', 'hy_out_w', 'out_w', 'out_b')}
    del _L3_ffn_all
    return {'x': x, 'adj': adj, 'L0_gnn_W': _L0_gnn_in['W'], 'L0_gnn_a': _L0_gnn_in['a'], 'L0_ffn_Wg': _L0_ffn_in['Wg'], 'L0_ffn_bg': _L0_ffn_in['bg'], 'L0_ffn_W1': _L0_ffn_in['W1'], 'L0_ffn_b1': _L0_ffn_in['b1'], 'L0_ffn_W2': _L0_ffn_in['W2'], 'L0_ffn_b2': _L0_ffn_in['b2'], 'L1_gnn_W': _L1_gnn_in['W'], 'L1_gnn_a': _L1_gnn_in['a'], 'L1_ffn_W_in': _L1_ffn_in['W_in'], 'L1_ffn_conv_w': _L1_ffn_in['conv_w'], 'L1_ffn_conv_b': _L1_ffn_in['conv_b'], 'L1_ffn_dt_bias': _L1_ffn_in['dt_bias'], 'L1_ffn_A_log': _L1_ffn_in['A_log'], 'L1_ffn_D': _L1_ffn_in['D'], 'L1_ffn_norm_w': _L1_ffn_in['norm_w'], 'L1_ffn_W_out': _L1_ffn_in['W_out'], 'L1_ffn_W_lin': _L1_ffn_in['W_lin'], 'L1_ffn_b_lin': _L1_ffn_in['b_lin'], 'L2_gnn_weight': _L2_gnn_in['weight'], 'L2_gnn_bias': _L2_gnn_in['bias'], 'L2_ffn_Wg': _L2_ffn_in['Wg'], 'L2_ffn_bg': _L2_ffn_in['bg'], 'L2_ffn_W1': _L2_ffn_in['W1'], 'L2_ffn_b1': _L2_ffn_in['b1'], 'L2_ffn_W2': _L2_ffn_in['W2'], 'L2_ffn_b2': _L2_ffn_in['b2'], 'L3_gnn_W': _L3_gnn_in['W'], 'L3_gnn_a': _L3_gnn_in['a'], 'L3_gnn_wtrans': _L3_gnn_in['wtrans'], 'L3_ffn_W_fx': _L3_ffn_in['W_fx'], 'L3_ffn_b_fx': _L3_ffn_in['b_fx'], 'L3_ffn_W_x': _L3_ffn_in['W_x'], 'L3_ffn_b_x': _L3_ffn_in['b_x'], 'L3_ffn_W_slice': _L3_ffn_in['W_slice'], 'L3_ffn_b_slice': _L3_ffn_in['b_slice'], 'L3_ffn_temperature': _L3_ffn_in['temperature'], 'L3_ffn_hy_in_w': _L3_ffn_in['hy_in_w'], 'L3_ffn_hy_conv_w': _L3_ffn_in['hy_conv_w'], 'L3_ffn_hy_conv_b': _L3_ffn_in['hy_conv_b'], 'L3_ffn_hy_dt_bias': _L3_ffn_in['hy_dt_bias'], 'L3_ffn_hy_A_log': _L3_ffn_in['hy_A_log'], 'L3_ffn_hy_D': _L3_ffn_in['hy_D'], 'L3_ffn_hy_fcD_w': _L3_ffn_in['hy_fcD_w'], 'L3_ffn_hy_norm_w': _L3_ffn_in['hy_norm_w'], 'L3_ffn_hy_out_w': _L3_ffn_in['hy_out_w'], 'L3_ffn_out_w': _L3_ffn_in['out_w'], 'L3_ffn_out_b': _L3_ffn_in['out_b']}

def reference(x, adj, L0_gnn_W, L0_gnn_a, L0_ffn_Wg, L0_ffn_bg, L0_ffn_W1, L0_ffn_b1, L0_ffn_W2, L0_ffn_b2, L1_gnn_W, L1_gnn_a, L1_ffn_W_in, L1_ffn_conv_w, L1_ffn_conv_b, L1_ffn_dt_bias, L1_ffn_A_log, L1_ffn_D, L1_ffn_norm_w, L1_ffn_W_out, L1_ffn_W_lin, L1_ffn_b_lin, L2_gnn_weight, L2_gnn_bias, L2_ffn_Wg, L2_ffn_bg, L2_ffn_W1, L2_ffn_b1, L2_ffn_W2, L2_ffn_b2, L3_gnn_W, L3_gnn_a, L3_gnn_wtrans, L3_ffn_W_fx, L3_ffn_b_fx, L3_ffn_W_x, L3_ffn_b_x, L3_ffn_W_slice, L3_ffn_b_slice, L3_ffn_temperature, L3_ffn_hy_in_w, L3_ffn_hy_conv_w, L3_ffn_hy_conv_b, L3_ffn_hy_dt_bias, L3_ffn_hy_A_log, L3_ffn_hy_D, L3_ffn_hy_fcD_w, L3_ffn_hy_norm_w, L3_ffn_hy_out_w, L3_ffn_out_w, L3_ffn_out_b):
    import jax
    import jax.numpy as jnp

    def _L0_gnn_ref(h, adj, W, a):
        import jax, jax.numpy as jnp
        import numpy as np
        ALPHA = 0.2
        NEG_FILL = -9000000000000000.0
        d_out = W.shape[1]
        Wh = h @ W
        Wh1 = Wh @ a[:d_out]
        Wh2 = Wh @ a[d_out:]
        e = Wh1 + Wh2.T
        e = jnp.where(e > 0, e, ALPHA * e)
        scores = jnp.where(adj > 0, e, NEG_FILL)
        attention = jax.nn.softmax(scores, axis=1)
        h_prime = attention @ Wh
        return jax.nn.elu(h_prime)

    def _L0_ffn_ref(x, Wg, bg, W1, b1, W2, b2):
        import jax, jax.numpy as jnp
        import numpy as np
        B, S, D, E, H, K = (4, 2048, 128, 8, 256, 2)
        Bv, Sv, Dv = x.shape
        gate_scores = x @ Wg + bg
        _, idx = jax.lax.top_k(gate_scores, K)
        mask = jax.nn.one_hot(idx, E, dtype=x.dtype).sum(axis=-2)
        xf = x.reshape(-1, Dv)
        mf = mask.reshape(-1, E)
        h = jax.nn.gelu(jnp.einsum('td,edh->teh', xf, W1) + b1[None], approximate=False)
        y = jnp.einsum('teh,ehd->ted', h, W2) + b2[None]
        out = jnp.einsum('ted,te->td', y, mf)
        return out.reshape(Bv, Sv, Dv)

    def _L1_gnn_ref(h, adj, W, a):
        import jax, jax.numpy as jnp
        import numpy as np
        NEG = -9000000000000000.0
        Wh = h @ W
        F_OUT = Wh.shape[1]
        a1, a2 = (a[:F_OUT], a[F_OUT:])
        s1 = Wh @ a1
        s2 = Wh @ a2
        e = jax.nn.leaky_relu(s1[:, None] + s2[None, :], negative_slope=0.2)
        e = jnp.where(adj > 0, e, NEG)
        attention = jax.nn.softmax(e, axis=-1)
        return attention @ Wh

    def _L1_ffn_ref(x, W_in, conv_w, conv_b, dt_bias, A_log, D, norm_w, W_out, W_lin, b_lin):
        import jax, jax.numpy as jnp
        import numpy as np
        D_MODEL = 128
        D_STATE = 64
        D_CONV = 4
        EXPAND = 2
        HEADDIM = 64
        D_INNER = EXPAND * D_MODEL
        NHEADS = D_INNER // HEADDIM
        CONV_DIM = D_INNER + 2 * D_STATE
        D_IN_PROJ = 2 * D_INNER + 2 * D_STATE + NHEADS
        CHUNK = 128
        EPS = 1e-05

        def segsum(a):
            T = a.shape[-1]
            cs = jnp.cumsum(a, axis=-1)
            ss = cs[..., :, None] - cs[..., None, :]
            mask = jnp.tril(jnp.ones((T, T), dtype=bool))
            return jnp.where(mask, ss, -jnp.inf)

        def mamba2_block(x, W_in, conv_w, conv_b, dt_bias, A_log, D, norm_w, W_out, W_lin, b_lin):
            Bsz, L, _ = x.shape
            zxbcdt = x @ W_in
            z, xBC, dt = jnp.split(zxbcdt, [D_INNER, D_INNER + CONV_DIM], axis=-1)
            xp = jnp.pad(xBC, ((0, 0), (D_CONV - 1, 0), (0, 0)))
            conv = conv_b + sum((xp[:, k:k + L, :] * conv_w[:, k] for k in range(D_CONV)))
            xBC = jax.nn.silu(conv)
            xh, Bmat, Cmat = jnp.split(xBC, [D_INNER, D_INNER + D_STATE], axis=-1)
            dt = jax.nn.softplus(dt + dt_bias)
            A = -jnp.exp(A_log)
            nc = L // CHUNK
            xh = xh.reshape(Bsz, nc, CHUNK, NHEADS, HEADDIM)
            Bc = Bmat.reshape(Bsz, nc, CHUNK, D_STATE)
            Cc = Cmat.reshape(Bsz, nc, CHUNK, D_STATE)
            dtc = dt.reshape(Bsz, nc, CHUNK, NHEADS)
            dA = jnp.einsum('bclh,h->bhcl', dtc, A)
            A_cum = jnp.cumsum(dA, axis=-1)
            Lmat = jnp.exp(segsum(dA))
            xdt = xh * dtc[..., None]
            Y_diag = jnp.einsum('bcln,bcsn,bhcls,bcshp->bclhp', Cc, Bc, Lmat, xdt)
            decay_states = jnp.exp(A_cum[..., -1:] - A_cum)
            states = jnp.einsum('bcln,bhcl,bclhp->bchpn', Bc, decay_states, xdt)
            chunk_decay = jnp.exp(A_cum[..., -1])

            def step(h, inp):
                s, d = inp
                return (h * d[..., None, None] + s, h)
            _, prevs = jax.lax.scan(step, jnp.zeros_like(states[:, 0]), (jnp.moveaxis(states, 1, 0), jnp.moveaxis(chunk_decay, 2, 0)))
            prevs = jnp.moveaxis(prevs, 0, 1)
            Y_off = jnp.einsum('bcln,bchpn,bhcl->bclhp', Cc, prevs, jnp.exp(A_cum))
            Y = (Y_diag + Y_off + xh * D[:, None]).reshape(Bsz, L, D_INNER)
            Y = Y * jax.nn.silu(z)
            Y = Y * jax.lax.rsqrt(jnp.mean(Y * Y, axis=-1, keepdims=True) + EPS) * norm_w
            out = Y @ W_out
            return out @ W_lin + b_lin
        return mamba2_block(x, W_in, conv_w, conv_b, dt_bias, A_log, D, norm_w, W_out, W_lin, b_lin)

    def _L2_gnn_ref(x, adj, weight, bias):
        import jax, jax.numpy as jnp
        import numpy as np
        N = 8192
        F_IN = 128
        F_OUT = 128
        a = adj.astype(x.dtype)
        deg = jnp.sum(a, axis=1, keepdims=True)
        x1 = a @ x / deg
        n_x = jnp.concatenate([x1, x], axis=1)
        return n_x @ weight + bias

    def _L2_ffn_ref(x, Wg, bg, W1, b1, W2, b2):
        import jax, jax.numpy as jnp
        import numpy as np
        B, S, D, H, E, K = (8, 4096, 128, 512, 8, 2)
        gate_scores = jnp.einsum('bsd,ed->bse', x, Wg) + bg
        topk_scores, topk_idx = jax.lax.top_k(gate_scores, K)
        topk_probs = jax.nn.softmax(topk_scores, axis=-1)
        combine = jnp.sum(topk_probs[..., None] * jax.nn.one_hot(topk_idx, E, dtype=x.dtype), axis=-2)
        out = jnp.zeros_like(x)
        for e in range(E):
            h = jax.nn.relu(jnp.einsum('bsd,hd->bsh', x, W1[e]) + b1[e])
            y = jnp.einsum('bsh,dh->bsd', h, W2[e]) + b2[e]
            out = out + combine[..., e:e + 1] * y
        return out

    def _L3_gnn_ref(inp, adj, W, a, wtrans):
        import jax, jax.numpy as jnp
        import numpy as np
        N, FEAT = (4096, 128)
        ALPHA = 0.2
        NEG_INF = jnp.float32(-1000000000000.0)
        out_features = W.shape[1]
        h = inp @ W
        Wh1 = h @ a[:out_features]
        Wh2 = h @ a[out_features:]
        e = jax.nn.leaky_relu(Wh1 + Wh2.T, negative_slope=ALPHA)
        mask = adj > 0
        attention = jax.nn.softmax(jnp.where(mask, e, NEG_INF), axis=1)
        negative_attention = -jax.nn.softmax(jnp.where(mask, -e, NEG_INF), axis=1)
        h_prime = attention @ inp
        h_prime_negative = negative_attention @ inp
        h_prime_double = jnp.concatenate([h_prime, h_prime_negative], axis=1)
        new_h_prime = h_prime_double @ wtrans
        return jax.nn.elu(new_h_prime)

    def _L3_ffn_ref(x, W_fx, b_fx, W_x, b_x, W_slice, b_slice, temperature, hy_in_w, hy_conv_w, hy_conv_b, hy_dt_bias, hy_A_log, hy_D, hy_fcD_w, hy_norm_w, hy_out_w, out_w, out_b):
        import jax, jax.numpy as jnp
        import numpy as np
        H, P, G, NS, K = (8, 64, 64, 64, 3)
        D_INNER = H * P
        CONV_DIM = D_INNER + 2 * NS
        D_IN_PROJ = 2 * D_INNER + 2 * NS + 2 * H

        def _hydra(u, in_w, conv_w, conv_b, dt_bias, A_log, Dp, fcD_w, norm_w, out_w):
            Bt, L, _ = u.shape
            zxbcdt = u @ in_w.T
            z = zxbcdt[..., :D_INNER]
            xBC = zxbcdt[..., D_INNER:D_INNER + CONV_DIM]
            dt = zxbcdt[..., -2 * H:]
            dt = jnp.concatenate([dt[..., :H], jnp.flip(dt[..., H:], axis=1)], axis=0)
            dt = jax.nn.softplus(dt + dt_bias)
            xp = jnp.pad(xBC, ((0, 0), (K - 1, 0), (0, 0)))
            xBC = sum((xp[:, k:k + L, :] * conv_w[:, k] for k in range(K))) + conv_b
            xBC = jax.nn.silu(xBC)
            x = xBC[..., :D_INNER]
            Bm = xBC[..., D_INNER:D_INNER + NS]
            Cm = xBC[..., D_INNER + NS:]
            x_og = x
            x2 = jnp.concatenate([x, jnp.flip(x, 1)], 0).reshape(2 * Bt, L, H, P)
            B2 = jnp.concatenate([Bm, jnp.flip(Bm, 1)], 0)
            C2 = jnp.concatenate([Cm, jnp.flip(Cm, 1)], 0)
            dA = jnp.exp(dt * -jnp.exp(A_log))
            dBx = jnp.einsum('blh,bln,blhp->blhpn', dt, B2, x2)

            def step(h, inp):
                dA_t, dBx_t, C_t = inp
                h = h * dA_t[:, :, None, None] + dBx_t
                return (h, jnp.einsum('bhpn,bn->bhp', h, C_t))
            h0 = jnp.zeros((2 * Bt, H, P, NS), u.dtype)
            _, ys = jax.lax.scan(step, h0, (dA.transpose(1, 0, 2), dBx.transpose(1, 0, 2, 3, 4), C2.transpose(1, 0, 2)))
            y = ys.transpose(1, 0, 2, 3).reshape(2 * Bt, L, D_INNER)
            y_fw, y_bw = (y[:Bt], jnp.flip(y[Bt:], 1))
            y = jnp.pad(y_fw[:, :-1], ((0, 0), (1, 0), (0, 0))) + jnp.pad(y_bw[:, 1:], ((0, 0), (0, 1), (0, 0)))
            y = y + x_og * jnp.repeat(x_og @ fcD_w.T + Dp, P, axis=-1)
            yg = y * jax.nn.silu(z)
            yg = yg * jax.lax.rsqrt(jnp.mean(jnp.square(yg), -1, keepdims=True) + 1e-05) * norm_w
            return yg @ out_w.T
        B, N, _ = x.shape
        fx = (x @ W_fx.T + b_fx).reshape(B, N, H, P).transpose(0, 2, 1, 3)
        xm = (x @ W_x.T + b_x).reshape(B, N, H, P).transpose(0, 2, 1, 3)
        temp = jnp.maximum(temperature, 1e-06)
        sw = jax.nn.softmax((xm @ W_slice.T + b_slice) / temp, axis=-1)
        snorm = sw.sum(2)
        st = jnp.einsum('bhnc,bhng->bhgc', fx, sw) / (snorm + 1e-05)[..., None]
        st = st.transpose(0, 2, 1, 3).reshape(B, G, D_INNER)
        ot = _hydra(st, hy_in_w, hy_conv_w, hy_conv_b, hy_dt_bias, hy_A_log, hy_D, hy_fcD_w, hy_norm_w, hy_out_w)
        ot = ot.reshape(B, G, H, P).transpose(0, 2, 1, 3)
        out = jnp.einsum('bhgc,bhng->bhnc', ot, sw).transpose(0, 2, 1, 3).reshape(B, N, D_INNER)
        return out @ out_w.T + out_b
    x = x + _L0_gnn_ref(_layernorm(x, axis=-1), adj, L0_gnn_W, L0_gnn_a)
    x = x + _L0_ffn_ref(_layernorm(x, axis=-1)[None], L0_ffn_Wg, L0_ffn_bg, L0_ffn_W1, L0_ffn_b1, L0_ffn_W2, L0_ffn_b2)[0]
    x = x + _L1_gnn_ref(_layernorm(x, axis=-1), adj, L1_gnn_W, L1_gnn_a)
    x = x + _L1_ffn_ref(_layernorm(x, axis=-1)[None], L1_ffn_W_in, L1_ffn_conv_w, L1_ffn_conv_b, L1_ffn_dt_bias, L1_ffn_A_log, L1_ffn_D, L1_ffn_norm_w, L1_ffn_W_out, L1_ffn_W_lin, L1_ffn_b_lin)[0]
    x = x + _L2_gnn_ref(_layernorm(x, axis=-1), adj, L2_gnn_weight, L2_gnn_bias)
    x = x + _L2_ffn_ref(_layernorm(x, axis=-1)[None], L2_ffn_Wg, L2_ffn_bg, L2_ffn_W1, L2_ffn_b1, L2_ffn_W2, L2_ffn_b2)[0]
    x = x + _L3_gnn_ref(_layernorm(x, axis=-1), adj, L3_gnn_W, L3_gnn_a, L3_gnn_wtrans)
    x = x + _L3_ffn_ref(_layernorm(x, axis=-1)[None], L3_ffn_W_fx, L3_ffn_b_fx, L3_ffn_W_x, L3_ffn_b_x, L3_ffn_W_slice, L3_ffn_b_slice, L3_ffn_temperature, L3_ffn_hy_in_w, L3_ffn_hy_conv_w, L3_ffn_hy_conv_b, L3_ffn_hy_dt_bias, L3_ffn_hy_A_log, L3_ffn_hy_D, L3_ffn_hy_fcD_w, L3_ffn_hy_norm_w, L3_ffn_hy_out_w, L3_ffn_out_w, L3_ffn_out_b)[0]
    return x

_drawn_inputs = setup_inputs


def setup_inputs(seed=0):
    import zlib

    import numpy as np

    out = dict(_drawn_inputs(seed))
    spreads = {'L0_ffn_bg': (0.0, 0.1),
     'L0_ffn_b1': (0.0, 0.291),
     'L0_ffn_b2': (0.0, 0.1),
     'L1_ffn_D': (1.0, 0.2),
     'L1_ffn_norm_w': (1.0, 0.2),
     'L1_ffn_b_lin': (0.0, 0.1),
     'L2_gnn_bias': (0.0, 0.1),
     'L3_ffn_b_fx': (0.0, 0.1),
     'L3_ffn_b_x': (0.0, 0.8),
     'L3_ffn_b_slice': (0.0, 0.8),
     'L3_ffn_temperature': (0.5, 0.6),
     'L3_ffn_hy_conv_b': (0.0, 0.1),
     'L3_ffn_hy_dt_bias': (-4.600166320800781, 0.6),
     'L3_ffn_hy_D': (1.0, 0.6),
     'L3_ffn_hy_norm_w': (1.0, 0.6),
     'L3_ffn_out_b': (0.0, 0.1)}
    factors = {'L1_ffn_A_log': 5.981,
     'L2_ffn_bg': 2.807,
     'L2_ffn_b1': 7.422,
     'L2_ffn_b2': 5.81,
     'L3_gnn_W': 2.812,
     'L3_ffn_W_fx': 2.796,
     'L3_ffn_W_x': 8.0,
     'L3_ffn_W_slice': 8.0,
     'L3_ffn_hy_conv_w': 8.0,
     'L3_ffn_hy_A_log': 64.0,
     'L3_ffn_hy_fcD_w': 35.95}
    for name, (base, spread) in spreads.items():
        noise = np.random.default_rng([zlib.crc32(name.encode()), seed]).standard_normal(out[name].shape)
        drawn = base * np.exp(spread * noise) if base else spread * noise
        out[name] = jnp.asarray(drawn.astype(out[name].dtype))
    for name, factor in factors.items():
        out[name] = (out[name] * factor).astype(out[name].dtype)
    return out
```

```python
from contextlib import ExitStack

import numpy as np
import concourse.bass as bass
from concourse import mybir

F32 = mybir.dt.float32
BF16 = mybir.dt.bfloat16
I32 = mybir.dt.int32
ALU = mybir.AluOpType
ACT = mybir.ActivationFunctionType
AX = mybir.AxisListType

P = 128
N = 2048
D = 128
NT = N // P
NG = N // 512
EPS = 1e-5
SLOPE = 0.2
RISE = 1.0 - SLOPE
CLAMP = 75.0 / RISE
E = 8
HC = {"L0": 2, "L2": 4}
VC = D + 1
TPB = 3
NBK = -(-NT // TPB)
RING = 4
LAG = 3
DI = 256
NH = 4
HD = DI // NH
NS = 64
SH = 8
SG = 64
SI = 512
HYP = 2 * SI + 2 * NS + 2 * SH
STAGES = ["gnn0", "moe0", "gnn1", "mamba", "sage", "moe2", "gnn3", "slice"]


def program(nc, t, outs):
    with ExitStack() as ctx:
        def sb(name, shape, dt=F32):
            return ctx.enter_context(nc.sbuf_tensor(name, shape, dt))

        sems = {}
        reused = {}

        def S(name):
            name = reused.get(name, (name,))[0]
            if name not in sems:
                sems[name] = ctx.enter_context(nc.semaphore(name))
            return sems[name]

        x = sb("x", [P, NT, D])
        hT = sb("hT", [P, N])
        adjT = sb("adjT", [P, NT, N], BF16)
        ps = ctx.enter_context(nc.psum_tensor("ps", [P, 8, 512], F32))

        ident = sb("ident", [P, P])
        zeros = sb("zeros", [P, TPB * VC], BF16)
        h_rows = sb("h_rows", [P, 4, D])
        stats = sb("stats", [P, 4, 6])
        mean_var = sb("mean_var", [P, 4, 2])
        std = sb("std", [P, 4])
        rstd = sb("rstd", [P, 4])

        gat_wT = sb("gat_wT", [P, 3, D])
        gat_a = sb("gat_a", [P, 3, 2])
        value_w = sb("value_w", [P, 4, VC])
        score_w = sb("score_w", [P, 3, 2, P])
        s2_bound = sb("s2_bound", [P, 2])
        s2_rel = sb("s2_rel", [P, 2, NT])
        K = sb("K", [P, 2, NT])
        F = sb("F", [P, 2, NT])
        rowrec = sb("rowrec", [P, NT])

        big = sb("big", [P, 8 * N])
        R = big[:, 0:2 * N].rearrange("p (s n) -> p s n", s=2)
        T = big[:, 2 * N:4 * N].rearrange("p (s n) -> p s n", s=2)
        PR = big[:, 4 * N:6 * N].rearrange("p (s n) -> p s n", s=2)
        adj_in = big[:, 6 * N:8 * N].bitcast(I32).rearrange("p (s n) -> p s n", s=2)
        G = sb("G", [P, 2, NT, VC])
        rows_a = T[:, 0, :].rearrange("p (i d) -> p i d", d=D)
        rows_b = T[:, 1, :].rearrange("p (i d) -> p i d", d=D)
        rows_c = R[:, 0, :].rearrange("p (i d) -> p i d", d=D)

        comb_b = big[:, 0:2 * N].rearrange("p (s n) -> p s n", s=2)
        act_h = big[:, 2 * N:3 * N].rearrange("p (r n) -> p r n", r=RING)
        mul_h = big[:, 3 * N:4 * N].rearrange("p (r n) -> p r n", r=RING)
        out_T = big[:, 4 * N:5 * N].rearrange("p (c n) -> p c n", c=NG)
        comb8 = big[0:E, 5 * N:6 * N]
        w1_e = sb("w1_e", [P, 2, 512])
        w2_e = sb("w2_e", [P, 2, 4, P])
        gate_w = sb("gate_w", [P, 2, E])
        gate_b = sb("gate_b", [P, 2, E])
        first = sb("first", [P, E])
        b1_T = {"L0": sb("b1_T0", [P, E * 2]), "L2": sb("b1_T2", [P, E * 4])}
        b2 = sb("b2", [E, 2, D])
        top = sb("top", [P, 8, NT, E])
        topm = sb("topm", [P, 8, NT])
        comb = sb("comb", [P, E, NT])
        comb_T = sb("comb_T", [P, P])
        comb_dram = {L: nc.dram_tensor(f"comb_{L}", [E, N], F32, kind="Internal").ap() for L in ("L0", "L2")}

        o = [0]

        def part(n, rows=P):
            o[0] += n
            assert o[0] <= 8 * N
            return big[0:rows, o[0] - n:o[0]]

        conv_raw = part(4 * 516).rearrange("p (q n) -> p q n", q=4)
        conv = part(4 * 512).rearrange("p (q n) -> p q n", q=4)
        z_gate = part(NT * DI).rearrange("p (i d) -> p i d", d=DI)
        y_rows = part(NT * D).rearrange("p (i d) -> p i d", d=D)
        xb_rows = part(4 * 320).rearrange("p (i d) -> p i d", d=320)
        cb_masked = part(4 * P).rearrange("p (i l) -> p i l", i=4)
        mixm = part(2 * 512).rearrange("p (b n) -> p b n", b=2)
        x_dt = part(2 * DI).rearrange("p (b n) -> p b n", b=2)
        x_decayed = part(2 * DI).rearrange("p (b n) -> p b n", b=2)
        x_skip = part(2 * DI).rearrange("p (b n) -> p b n", b=2)
        y_gated = part(2 * DI).rearrange("p (b n) -> p b n", b=2)
        y_T = part(2 * DI).rearrange("p (b n) -> p b n", b=2)
        state = part(DI, 64)
        Gf = G[:, :, :, :].rearrange("p s i c -> p (s i c)")
        conv_tanh = Gf[:, 0:2048].rearrange("p (q n) -> p q n", q=4)
        tri_dA = Gf[:, 2048:3072].rearrange("p (b n) -> p b n", b=2)
        decay = Gf[:, 3072:4096].rearrange("p (b n) -> p b n", b=2)
        y_a = sb("y_a", [P, DI])
        y_b = sb("y_b", [P, DI])
        z_tanh = sb("z_tanh", [P, 2, DI])
        y_square = sb("y_square", [P, DI])
        tri = sb("tri", [P, P])
        after = sb("after", [P, P])
        ones = sb("ones", [P, P])
        win_x = sb("win_x", [P, 384])
        win_zd = sb("win_zd", [P, DI + NH])
        conv_w = sb("conv_w", [P, 4, 4])
        conv_b = sb("conv_b", [P, 4])
        small_in = sb("small_in", [P, 3, NH])
        wout_T = sb("wout_T", [P, 2, P])
        w_lin = sb("w_lin", [P, P])
        norm_w = sb("norm_w", [P, 2])
        b_lin = sb("b_lin", [P, D])
        w_proj = sb("w_proj", [P, 2, P])
        dts = sb("dts", [P, 6, NT * NH])
        exp_A = sb("exp_A", [P, NH])
        carry = sb("carry", [P, 2, NT * NH])
        sumsq = sb("sumsq", [P, NT])

        sage_w = sb("sage_w", [P, 2 * D])
        sage_b = sb("sage_b", [P, D])
        sage_y = big[:, 0:NT * 200].bitcast(BF16)[:, 0:NT * 386].rearrange("p (i c) -> p i c", c=386)
        sage_r = big[:, NT * 200:NT * 200 + N].rearrange("p (i d) -> p i d", d=D)
        sage_sum = sb("sage_sum", [P, 2, D])
        sage_rec = sb("sage_rec", [P, 2])

        adj_words = adjT[:, :, :].rearrange("p i n -> p (i n)").bitcast(F32)
        a_o = [0]

        def in_adj(n, rows=P):
            a_o[0] += n
            assert a_o[0] <= NT * N // 2
            return adj_words[0:rows, a_o[0] - n:a_o[0]]

        wx_h = in_adj(SH * D, NS).rearrange("p (h d) -> p h d", h=SH)
        ws_T = in_adj(SG, NS)
        bx_T = in_adj(SH, NS)
        bs_b = in_adj(SG)
        temp_b = in_adj(SH)
        wfx_T = in_adj(SI)
        bfx_T = in_adj(4)
        hy_in = in_adj(4 * HYP).rearrange("p (k n) -> p k n", k=4)
        hy_cw = in_adj(6 * 3).rearrange("p (q k) -> p q k", q=6)
        hy_cb = in_adj(6)
        hy_small = in_adj(4 * SH).rearrange("p (q h) -> p q h", q=4)
        hy_fcD = in_adj(4 * SH).rearrange("p (k h) -> p k h", k=4)
        hy_nw = in_adj(4)
        hy_out = in_adj(4 * SI).rearrange("p (k n) -> p k n", k=4)
        wo_T = in_adj(4 * D).rearrange("p (k d) -> p k d", k=4)
        ob_T = in_adj(1)
        logit_w = in_adj(SI)
        logit_c = in_adj(SI)
        A_T = in_adj(SI)
        q_rows = in_adj(SI)
        sn_rec = in_adj(SI)
        st_T = in_adj(4 * SG).rearrange("p (k g) -> p k g", k=4)
        block_o = in_adj(4 * P).rearrange("p (k g) -> p k g", k=4)
        slice_w = in_adj(4 * D).rearrange("p (k d) -> p k d", k=4)
        hc_raw = in_adj(6 * 66).rearrange("p (q l) -> p q l", q=6)
        hc = in_adj(6 * SG).rearrange("p (q l) -> p q l", q=6)
        hc_tanh = in_adj(6 * SG).rearrange("p (q l) -> p q l", q=6)
        yg_T = in_adj(4 * SG).rearrange("p (k g) -> p k g", k=4)
        hx_rows = in_adj(SI, SG)
        hy_a = in_adj(SI, SG)
        hy_cbm = in_adj(2 * SG, SG).rearrange("p (s l) -> p s l", s=2)
        hy_dt = in_adj(6 * 2 * SH, SG).rearrange("p (q h) -> p q h", q=6)
        hy_fD = in_adj(SH, SG)
        hy_ss = in_adj(2, SG)
        sw_T = big[:, 0:4 * N].rearrange("p (k n) -> p k n", k=4)
        s_out_T = big[:, 4 * N:5 * N].rearrange("p (c n) -> p c n", c=NG)
        o5 = 5 * N
        s_logit = big[:, o5:o5 + 1024].rearrange("p (b n) -> p b n", b=2)
        s_exp = big[:, o5 + 1024:o5 + 2048].rearrange("p (b n) -> p b n", b=2)
        s_sw = big[:, o5 + 2048:o5 + 3072].rearrange("p (b n) -> p b n", b=2)
        s_acc = big[:, o5 + 3072:o5 + 3584]
        s_hT = big[:, o5 + 3584:o5 + 4096]
        s_h = big[:, o5 + 4096:o5 + 4608].rearrange("p (i d) -> p i d", d=D)
        h_all = Gf[:, 0:N].rearrange("p (i d) -> p i d", d=D)
        hz, hy_b, hy_mix = (Gf[0:SG, N + q * SI:N + (q + 1) * SI] for q in range(3))
        hy_tdA, hy_dec = s_logit[0:SG], s_exp[0:SG]
        s_max = sb("s_max", [P, 2, SH])
        s_sum = sb("s_sum", [P, 2, SH])
        s_rec = sb("s_rec", [P, 2, SH])
        before = sb("before", [SG, SG])
        low = sb("low", [SG, SG])

        x_count = [16]
        ndbg = [0]

        def bank_rows(b0, b1, c0, c1):
            return ps[:, b0:b1, 0:TPB * VC].rearrange("p b (k c) -> p b k c", c=VC)[:, :, :, c0:c1]

        def tiles3(ap, b0, b1):
            return ap[:, TPB * b0:TPB * b1, :].rearrange("p (b k) d -> p b k d", k=TPB)

        FULL = NT // TPB

        block = ctx.enter_context(nc.Block())
        plan = []

        def norm_vector(dve, n, need):
            dve.wait_ge(S("x_updates"), need)
            with dve.Fori(0, NG) as g:
                k = g * 4 + (16 * n)
                for i in range(4):
                    dve.bn_stats(stats[:, i, :], x[:, bass.ds(g * 4 + i, 1), :]).then_inc(S("stats"), 1)
                dve.wait_ge(S("stats"), k + 4)
                dve.sem_inc(S("stats_seen"), 1)
                for i in range(4):
                    dve.bn_aggr(mean_var[:, i, :], stats[:, i, :]).then_inc(S("mean_var"), 1)
                dve.wait_ge(S("std"), g + (4 * n + 1))
                dve.reciprocal(rstd[:, :], std[:, :]).then_inc(S("rstd"), 1)
                dve.wait_ge(S("rstd"), g + (4 * n + 1))
                dve.wait_ge(S("h_turned"), k + 1)
                if n == 7:
                    dve.wait_ge(S("h_kept"), g + 1)
                for i in range(4):
                    dve.tensor_scalar(h_rows[:, i, :], x[:, bass.ds(g * 4 + i, 1), :], mean_var[:, i, 0:1],
                                      rstd[:, i:i + 1], ALU.subtract, ALU.mult).then_inc(S("h_rows"), 1)
                dve.wait_ge(S("h_rows"), k + 4)

        def norm_scalar(act, n):
            with act.Fori(0, NG) as g:
                act.wait_ge(S("mean_var"), g * 4 + (16 * n + 4))
                act.activation(std[:, :], mean_var[:, :, 1], ACT.Sqrt, bias=EPS).then_inc(S("std"), 1)
                act.wait_ge(S("h_turned"), g * 4 + (16 * n + 4 + 4))
                act.copy(hT[:, bass.ts(g, 512)], ps[:, 6, :]).then_inc(S("hT"), 1)

        def norm_tensor(pe, n):
            with pe.Fori(0, NG) as g:
                pe.wait_ge(S("h_rows"), g * 4 + (16 * n + 4))
                pe.wait_ge(S("hT"), g + (4 * n + 1))
                for i in range(4):
                    pe.transpose(ps[:, 6, i * P:(i + 1) * P], h_rows[:, i, :], ident[:, :]).then_inc(S("h_turned"), 1)

        def hT_ready(eng, n):
            eng.wait_ge(S("hT"), 4 * n + 4 + 1)

        GAT = {"L0": 0, "L1": 1, "L3": 2}
        VAL = {"L0": [0], "L1": [1], "L3": [2, 3]}

        def gat_setup_tensor(pe):
            pe.wait_ge(S("gat_loaded"), 16 * 10)
            for l in range(3):
                pe.matmul(ps[:, 7, 2 * l:2 * l + 2], gat_wT[:, l, :], gat_a[:, l, :], start=True, stop=True)\
                    .then_inc(S("score_vec"), 1)

        def gat_setup_vector(dve):
            dve.memset(zeros[:, :], 0.0).then_inc(S("zeros"), 1)
            dve.wait_ge(S("score_vec"), 3)
            dve.wait_ge(S("gat_loaded"), 16 * 10)
            for l in range(3):
                for s in range(2):
                    dve.tensor_copy(score_w[:, l, s, :], ps[:, 7, 2 * l + s:2 * l + s + 1].to_broadcast([P, P]))\
                        .then_inc(S("score_w"), 1)
            for v, l in enumerate((0, 1, 2, 2)):
                dve.tensor_copy(value_w[:, v, D:VC], ps[:, 7, 2 * l + 1:2 * l + 2]).then_inc(S("score_w"), 1)

        def gat_tensor(pe, L, n):
            l = GAT[L]
            pe.wait_ge(S("score_w"), 10)
            hT_ready(pe, n)
            for s in range(2):
                for c in range(NG):
                    pe.matmul(ps[:, 4 * s + c, :], score_w[:, l, s, :], hT[:, c * 512:(c + 1) * 512],
                              start=True, stop=True).then_inc(S("scores"), 1)
            for sign, v in enumerate(VAL[L]):
                if sign == 0:
                    pe.wait_ge(S("clamped"), clamp_end[L])
                else:
                    pe.wait_ge(S("x_updates"), pass_end[L])
                for i in range(NT):
                    pe.matmul(ps[:, i // TPB, (i % TPB) * VC:(i % TPB + 1) * VC], hT[:, i * P:(i + 1) * P],
                              value_w[:, v, :], start=True, stop=True).then_inc(S("values"), 1)
                pe.wait_ge(S("G"), 3 * (v + 1))
                pe.wait_ge(S("zeros"), 1)
                for b in range(NBK):
                    w = VC * (TPB if b < FULL else NT - FULL * TPB)
                    pe.matmul(ps[:, b, 0:w], zeros[:, 0:P], zeros[:, 0:w], start=True, stop=False,
                              skip_group_check=True).then_inc(S("cleared"), 1)
                pe.wait_ge(S("cleared"), NBK * (v + 1))
                with pe.Fori(0, NT // 2) as jj:
                    for b in range(2):
                        pe.wait_ge(S("weights"), jj * 2 + (NT * v + b + 1 + 2))
                        for i in range(NT):
                            mm = pe.matmul(ps[:, i // TPB, (i % TPB) * VC:(i % TPB + 1) * VC],
                                           PR[:, b, i * P:(i + 1) * P], G[:, sign, bass.ds(jj * 2 + b, 1), :],
                                           start=False, stop=False, skip_group_check=True)
                        mm.then_inc(S("weights_used"), 1)

        def gat_scalar(act, L, n):
            for sign, v in enumerate(VAL[L]):
                s = (1.0, -1.0)[sign]
                act.wait_ge(S("clamped"), clamp_end[L] - (len(VAL[L]) - 1) * (1 - sign))
                act.activation(R[:, sign, :], R[:, sign, :], ACT.Exp, scale=s * RISE).then_inc(S("R"), 1)
                act.wait_ge(S("s2_rel"), 2 * (v + 1))
                act.activation(K[:, sign, :], s2_rel[:, sign, :], ACT.Exp, scale=s * RISE).then_inc(S("KF"), 1)
                act.activation(F[:, sign, :], s2_rel[:, sign, :], ACT.Exp, scale=s * SLOPE).then_inc(S("KF"), 1)
                if sign == 0:
                    act.wait_ge(S("R"), v + 1)
                    act.wait_ge(S("KF"), 2 * v + 2)
                    k = VNUM[v]
                    with act.Fori(0, NT // 2) as jj:
                        for b in range(2):
                            act.wait_ge(S("weights"), jj * 2 + (NT * v + b + 1))
                            act.activation(T[:, b, :], R[:, 0, :], ACT.Relu, bias=-1.0,
                                           scale=K[:, 0, bass.ds(jj * 2 + b, 1)]).then_inc(S("T"), 1)
                if L == "L0" or sign == 1:
                    for q in range(3):
                        act.wait_ge(S("elu_in"), 3 * ELU[L] + q + 1)
                        lo, hi = PIECES[q]
                        act.activation(rows_b[:, lo:hi, :], rows_b[:, lo:hi, :], ACT.Exp).then_inc(S("elu_exp"), 1)

        VNUM = [0, 1, 2, 3]
        ELU = {"L0": 0, "L3": 1}
        PIECES = [(0, 9), (9, 15), (15, 16)]
        clamp_end = {"L0": 1, "L1": 2, "L3": 5}
        pass_end = {}

        def rows_of(q, c0, c1):
            lo, hi = PIECES[q]
            if hi <= FULL * TPB:
                return bank_rows(lo // TPB, hi // TPB, c0, c1)
            return ps[:, FULL:FULL + 1, c0:c1]

        def match(ap, q):
            lo, hi = PIECES[q]
            if hi <= FULL * TPB:
                return ap[:, lo:hi, :].rearrange("p (b k) d -> p b k d", k=TPB)
            return ap[:, lo:hi, :]

        def match1(ap, q, w):
            lo, hi = PIECES[q]
            if hi <= FULL * TPB:
                return ap[:, lo:hi].rearrange("p (b k) -> p b k", k=TPB).unsqueeze(3)\
                    .to_broadcast([P, (hi - lo) // TPB, TPB, w])
            return ap[:, lo:hi].unsqueeze(2).to_broadcast([P, hi - lo, w])

        def gat_vector(dve, L, n):
            l = GAT[L]
            base = clamp_end[L] - (1 if len(VAL[L]) == 1 else 3)
            dve.wait_ge(S("scores"), 8 * (l + 1))
            dve.tensor_reduce(s2_bound[:, 0:1], ps[:, 4:8, :], AX.XY, ALU.max).then_inc(S("bound"), 1)
            dve.wait_ge(S("bound"), l + 1)
            dve.tensor_scalar(R[:, 0, :], ps[:, 0:4, :], s2_bound[:, 0:1], CLAMP, ALU.add, ALU.min)\
                .then_inc(S("clamped"), 1)
            if L == "L3":
                dve.tensor_reduce(s2_bound[:, 1:2], ps[:, 4:8, :], AX.XY, ALU.min).then_inc(S("bound"), 1)
                dve.wait_ge(S("bound"), l + 2)
                dve.tensor_scalar(R[:, 1, :], ps[:, 0:4, :], s2_bound[:, 1:2], -CLAMP, ALU.add, ALU.max)\
                    .then_inc(S("clamped"), 1)
                dve.wait_ge(S("clamped"), base + 2)
                dve.tensor_scalar(R[:, 1, :], R[:, 1, :], CLAMP, None, ALU.min).then_inc(S("clamped"), 1)
            for sign, v in enumerate(VAL[L]):
                dve.wait_ge(S("values"), NT * (v + 1))
                dve.tensor_scalar(s2_rel[:, sign, 0:15].rearrange("p (b k) -> p b k", k=TPB),
                                  bank_rows(0, FULL, D, VC).squeeze(3) if False else
                                  ps[:, 0:FULL, 0:TPB * VC].rearrange("p b (k c) -> p b k c", c=VC)[:, :, :, D],
                                  s2_bound[:, sign:sign + 1], None, ALU.subtract).then_inc(S("s2_rel"), 1)
                dve.tensor_scalar(s2_rel[:, sign, 15:16], ps[:, FULL, D:VC], s2_bound[:, sign:sign + 1], None,
                                  ALU.subtract).then_inc(S("s2_rel"), 1)
                dve.wait_ge(S("KF"), 2 * v + 2)
                dve.tensor_copy(G[:, sign, :, D], F[:, sign, :]).then_inc(S("G"), 1)
                for b0, b1 in ((0, FULL), (FULL, NBK)):
                    if b1 == FULL:
                        o = G[:, sign, 0:15, 0:D].rearrange("p (b k) d -> p b k d", k=TPB)
                        i0 = bank_rows(0, FULL, 0, D)
                        i1 = F[:, sign, 0:15].rearrange("p (b k) -> p b k", k=TPB).unsqueeze(3).to_broadcast(
                            [P, FULL, TPB, D])
                        dve.tensor_tensor(o, i0, i1, ALU.mult).then_inc(S("G"), 1)
                    else:
                        dve.tensor_scalar(G[:, sign, 15, 0:D], ps[:, FULL, 0:D], F[:, sign, 15:16], None, ALU.mult)\
                            .then_inc(S("G"), 1)
                dve.wait_ge(S("R"), v + 1)
                with dve.Fori(0, NT // 2) as jj:
                    for b in range(2):
                        j = jj * 2 + b
                        if L == "L0":
                            dve.wait_ge(S(f"adj_landed{b}"), jj * 16 + 16)
                            dve.tensor_copy(adjT[:, bass.ds(j, 1), :], adj_in[:, b, :]).then_inc(S("adjT"), 1)
                        if sign == 0:
                            dve.wait_ge(S("T"), j + (NT * TNUM[v] + 1))
                        else:
                            dve.wait_ge(S("weights"), j + (NT * v + 1))
                            dve.tensor_scalar(T[:, b, :], R[:, 1, :], K[:, 1, bass.ds(j, 1)], 1.0, ALU.mult,
                                              ALU.min).then_inc(S("T_neg"), 1)
                            dve.wait_ge(S("T_neg"), j + 1)
                        dve.wait_ge(S("weights_used"), j + (NT * v + 1))
                        if L == "L0":
                            dve.wait_ge(S("adjT"), j + 1)
                        if sign == 0:
                            dve.scalar_tensor_tensor(PR[:, b, :], T[:, b, :], 1.0, adjT[:, bass.ds(j, 1), :],
                                                     ALU.add, ALU.mult).then_inc(S("weights"), 1)
                        else:
                            dve.tensor_tensor(PR[:, b, :], T[:, b, :], adjT[:, bass.ds(j, 1), :], ALU.mult)\
                                .then_inc(S("weights"), 1)
                dve.wait_ge(S("weights_used"), NT * (v + 1) + 2)
                for q in range(3):
                    lo, hi = PIECES[q]
                    cols = ps[:, lo // TPB:hi // TPB, 0:TPB * VC].rearrange("p b (k c) -> p b k c", c=VC)[:, :, :, D] \
                        if q < 2 else ps[:, FULL, D:VC]
                    o = rowrec[:, lo:hi].rearrange("p (b k) -> p b k", k=TPB) if q < 2 else rowrec[:, lo:hi]
                    dve.reciprocal(o, cols).then_inc(S("rowrec"), 1)
                dve.wait_ge(S("rowrec"), 3 * (v + 1))
                if L == "L3" and sign == 0:
                    for q in range(3):
                        dve.tensor_tensor(match(rows_c, q), rows_of(q, 0, D), match1(rowrec, q, D), ALU.mult)\
                            .then_inc(S("x_updates"), 1)
                    continue
                for q in range(3):
                    dve.tensor_tensor(match(rows_a, q), rows_of(q, 0, D), match1(rowrec, q, D), ALU.mult)\
                        .then_inc(S("att_rows"), 1)
                a0 = ATT[L] * 3
                for q in range(3):
                    lo, hi = PIECES[q]
                    dve.wait_ge(S("att_rows"), a0 + q + 1)
                    if L == "L1":
                        dve.tensor_tensor(x[:, lo:hi, :], x[:, lo:hi, :], rows_a[:, lo:hi, :], ALU.add)\
                            .then_inc(S("x_updates"), 1)
                        continue
                    if sign == 1:
                        dve.tensor_tensor(rows_a[:, lo:hi, :], rows_c[:, lo:hi, :], rows_a[:, lo:hi, :],
                                          ALU.subtract).then_inc(S("att_diff"), 1)
                        dve.wait_ge(S("att_diff"), q + 1)
                    dve.tensor_scalar(rows_b[:, lo:hi, :], rows_a[:, lo:hi, :], 0.0, None, ALU.min)\
                        .then_inc(S("elu_in"), 1)
                if L == "L1":
                    continue
                for q in range(3):
                    lo, hi = PIECES[q]
                    dve.wait_ge(S("elu_exp"), 3 * ELU[L] + q + 1)
                    dve.scalar_tensor_tensor(rows_a[:, lo:hi, :], rows_a[:, lo:hi, :], 0.0, rows_b[:, lo:hi, :],
                                             ALU.max, ALU.add).then_inc(S("elu_sum"), 1)
                    dve.wait_ge(S("elu_sum"), 3 * ELU[L] + q + 1)
                    dve.scalar_tensor_tensor(x[:, lo:hi, :], rows_a[:, lo:hi, :], -1.0, x[:, lo:hi, :],
                                             ALU.add, ALU.add).then_inc(S("x_updates"), 1)

        TNUM = [0, 1, 2]
        ATT = {"L0": 0, "L1": 1, "L3": 2}

        MOE = {"L0": 0, "L2": 1}
        ITEMS = {L: NG * HC[L] for L in HC}
        BASE = {"L0": 0, "L2": E * ITEMS["L0"]}

        def moe_items(L):
            out = []
            for s in range(2):
                for c in range(NG):
                    for k in range(HC[L]):
                        out.append((len(out), s, c, k))
            return out

        def moe_tensor(pe, L, n):
            m, items, base = MOE[L], moe_items(L), BASE[L]
            per = len(items)
            hT_ready(pe, n)
            pe.wait_ge(S("moe_loaded"), 16 * 9)
            for i in range(NT):
                mm = pe.matmul(ps[:, 0, i * E:(i + 1) * E], hT[:, i * P:(i + 1) * P], gate_w[:, m, :],
                               start=True, stop=True)
            mm.then_inc(S("gates"), 1)

            def up(jj, item, extra=0):
                i, s, c, k = item
                at = jj * per + (base + i + extra)
                if (c, k) == (0, 0):
                    pe.wait_ge(S(f"expert_w{s}"), (jj + (1 if extra else 0) + 1) * 32 + 32 * 4 * m)
                pe.wait_ge(S("act_h"), at + 1)
                pe.matmul(ps[:, 4 + i % RING, :], w1_e[:, s, k * P:(k + 1) * P], hT[:, c * 512:(c + 1) * 512],
                          start=True, stop=True).then_inc(S("up"), 1)

            def down(jj, item):
                i, s, c, k = item
                pe.wait_ge(S("mul_h"), jj * per + (base + i + 1 + RING))
                pe.matmul(ps[:, c, :], w2_e[:, s, k, :], mul_h[:, i % RING, :], start=False, stop=False,
                          skip_group_check=True).then_inc(S("down"), 1)

            for i in range(LAG):
                up(0, items[i])
            pe.wait_ge(S("comb"), m + 1)
            pe.transpose(ps[:, 1, 0:P], comb[:, :, :].rearrange("p e i -> p (e i)"), ident[:, :])\
                .then_inc(S("comb_turned"), 1)
            pe.wait_ge(S("comb8"), 16 * (m + 1))
            pe.wait_ge(S("comb_T"), m + 1)
            for c in range(NG):
                mm = pe.matmul(ps[:, c, :], b2[:, m, :], comb8[:, c * 512:(c + 1) * 512], start=True, stop=False,
                               skip_group_check=True)
            mm.then_inc(S("b2_in"), 1)
            pe.wait_ge(S("b2_in"), m + 1)
            with pe.Fori(0, E // 2 - 1) as jj:
                for i in range(per):
                    if i + LAG < per:
                        up(jj, items[i + LAG])
                    else:
                        up(jj, items[i + LAG - per], per)
                    down(jj, items[i])
            for i in range(per):
                if i + LAG < per:
                    up(E // 2 - 1, items[i + LAG])
                down(E // 2 - 1, items[i])
            for c in range(NG):
                pe.wait_ge(S("out_T"), NG * m + c + 1)
                for i in range(4):
                    mm = pe.transpose(ps[:, 4 + c, i * P:(i + 1) * P], out_T[:, c, i * P:(i + 1) * P], ident[:, :])
                mm.then_inc(S("out_turned"), 1)

        def moe_scalar(act, L, n):
            m, items, base = MOE[L], moe_items(L), BASE[L]
            per = len(items)
            act.wait_ge(S("moe_loaded"), 16 * 9)
            if L == "L2":
                act.wait_ge(S("top"), 2 * RANK_STEPS + 1)
                act.activation(topm[:, 4, :], topm[:, 4, :], ACT.Exp).then_inc(S("top_exp"), 1)
            with act.Fori(0, E // 2) as jj:
                for i, s, c, k in items:
                    at = jj * per + (base + i)
                    act.wait_ge(S("up"), at + 1)
                    act.wait_ge(S("mul_h"), at + 1)
                    act.sem_inc(S("act_seen"), 1)
                    act.activation(act_h[:, i % RING, :], ps[:, 4 + i % RING, :], ACT.Gelu if L == "L0" else ACT.Relu,
                                   bias=b1_T[L][:, bass.ds(jj * (2 * HC[L]) + (s * HC[L] + k), 1)])\
                        .then_inc(S("act_h"), 1)
            act.wait_ge(S("down"), BASE[L] + E * ITEMS[L] + RING)
            for c in range(NG):
                act.copy(out_T[:, c, :], ps[:, c, :]).then_inc(S("out_T"), 1)

        RANK_STEPS = 11

        def moe_vector(dve, L, n):
            m, items, base = MOE[L], moe_items(L), BASE[L]
            per = len(items)
            count = [RANK_STEPS * m]

            def step(ins):
                ins.then_inc(S("top"), 1)
                count[0] += 1
                dve.wait_ge(S("top"), count[0])

            def over_e(ap):
                return ap.unsqueeze(2).to_broadcast([P, NT, E])

            def over_i(ap):
                return ap.unsqueeze(1).to_broadcast([P, NT, E])

            sc, key, oh1, oh2, sc2 = (top[:, q, :, :] for q in range(5))
            m1, m2, k1 = (topm[:, q, :] for q in range(3))
            dve.wait_ge(S("moe_loaded"), 16 * 9)
            dve.wait_ge(S("gates"), m + 1)
            step(dve.tensor_tensor(sc, ps[:, 0, 0:NT * E].rearrange("p (i e) -> p i e", e=E),
                                   over_i(gate_b[:, m, :]), ALU.add))
            step(dve.tensor_reduce(m1, sc, AX.X, ALU.max))
            step(dve.tensor_tensor(key, sc, over_e(m1), ALU.is_equal))
            step(dve.tensor_tensor(key, key, over_i(first[:, :]), ALU.mult))
            step(dve.tensor_reduce(k1, key, AX.X, ALU.max))
            step(dve.tensor_tensor(oh1, key, over_e(k1), ALU.is_equal))
            step(dve.scalar_tensor_tensor(sc2, oh1, -3.0e38, sc, ALU.mult, ALU.add))
            step(dve.tensor_reduce(m2, sc2, AX.X, ALU.max))
            step(dve.tensor_tensor(key, sc2, over_e(m2), ALU.is_equal))
            step(dve.tensor_tensor(key, key, over_i(first[:, :]), ALU.mult))
            step(dve.tensor_reduce(k1, key, AX.X, ALU.max))
            by_e = comb[:, :, :].rearrange("p e i -> p i e")
            if L == "L0":
                dve.tensor_tensor(oh2, key, over_e(k1), ALU.is_equal).then_inc(S("oh2"), 1)
                dve.wait_ge(S("oh2"), 1)
                dve.tensor_tensor(by_e, oh1, oh2, ALU.add).then_inc(S("comb"), 1)
            else:
                p1, p2 = topm[:, 5, :], topm[:, 6, :]
                step(dve.tensor_tensor(topm[:, 4, :], m2, m1, ALU.subtract))

                step(dve.tensor_tensor(oh2, key, over_e(k1), ALU.is_equal))
                dve.wait_ge(S("top_exp"), 1)
                step(dve.tensor_scalar(p1, topm[:, 4, :], 1.0, None, ALU.add))
                step(dve.reciprocal(p1, p1))
                step(dve.tensor_tensor(p2, topm[:, 4, :], p1, ALU.mult))
                dve.tensor_tensor(oh1, oh1, over_e(p1), ALU.mult).then_inc(S("oh2"), 1)
                dve.tensor_tensor(oh2, oh2, over_e(p2), ALU.mult).then_inc(S("oh2"), 1)
                dve.wait_ge(S("oh2"), 3)
                dve.tensor_tensor(by_e, oh1, oh2, ALU.add).then_inc(S("comb"), 1)
            dve.wait_ge(S("comb_turned"), m + 1)
            dve.tensor_copy(comb_T[:, :], ps[:, 1, 0:P]).then_inc(S("comb_T"), 1)
            with dve.Fori(0, E // 2) as jj:
                for i, s, c, k in items:
                    at = jj * per + (base + i)
                    if (c, k) == (0, 0):
                        dve.wait_ge(S(f"comb_b{s}"), jj * 16 + 16 * (4 * m + 1))
                    dve.wait_ge(S("act_h"), at + 1 + RING)
                    dve.wait_ge(S("down"), at + 1)
                    dve.tensor_tensor(mul_h[:, i % RING, :], act_h[:, i % RING, :],
                                      comb_b[:, s, c * 512:(c + 1) * 512], ALU.mult).then_inc(S("mul_h"), 1)
            for c in range(NG):
                dve.wait_ge(S("out_turned"), NG * m + c + 1)
                dve.tensor_tensor(x[:, 4 * c:4 * c + 4, :], x[:, 4 * c:4 * c + 4, :],
                                  ps[:, 4 + c, :].rearrange("p (i d) -> p i d", d=D), ALU.add)\
                    .then_inc(S("x_updates"), 1)

        def moe_sync(sp, L, n):
            m, base = MOE[L], BASE[L]
            H = HC[L] * P
            w1, w2 = t[f"{L}_ffn_W1"], t[f"{L}_ffn_W2"]

            def weights(e, s):
                sp.dma_start(w1_e[:, s, 0:H], w1[bass.ds(e, 1), :, :].rearrange("e d h -> d (e h)"))\
                    .then_inc(S(f"expert_w{s}"), 16)
                sp.dma_start(w2_e[:, s, 0:HC[L], :],
                             w2[bass.ds(e, 1), :, :].rearrange("e (k p) d -> p (e k) d", p=P))\
                    .then_inc(S(f"expert_w{s}"), 16)

            def mix(e, s):
                sp.dma_start(comb_b[:, s, :],
                             comb_dram[L][bass.ds(e, 1), :].to_broadcast([P, N])).then_inc(S(f"comb_b{s}"), 16)

            for s in range(2):
                if m:
                    sp.wait_ge(S("down"), BASE["L2"] + RING)
                weights(s, s)
            sp.wait_ge(S("comb_T"), m + 1)
            sp.dma_start(comb_dram[L].rearrange("e (i n) -> (e i) n", n=P), comb_T[:, :]).then_inc(S("comb_out"), 16)
            sp.wait_ge(S("comb_out"), 16 * (m + 1))
            sp.dma_start(comb8, comb_dram[L][:, :]).then_inc(S("comb8"), 16)
            for s in range(2):
                mix(s, s)
            with sp.Fori(1, E // 2) as jj:
                for s in range(2):
                    e = jj * 2 + s
                    sp.wait_ge(S("mul_h"), e * ITEMS[L] + (base - ITEMS[L] + RING))
                    mix(e, s)
                    sp.wait_ge(S("down"), e * ITEMS[L] + (base - ITEMS[L] + RING))
                    weights(e, s)

        PARTS = [(0, 0, P), (1, P, P), (2, 2 * P, NS), (3, 2 * P + NS, NS)]
        HALO = 3

        def on_chunk(eng, g, name, k):
            eng.wait_ge(S(name), g * 4 + (k + 1 + 2))

        def on_group(eng, g, name, k, per=1):
            eng.wait_ge(S(name), g * per + (k + 2) * per)

        CHUNKS = ["m_turned", "m_rows", "m_tri_dA", "m_segsum", "m_decay", "m_mix", "m_x_dt", "m_x_decayed",
                  "m_x_skip", "m_y_parts", "m_state_new", "m_state", "m_y_sum", "m_y_skip", "m_y_gated",
                  "m_yT_turned", "m_yT", "m_out", "m_y_rows", "m_square"]
        GROUPS = {"m_conv_in": 1, "m_conv_raw": 4, "m_conv_seed": 4, "m_conv_tap": 12, "m_conv_tanh": 2, "m_conv": 2,
                  "m_cb": 1, "m_cb_masked": 1, "m_halo": 1}

        def mamba_tensor(pe, n):
            pe.wait_ge(S("mamba_loaded"), 16 * 10)
            hT_ready(pe, n)
            for k in range(2):
                mm = pe.matmul(ps[:, 5, k * P:(k + 1) * P], wout_T[:, k, :], w_lin[:, :], start=True, stop=True)
            mm.then_inc(S("m_proj"), 1)
            pe.wait_ge(S("m_halved"), 3)
            for i in range(NT):
                if i >= 4:
                    pe.wait_ge(S("m_z_gate"), i - 3)
                    pe.wait_ge(S("m_dt_raw"), i - 3)
                pe.matmul(ps[:, i % 4, 0:DI + NH], hT[:, i * P:(i + 1) * P], win_zd[:, :], start=True, stop=True)\
                    .then_inc(S("m_zd"), 1)
            pe.wait_ge(S("m_dA"), 1)
            pe.matmul(ps[:, 4, 0:64], tri[:, :], dts[:, 4, :], start=True, stop=True)
            pe.matmul(ps[:, 4, 64:128], ones[:, :], dts[:, 4, :], start=True, stop=True).then_inc(S("m_cum"), 1)
            pe.wait_ge(S("m_carry"), 1)
            with pe.Fori(0, NG) as g:
                on_chunk(pe, g, "m_y_sum", -1)
                on_chunk(pe, g, "m_state", -1)
                on_chunk(pe, g, "m_y_rows", -1)
                for q, c0, w in PARTS:
                    mm = pe.matmul(ps[0:w, q, :], win_x[:, c0:c0 + w], hT[:, bass.ts(g, 512)], start=True, stop=True)
                mm.then_inc(S("m_conv_in"), 1)
                on_group(pe, g, "m_conv", 0, 2)
                for i in range(4):
                    on_chunk(pe, g, "m_rows", i - 2)
                    bank = 4 + i % 2
                    for q in range(2):
                        pe.transpose(ps[:, bank, q * P:(q + 1) * P], conv[:, q, i * P:(i + 1) * P], ident[:, :])
                    pe.transpose(ps[:, bank, DI:DI + NS], conv[0:NS, 2, i * P:(i + 1) * P], ident[0:NS, 0:NS])\
                        .then_inc(S("m_turned"), 1)
                on_group(pe, g, "m_cb_masked", -1)
                for i in range(4):
                    mm = pe.matmul(ps[:, 6, i * P:(i + 1) * P], conv[0:NS, 2, i * P:(i + 1) * P],
                                   conv[0:NS, 3, i * P:(i + 1) * P], start=True, stop=True)
                mm.then_inc(S("m_cb"), 1)

                def segsum(i):
                    on_chunk(pe, g, "m_tri_dA", i)
                    on_chunk(pe, g, "m_decay", i - 1)
                    pe.matmul(ps[:, 7, :], after[:, :], tri_dA[:, i % 2, :], start=True, stop=True)\
                        .then_inc(S("m_segsum"), 1)

                def tail(i):
                    on_chunk(pe, g, "m_y_gated", i)
                    on_chunk(pe, g, "m_y_rows", i - 1)
                    for k in range(2):
                        mm = pe.transpose(ps[:, 3, k * P:(k + 1) * P], y_gated[:, i % 2, k * P:(k + 1) * P],
                                          ident[:, :])
                    mm.then_inc(S("m_yT_turned"), 1)
                    on_chunk(pe, g, "m_yT", i)
                    for k in range(2):
                        mm = pe.matmul(ps[:, 3, DI:DI + D], y_T[:, i % 2, k * P:(k + 1) * P], w_proj[:, k, :],
                                       start=(k == 0), stop=(k == 1))
                    mm.then_inc(S("m_out"), 1)

                segsum(0)
                for i in range(4):
                    if i < 3:
                        segsum(i + 1)
                    on_chunk(pe, g, "m_state", i - 1)
                    on_chunk(pe, g, "m_y_sum", i - 2)
                    pe.matmul(ps[:, i % 2, DI:2 * DI], conv[0:NS, 3, i * P:(i + 1) * P], state[:, :],
                              start=True, stop=True)
                    on_chunk(pe, g, "m_mix", i)
                    on_chunk(pe, g, "m_x_dt", i)
                    for h in range(NH):
                        mm = pe.matmul(ps[:, i % 2, h * HD:(h + 1) * HD], mixm[:, i % 2, h * P:(h + 1) * P],
                                       x_dt[:, i % 2, h * HD:(h + 1) * HD], start=True, stop=True)
                    mm.then_inc(S("m_y_parts"), 1)
                    on_chunk(pe, g, "m_x_decayed", i)
                    pe.matmul(ps[0:NS, 2, 0:DI], xb_rows[:, i, DI:DI + NS], x_decayed[:, i % 2, :],
                              start=True, stop=True).then_inc(S("m_state_new"), 1)
                    if i >= 1:
                        tail(i - 1)
                tail(3)

        def mamba_scalar(act, n):
            act.wait_ge(S("mamba_loaded"), 16 * 10)
            act.activation(exp_A[:, :], small_in[:, 1, :], ACT.Exp).then_inc(S("m_expA"), 1)
            for i in range(NT):
                act.wait_ge(S("m_zd"), i + 1)
                if i >= 2:
                    act.wait_ge(S("m_z_gate"), i - 1)
                act.activation(z_tanh[:, i % 2, :], ps[:, i % 4, 0:DI], ACT.Tanh).then_inc(S("m_z_tanh"), 1)
            act.wait_ge(S("m_dt_abs"), 1)
            act.activation(dts[:, 2, :], dts[:, 1, :], ACT.Exp, scale=-1.0).then_inc(S("m_dt_exp"), 1)
            act.wait_ge(S("m_dt_exp"), 1)
            act.activation(dts[:, 5, :], dts[:, 2, :], ACT.Ln, bias=1.0).then_inc(S("m_dt_ln"), 1)
            act.wait_ge(S("m_cum"), 1)
            act.activation(carry[:, :, :], ps[:, 4, 0:128].rearrange("p (s n) -> p s n", s=2), ACT.Exp)\
                .then_inc(S("m_carry"), 1)
            with act.Fori(0, NG) as g:
                on_group(act, g, "m_conv_in", 0)
                on_group(act, g, "m_conv", -1, 2)
                act.copy(conv_raw[:, :, 0:HALO], conv_raw[:, :, 512:512 + HALO]).then_inc(S("m_halo"), 1)
                on_group(act, g, "m_halo", 0)
                on_chunk(act, g, "m_y_parts", -1)
                for q, c0, w in PARTS:
                    act.copy(conv_raw[0:w, q, HALO:HALO + 512], ps[0:w, q, :]).then_inc(S("m_conv_raw"), 1)
                    act.activation(conv[0:w, q, :], ps[0:w, q, :], ACT.Identity, bias=conv_b[0:w, q:q + 1],
                                   scale=conv_w[0:w, q, HALO:HALO + 1]).then_inc(S("m_conv_seed"), 1)
                on_group(act, g, "m_conv_tap", 0, 12)
                act.activation(conv_tanh[:, 0:2, :], conv[:, 0:2, :], ACT.Tanh).then_inc(S("m_conv_tanh"), 1)
                act.activation(conv_tanh[0:NS, 2:4, :], conv[0:NS, 2:4, :], ACT.Tanh).then_inc(S("m_conv_tanh"), 1)
                on_chunk(act, g, "m_state_new", -1)
                on_chunk(act, g, "m_x_skip", -1)
                for i in range(4):
                    on_chunk(act, g, "m_turned", i)
                    act.copy(xb_rows[:, i, :], ps[:, 4 + i % 2, 0:DI + NS]).then_inc(S("m_rows"), 1)

                def tail(i):
                    on_chunk(act, g, "m_yT_turned", i)
                    on_chunk(act, g, "m_out", i - 2)
                    act.copy(y_T[:, i % 2, :], ps[:, 3, 0:DI]).then_inc(S("m_yT"), 1)
                    on_chunk(act, g, "m_square", i - 1)
                    act.activation(y_square[:, :], y_gated[:, i % 2, :], ACT.Square,
                                   accum_out=sumsq[:, bass.ds(g * 4 + i, 1)]).then_inc(S("m_square"), 1)
                    on_chunk(act, g, "m_out", i)
                    act.copy(y_rows[:, bass.ds(g * 4 + i, 1), :], ps[:, 3, DI:DI + D]).then_inc(S("m_y_rows"), 1)

                for i in range(4):
                    on_chunk(act, g, "m_segsum", i)
                    on_chunk(act, g, "m_mix", i - 2)
                    on_chunk(act, g, "m_x_decayed", i - 2)
                    act.activation(decay[:, i % 2, :], ps[:, 7, :], ACT.Exp).then_inc(S("m_decay"), 1)
                    if i >= 1:
                        tail(i - 1)
                tail(3)
            act.wait_ge(S("m_square"), NT + 2)
            act.activation(sumsq[:, :], sumsq[:, :], ACT.Sqrt, scale=1.0 / DI, bias=EPS).then_inc(S("m_rms"), 1)

        def mamba_pool(pool):
            pool.wait_ge(S("m_dA"), 1)
            with pool.Fori(0, NG) as g:
                def heads(ap, c, w):
                    return ap[:, bass.ds(g * 16 + c * NH, NH)].unsqueeze(2).to_broadcast([P, NH, w])

                def tri_times(i):
                    on_chunk(pool, g, "m_segsum", i - 2)
                    pool.tensor_tensor(tri_dA[:, i % 2, :].rearrange("p (h l) -> p h l", h=NH),
                                       tri[:, :].unsqueeze(1).to_broadcast([P, NH, P]), heads(dts[:, 4, :], i, P),
                                       ALU.mult).then_inc(S("m_tri_dA"), 1)

                tri_times(0)
                for i in range(4):
                    if i < 3:
                        tri_times(i + 1)
                    on_chunk(pool, g, "m_rows", i)
                    on_chunk(pool, g, "m_y_parts", i - 2)
                    on_chunk(pool, g, "m_x_decayed", i - 2)
                    x3 = xb_rows[:, i, 0:DI].rearrange("p (h d) -> p h d", h=NH)
                    pool.tensor_tensor(x_dt[:, i % 2, :].rearrange("p (h d) -> p h d", h=NH), x3,
                                       heads(dts[:, 3, :], i, HD), ALU.mult).then_inc(S("m_x_dt"), 1)
                    on_chunk(pool, g, "m_y_skip", i - 2)
                    pool.tensor_tensor(x_skip[:, i % 2, :].rearrange("p (h d) -> p h d", h=NH), x3,
                                       small_in[:, 2, :].unsqueeze(2).to_broadcast([P, NH, HD]), ALU.mult)\
                        .then_inc(S("m_x_skip"), 1)
                    on_chunk(pool, g, "m_x_dt", i)
                    on_chunk(pool, g, "m_decay", i)
                    on_chunk(pool, g, "m_state_new", i - 2)
                    last = decay[:, i % 2, :].rearrange("p (h l) -> p h l", h=NH)[:, :, P - 1]
                    pool.tensor_tensor(x_decayed[:, i % 2, :].rearrange("p (h d) -> p h d", h=NH),
                                       x_dt[:, i % 2, :].rearrange("p (h d) -> p h d", h=NH),
                                       last.unsqueeze(2).to_broadcast([P, NH, HD]), ALU.mult)\
                        .then_inc(S("m_x_decayed"), 1)

        def mamba_vector(dve, n):
            dve.wait_ge(S("mamba_loaded"), 16 * 10)
            dve.tensor_scalar(win_zd[:, 0:DI], win_zd[:, 0:DI], 0.5, None, ALU.mult).then_inc(S("m_halved"), 1)
            dve.tensor_scalar(conv_w[:, :, :], conv_w[:, :, :], 0.5, None, ALU.mult).then_inc(S("m_halved"), 1)
            dve.tensor_scalar(conv_b[:, :], conv_b[:, :], 0.5, None, ALU.mult).then_inc(S("m_halved"), 1)
            dve.memset(ones[:, :], 1.0).then_inc(S("m_clear"), 1)
            dve.memset(conv_raw[:, :, :], 0.0).then_inc(S("m_clear"), 1)
            dve.memset(state[:, :], 0.0).then_inc(S("m_clear"), 1)
            dve.wait_ge(S("m_proj"), 1)
            for k in range(2):
                dve.tensor_scalar(w_proj[:, k, :], ps[:, 5, k * P:(k + 1) * P], norm_w[:, k:k + 1], None, ALU.mult)\
                    .then_inc(S("m_clear"), 1)
            dve.wait_ge(S("m_clear"), 5)
            for i in range(NT):
                dve.wait_ge(S("m_z_tanh"), i + 1)
                dve.tensor_copy(dts[:, 0, i * NH:(i + 1) * NH], ps[:, i % 4, DI:DI + NH]).then_inc(S("m_dt_raw"), 1)
                dve.scalar_tensor_tensor(z_gate[:, i, :], z_tanh[:, i % 2, :], 1.0, ps[:, i % 4, 0:DI],
                                         ALU.add, ALU.mult).then_inc(S("m_z_gate"), 1)
            dt3 = [dts[:, q, :].rearrange("p (c h) -> p c h", h=NH) for q in range(6)]
            dve.wait_ge(S("m_dt_raw"), NT)
            dve.tensor_tensor(dt3[0], dt3[0], small_in[:, 0, :].unsqueeze(1).to_broadcast([P, NT, NH]), ALU.add)\
                .then_inc(S("m_dt_bias"), 1)
            dve.wait_ge(S("m_dt_bias"), 1)
            dve.scalar_tensor_tensor(dts[:, 1, :], dts[:, 0, :], -1.0, dts[:, 0, :], ALU.mult, ALU.max)\
                .then_inc(S("m_dt_abs"), 1)
            dve.wait_ge(S("m_dt_ln"), 1)
            dve.scalar_tensor_tensor(dts[:, 3, :], dts[:, 0, :], 0.0, dts[:, 5, :], ALU.max, ALU.add)\
                .then_inc(S("m_dt_bias"), 1)
            dve.wait_ge(S("m_dt_bias"), 2)
            dve.wait_ge(S("m_expA"), 1)
            dve.scalar_tensor_tensor(dt3[4], dt3[3], -1.0, exp_A[:, :].unsqueeze(1).to_broadcast([P, NT, NH]),
                                     ALU.mult, ALU.mult).then_inc(S("m_dA"), 1)
            dve.wait_ge(S("m_carry"), 1)
            with dve.Fori(0, NG) as g:
                def heads(ap, rows, c, w):
                    return ap[0:rows, bass.ds(g * 16 + c * NH, NH)].unsqueeze(2).to_broadcast([rows, NH, w])

                for k in range(HALO):
                    for q, c0, w in PARTS:
                        if k == 0:
                            dve.wait_ge(S("m_conv_seed"), g * 4 + (q + 1 + 4))
                        else:
                            dve.wait_ge(S("m_conv_tap"), g * 12 + (12 + 4 * k + q - 3))
                        dve.scalar_tensor_tensor(conv[0:w, q, :], conv_raw[0:w, q, k:k + 512],
                                                 conv_w[0:w, q, k:k + 1], conv[0:w, q, :], ALU.mult, ALU.add)\
                            .then_inc(S("m_conv_tap"), 1)
                dve.wait_ge(S("m_conv_tanh"), g * 2 + 3)
                dve.scalar_tensor_tensor(conv[:, 0:2, :], conv_tanh[:, 0:2, :], 1.0, conv[:, 0:2, :],
                                         ALU.add, ALU.mult).then_inc(S("m_conv"), 1)
                dve.wait_ge(S("m_conv_tanh"), g * 2 + 4)
                dve.scalar_tensor_tensor(conv[0:NS, 2:4, :], conv_tanh[0:NS, 2:4, :], 1.0, conv[0:NS, 2:4, :],
                                         ALU.add, ALU.mult).then_inc(S("m_conv"), 1)
                on_group(dve, g, "m_cb", 0)
                on_chunk(dve, g, "m_mix", -1)
                dve.tensor_tensor(cb_masked[:, :, :], ps[:, 6, :].rearrange("p (i l) -> p i l", i=4),
                                  tri[:, :].unsqueeze(1).to_broadcast([P, 4, P]), ALU.mult)\
                    .then_inc(S("m_cb_masked"), 1)
                on_group(dve, g, "m_cb_masked", 0)
                for i in range(4):
                    b = i % 2
                    on_chunk(dve, g, "m_decay", i)
                    on_chunk(dve, g, "m_y_parts", i - 2)
                    dve.tensor_tensor(mixm[:, b, :].rearrange("p (h l) -> p h l", h=NH),
                                      decay[:, b, :].rearrange("p (h l) -> p h l", h=NH),
                                      cb_masked[:, i, :].unsqueeze(1).to_broadcast([P, NH, P]), ALU.mult)\
                        .then_inc(S("m_mix"), 1)
                    on_chunk(dve, g, "m_y_parts", i)
                    on_chunk(dve, g, "m_y_sum", i - 1)
                    dve.tensor_tensor(y_a[:, :].rearrange("p (h d) -> p h d", h=NH),
                                      ps[:, b, DI:2 * DI].rearrange("p (h d) -> p h d", h=NH),
                                      heads(carry[:, 0, :], P, i, HD), ALU.mult).then_inc(S("m_y_a"), 1)
                    on_chunk(dve, g, "m_state_new", i)
                    dve.tensor_tensor(state.rearrange("p (h d) -> p h d", h=NH),
                                      state.rearrange("p (h d) -> p h d", h=NH),
                                      heads(carry[:, 1, :], NS, i, HD), ALU.mult).then_inc(S("m_state_aged"), 1)
                    dve.wait_ge(S("m_y_a"), g * 4 + (i + 1))
                    on_chunk(dve, g, "m_y_skip", i - 1)
                    dve.tensor_tensor(y_b[:, :], y_a[:, :], ps[:, b, 0:DI], ALU.add).then_inc(S("m_y_sum"), 1)
                    dve.wait_ge(S("m_state_aged"), g * 4 + (i + 1))
                    dve.tensor_tensor(state[:, :], state[:, :], ps[0:NS, 2, 0:DI], ALU.add)\
                        .then_inc(S("m_state"), 1)
                    on_chunk(dve, g, "m_y_sum", i)
                    on_chunk(dve, g, "m_x_skip", i)
                    on_chunk(dve, g, "m_yT_turned", i - 2)
                    on_chunk(dve, g, "m_square", i - 2)
                    dve.tensor_tensor(y_b[:, :], y_b[:, :], x_skip[:, b, :], ALU.add).then_inc(S("m_y_skip"), 1)
                    on_chunk(dve, g, "m_y_skip", i)
                    dve.tensor_tensor(y_gated[:, b, :], y_b[:, :], z_gate[:, bass.ds(g * 4 + i, 1), :], ALU.mult)\
                        .then_inc(S("m_y_gated"), 1)
            dve.wait_ge(S("m_rms"), 1)
            dve.reciprocal(sumsq[:, :], sumsq[:, :]).then_inc(S("m_rms_inv"), 1)
            dve.wait_ge(S("m_y_rows"), NT + 2)
            dve.wait_ge(S("m_x_bias"), 1)
            dve.wait_ge(S("m_rms_inv"), 1)
            for i in range(NT):
                dve.scalar_tensor_tensor(x[:, i, :], y_rows[:, i, :], sumsq[:, i:i + 1], x[:, i, :],
                                         ALU.mult, ALU.add).then_inc(S("x_updates"), 1)

        def add_to_rows(pool, n, bias, name, loaded, count):
            hT_ready(pool, n)
            pool.wait_ge(S(loaded), 16 * count)
            pool.tensor_tensor(x[:, :, :], x[:, :, :], bias[:, :].unsqueeze(1).to_broadcast([P, NT, D]), ALU.add)\
                .then_inc(S(name), 1)

        PW = 3 * D + 1

        def sage_tensor(pe, n):
            pe.wait_ge(S("sage_loaded"), 16 * 2)
            hT_ready(pe, n)
            for i in range(NT):
                pe.matmul(ps[:, i // 2, (i % 2) * 2 * D:(i % 2 + 1) * 2 * D], hT[:, i * P:(i + 1) * P], sage_w[:, :],
                          start=True, stop=True).then_inc(S("g_in"), 1)
            pe.wait_ge(S("g_y"), 5 * NG + 1)
            with pe.Fori(0, NT // 2) as ii:
                for b in range(2):
                    pe.wait_ge(S("g_x"), ii * 2 + (b + 1 + NG))
                    for j in range(NT):
                        mm = pe.matmul(ps[:, b, 0:PW], adjT[:, j, bass.ds(ii * 2 * P + b * P, P)],
                                       sage_y[:, j, 0:PW], start=(j == 0), stop=(j == NT - 1))
                    mm.then_inc(S("g_sums"), 1)

        def sage_vector(dve, n):
            dve.wait_ge(S("g_x_bias"), 1)
            dve.memset(sage_y[:, :, 3 * D:PW], 1.0).then_inc(S("g_y"), 1)
            for c in range(NG):
                a = slice(4 * c, 4 * c + 4)
                psy = ps[:, 2 * c:2 * c + 2, :].rearrange("p b (k d) -> p b k d", k=2)
                four = lambda ap: ap.rearrange("p (b k) d -> p b k d", k=2)
                dve.wait_ge(S("g_in"), 4 * c + 4)
                k = 1 + 5 * c
                dve.tensor_copy(four(sage_y[:, a, 0:D]), psy[:, :, :, 0:D]).then_inc(S("g_y"), 1)
                dve.wait_ge(S("g_y"), k + 1)
                dve.tensor_tensor(four(sage_r[:, a, :]), psy[:, :, :, 0:D], four(sage_y[:, a, 0:D]), ALU.subtract)\
                    .then_inc(S("g_y"), 1)
                dve.wait_ge(S("g_y"), k + 2)
                dve.tensor_copy(sage_y[:, a, D:2 * D], sage_r[:, a, :]).then_inc(S("g_y"), 1)
                dve.wait_ge(S("g_y"), k + 3)
                dve.tensor_tensor(sage_r[:, a, :], sage_r[:, a, :], sage_y[:, a, D:2 * D], ALU.subtract)\
                    .then_inc(S("g_y"), 1)
                dve.wait_ge(S("g_y"), k + 4)
                dve.tensor_copy(sage_y[:, a, 2 * D:3 * D], sage_r[:, a, :]).then_inc(S("g_y"), 1)
            for c in range(NG):
                psy = ps[:, 2 * c:2 * c + 2, :].rearrange("p b (k d) -> p b k d", k=4)
                x4 = x[:, 4 * c:4 * c + 4, :].rearrange("p (b k) d -> p b k d", k=2)
                dve.tensor_tensor(x4, x4, ps[:, 2 * c:2 * c + 2, :].rearrange("p b (k s d) -> p b k s d", k=2, s=2)
                                  [:, :, :, 1, :], ALU.add).then_inc(S("g_x"), 1)
            with dve.Fori(0, NT // 2) as ii:
                for b in range(2):
                    at = ii * 2 + b
                    dve.wait_ge(S("g_sums"), at + 1)
                    dve.reciprocal(sage_rec[:, b:b + 1], ps[:, b, 3 * D:PW]).then_inc(S("g_rec"), 1)
                    dve.tensor_reduce(sage_sum[:, b, :], ps[:, b, 0:3 * D].rearrange("p (s d) -> p d s", s=3), AX.X,
                                      ALU.add).then_inc(S("g_x"), 1)
                    dve.wait_ge(S("g_rec"), at + 1)
                    dve.wait_ge(S("g_x"), at + (NG + 2 + 1))
                    dve.scalar_tensor_tensor(x[:, bass.ds(at, 1), :], sage_sum[:, b, :], sage_rec[:, b:b + 1],
                                             x[:, bass.ds(at, 1), :], ALU.mult, ALU.add)\
                        .then_inc(S("x_updates"), 1)

        def on_tile(eng, g, name, k):
            eng.wait_ge(S(name), g * 4 + (k + 1 + 2))

        last = {name: NT + 2 for name in CHUNKS} | {name: (NG + 1) * per for name, per in GROUPS.items()}
        last |= {"m_zd": NT, "m_z_tanh": NT, "m_z_gate": NT, "m_dt_raw": NT, "m_dt_bias": 2, "m_dt_abs": 1,
                 "m_dt_exp": 1, "m_dt_ln": 1, "m_dA": 1, "m_cum": 1, "m_carry": 1, "m_y_a": NT, "m_state_aged": NT}
        signals = """y_A_min y_block y_cb y_cbm y_clear y_conv y_conv_in y_dec y_dec_cb y_dt y_dt_abs y_dt_in y_exp y_fD y_gT y_gT_w y_gated y_halved y_ln y_mix y_normed y_o y_q y_raw y_rms y_rows y_slice_w y_spans y_ss y_t y_tanh y_tap y_tdA y_turned y_y y_z y_z_in y_z_tanh""".split()
        reused.update({y: (m, last[m]) for y, m in zip(signals, sorted(last), strict=False)})

        def after_mamba(name, count):
            return reused[name][1] + count

        TILES = ["s_logits", "s_add", "s_maxed", "s_sub", "s_exped", "s_summed", "s_rec", "s_sw", "s_acc", "s_A",
                 "s_turned", "s_swT"]
        S_LOADED = 16 * 20
        HPARTS = [(0, P), (1, P), (2, P), (3, P), (4, NS), (5, NS)]

        def heads8(ap, rows, w):
            return ap.unsqueeze(2).to_broadcast([rows, SH, w])

        def by_head(ap):
            return ap.rearrange("p (h g) -> p h g", h=SH)

        def slice_tensor(pe, n):
            pe.wait_ge(S("s_loaded"), S_LOADED)
            for h in range(SH):
                pe.matmul(ps[:, 0, h * SG:(h + 1) * SG], wx_h[:, h, :], ws_T, start=True, stop=True)
            for h in range(SH):
                mm = pe.matmul(ps[:, 1, h * SG:(h + 1) * SG], bx_T[:, h:h + 1].to_broadcast([NS, P]), ws_T,
                               start=True, stop=True)
            mm.then_inc(S("s_weights"), 1)
            pe.wait_ge(S("s_logit_w"), 2)
            pe.wait_ge(S("zeros"), 1)
            for w in range(0, SI, 256):
                mm = pe.matmul(ps[:, 2, w:w + 256], zeros[:, 0:P], zeros[:, 0:256], start=(w == 0), stop=False,
                               skip_group_check=True)
            mm.then_inc(S("s_cleared"), 1)
            pe.wait_ge(S("s_cleared"), 1)
            with pe.Fori(0, NG) as g:
                def logits(i):
                    on_tile(pe, g, "s_add", i - 2)
                    pe.matmul(ps[:, i % 2, :], s_hT[:, i * P:(i + 1) * P], logit_w, start=True, stop=True)\
                        .then_inc(S("s_logits"), 1)

                pe.wait_ge(S("s_staged"), g * 2 + 2)
                logits(0)
                for i in range(4):
                    if i < 3:
                        logits(i + 1)
                    on_tile(pe, g, "s_sw", i)
                    pe.matmul(ps[:, 2, :], s_h[:, i, :], s_sw[:, i % 2, :], start=False, stop=False,
                              skip_group_check=True).then_inc(S("s_A"), 1)
                    on_tile(pe, g, "s_swT", i - 2)
                    for k in range(4):
                        mm = pe.transpose(ps[:, 3 + i % 2, k * P:(k + 1) * P], s_sw[:, i % 2, k * P:(k + 1) * P],
                                          ident[:, :])
                    mm.then_inc(S("s_turned"), 1)
            pe.wait_ge(S("s_acc"), NT + 2)
            pe.matmul(ps[:, 5, :], ones[:, :], s_acc, start=True, stop=True).then_inc(S("s_norm"), 1)
            pe.wait_ge(S("s_AT"), 1)
            for k in range(4):
                mm = pe.matmul(ps[:, 6, k * P:(k + 1) * P], wfx_T[:, k * P:(k + 1) * P], A_T[:, k * P:(k + 1) * P],
                               start=True, stop=True)
            mm.then_inc(S("s_st"), 1)
            pe.wait_ge(S("s_stT"), 8)
            pe.wait_ge(S("s_swT"), NT + 2)
            for k in range(4):
                mm = pe.matmul(ps[0:SG, 1, 0:2 * SH], st_T[:, k, :], hy_in[:, k, SI * 2 + 2 * NS:HYP],
                               start=(k == 0), stop=(k == 3))
            mm.then_inc(S("y_dt_in"), 1)
            for q, w in HPARTS:
                c0 = SI + q * P if q < 4 else 2 * SI + (q - 4) * NS
                for k in range(4):
                    mm = pe.matmul(ps[0:w, 3, q * SG:(q + 1) * SG], hy_in[:, k, c0:c0 + w], st_T[:, k, :],
                                   start=(k == 0), stop=(k == 3))
            mm.then_inc(S("y_conv_in"), 1)
            for k in range(4):
                mm = pe.matmul(ps[0:SG, 0, :], st_T[:, k, :], hy_in[:, k, 0:SI], start=(k == 0), stop=(k == 3))
            mm.then_inc(S("y_z_in"), 1)
            pe.wait_ge(S("y_tdA"), after_mamba("y_tdA", 2))
            pe.wait_ge(S("s_loaded"), S_LOADED)
            pe.matmul(ps[0:SG, 4, :], after[0:SG, 0:SG], hy_tdA[:, 0, :], start=True, stop=True)\
                .then_inc(S("y_spans"), 1)
            pe.matmul(ps[0:SG, 5, :], before[:, :], hy_tdA[:, 1, :], start=True, stop=True).then_inc(S("y_spans"), 1)
            pe.wait_ge(S("y_conv"), after_mamba("y_conv", 2))
            pe.matmul(ps[0:SG, 2, 0:SG], hc[0:NS, 4, :], hc[0:NS, 5, :], start=True, stop=True)
            for k in range(4):
                mm = pe.matmul(ps[0:SG, 2, SG:SG + SH], hc[:, k, :], hy_fcD[:, k, :], start=(k == 0), stop=(k == 3))
            mm.then_inc(S("y_cb"), 1)
            for k in range(4):
                mm = pe.transpose(ps[0:SG, 6, k * P:(k + 1) * P], hc[:, k, :], ident[:, :])
            mm.then_inc(S("y_turned"), 1)
            pe.wait_ge(S("y_mix"), after_mamba("y_mix", 2))
            pe.wait_ge(S("y_rows"), after_mamba("y_rows", 1))
            for h in range(SH):
                mm = pe.matmul(ps[0:SG, 7, h * SG:(h + 1) * SG], hy_mix[:, h * SG:(h + 1) * SG],
                               hx_rows[:, h * SG:(h + 1) * SG], start=True, stop=True)
            mm.then_inc(S("y_y"), 1)
            pe.wait_ge(S("y_normed"), after_mamba("y_normed", 1))
            for k in range(4):
                mm = pe.transpose(ps[:, 1, k * SG:(k + 1) * SG], hy_a[:, k * P:(k + 1) * P], ident[0:SG, 0:SG])
            mm.then_inc(S("y_gT"), 1)
            pe.wait_ge(S("y_gT_w"), after_mamba("y_gT_w", 4))
            for c in range(4):
                for k in range(4):
                    mm = pe.matmul(ps[:, 3, c * SG:(c + 1) * SG], hy_out[:, k, c * P:(c + 1) * P], yg_T[:, k, :],
                                   start=(k == 0), stop=(k == 3))
            mm.then_inc(S("y_o"), 1)
            pe.wait_ge(S("y_block"), after_mamba("y_block", 3))
            for c in range(4):
                mm = pe.matmul(ps[:, 2, c * P:(c + 1) * P], block_o[:, c, :], wo_T[:, c, :], start=True, stop=True)
            mm.then_inc(S("y_q"), 1)
            pe.wait_ge(S("y_slice_w"), after_mamba("y_slice_w", 1))
            for c in range(NG):
                for k in range(4):
                    mm = pe.matmul(ps[:, 4 + c, :], slice_w[:, k, :], sw_T[:, k, c * 512:(c + 1) * 512],
                                   start=(k == 0), stop=(k == 3))
                mm.then_inc(S("s_mixed"), 1)
            for c in range(NG):
                pe.wait_ge(S("s_out_T"), c + 1)
                for i in range(4):
                    mm = pe.transpose(ps[:, c, i * P:(i + 1) * P], s_out_T[:, c, i * P:(i + 1) * P], ident[:, :])
                mm.then_inc(S("s_out_turned"), 1)

        def slice_scalar(act, n):
            with act.Fori(0, NG) as g:
                def copy_out(i):
                    on_tile(act, g, "s_turned", i)
                    act.copy(sw_T[:, :, bass.ds(g * 512 + i * P, P)],
                             ps[:, 3 + i % 2, :].rearrange("p (k n) -> p k n", k=4)).then_inc(S("s_swT"), 1)

                for i in range(4):
                    on_tile(act, g, "s_sub", i)
                    on_tile(act, g, "s_sw", i - 2)
                    act.activation(s_exp[:, i % 2, :], s_logit[:, i % 2, :], ACT.Exp).then_inc(S("s_exped"), 1)
                    if i >= 1:
                        copy_out(i - 1)
                copy_out(3)
            act.wait_ge(S("y_dt_abs"), after_mamba("y_dt_abs", 1))
            act.activation(hy_dt[:, 2, :], hy_dt[:, 1, :], ACT.Exp, scale=-1.0).then_inc(S("y_exp"), 1)
            act.wait_ge(S("y_A_min"), after_mamba("y_A_min", 1))
            act.activation(hy_small[0:SG, 1, :], hy_small[0:SG, 1, :], ACT.Exp).then_inc(S("y_exp"), 1)
            act.wait_ge(S("y_exp"), after_mamba("y_exp", 2))
            act.activation(hy_dt[:, 3, :], hy_dt[:, 2, :], ACT.Ln, bias=1.0).then_inc(S("y_ln"), 1)
            act.wait_ge(S("y_conv_in"), after_mamba("y_conv_in", 1))
            act.wait_ge(S("y_clear"), after_mamba("y_clear", 2))
            act.copy(hc_raw[:, 0:4, 2:66], ps[:, 3, 0:256].rearrange("p (q l) -> p q l", q=4)).then_inc(S("y_raw"), 1)
            act.copy(hc_raw[0:NS, 4:6, 2:66], ps[0:NS, 3, 256:384].rearrange("p (q l) -> p q l", q=2))\
                .then_inc(S("y_raw"), 1)
            act.wait_ge(S("y_tap"), after_mamba("y_tap", 18))
            act.activation(hc_tanh[:, 0:4, :], hc[:, 0:4, :], ACT.Tanh).then_inc(S("y_tanh"), 1)
            act.activation(hc_tanh[0:NS, 4:6, :], hc[0:NS, 4:6, :], ACT.Tanh).then_inc(S("y_tanh"), 1)
            act.wait_ge(S("y_z_in"), after_mamba("y_z_in", 1))
            act.activation(hz, ps[0:SG, 0, :], ACT.Tanh, scale=0.5).then_inc(S("y_z_tanh"), 1)
            for s in range(2):
                act.wait_ge(S("y_spans"), after_mamba("y_spans", s + 1))
                act.activation(hy_dec[:, s, :], ps[0:SG, 4 + s, :], ACT.Exp).then_inc(S("y_dec"), 1)
            act.wait_ge(S("y_turned"), after_mamba("y_turned", 1))
            act.copy(hx_rows, ps[0:SG, 6, :]).then_inc(S("y_rows"), 1)
            act.wait_ge(S("y_gated"), after_mamba("y_gated", 1))
            act.activation(hy_b, hy_a, ACT.Square, scale=0.5, accum_out=hy_ss[:, 0:1]).then_inc(S("y_ss"), 1)
            act.wait_ge(S("y_ss"), after_mamba("y_ss", 1))
            act.activation(hy_ss[:, 0:1], hy_ss[:, 0:1], ACT.Sqrt, scale=1.0 / SI, bias=EPS).then_inc(S("y_rms"), 1)
            act.wait_ge(S("y_q"), after_mamba("y_q", 1))
            act.copy(slice_w.rearrange("p k d -> p (k d)"), ps[:, 2, :]).then_inc(S("y_slice_w"), 1)
            for c in range(NG):
                act.wait_ge(S("s_mixed"), c + 1)
                act.activation(s_out_T[:, c, :], ps[:, 4 + c, :], ACT.Identity, bias=ob_T).then_inc(S("s_out_T"), 1)

        def slice_pool(pool, n):
            with pool.Fori(0, NG) as g:
                pool.wait_ge(S("h_rows"), g * 4 + (16 * n + 4))
                pool.tensor_copy(h_all[:, bass.ds(g * 4, 4), :], h_rows[:, :, :]).then_inc(S("h_kept"), 1)
            hT_ready(pool, n)
            with pool.Fori(0, NG) as g:
                on_tile(pool, g, "s_logits", -1)
                pool.tensor_copy(s_hT, hT[:, bass.ts(g, 512)]).then_inc(S("s_staged"), 1)
                on_tile(pool, g, "s_A", -1)
                pool.wait_ge(S("h_kept"), NG + 1)
                pool.tensor_copy(s_h, h_all[:, bass.ds(g * 4, 4), :]).then_inc(S("s_staged"), 1)
                for i in range(4):
                    b = i % 2
                    on_tile(pool, g, "s_rec", i)
                    on_tile(pool, g, "s_turned", i - 2)
                    on_tile(pool, g, "s_acc", i - 2)
                    pool.tensor_tensor(by_head(s_sw[:, b, :]), by_head(s_exp[:, b, :]), heads8(s_rec[:, b, :], P, SG),
                                       ALU.mult).then_inc(S("s_sw"), 1)
                    on_tile(pool, g, "s_sw", i)
                    on_tile(pool, g, "s_acc", i - 1)
                    pool.tensor_tensor(s_acc, s_acc, s_sw[:, b, :], ALU.add).then_inc(S("s_acc"), 1)

        def slice_vector(dve, n):
            dve.memset(s_acc, 0.0).then_inc(S("s_zeroed"), 1)
            dve.memset(ones[:, :], 1.0).then_inc(S("s_zeroed"), 1)
            dve.memset(block_o[:, :, :], 0.0).then_inc(S("y_block"), 1)
            dve.memset(hc_raw[:, :, :], 0.0).then_inc(S("y_clear"), 1)
            dve.memset(hy_mix, 0.0).then_inc(S("y_clear"), 1)
            dve.wait_ge(S("s_loaded"), S_LOADED)
            dve.wait_ge(S("s_zeroed"), 2)
            dve.tensor_scalar(temp_b, temp_b, 1e-6, None, ALU.max).then_inc(S("s_temp"), 1)
            dve.wait_ge(S("s_temp"), 1)
            dve.reciprocal(temp_b, temp_b).then_inc(S("s_temp"), 1)
            dve.wait_ge(S("s_weights"), 1)
            dve.wait_ge(S("s_temp"), 2)
            dve.tensor_tensor(by_head(logit_w), by_head(ps[:, 0, :]), heads8(temp_b, P, SG), ALU.mult)\
                .then_inc(S("s_logit_w"), 1)
            dve.tensor_tensor(by_head(logit_c), by_head(ps[:, 1, :]), bs_b.unsqueeze(1).to_broadcast([P, SH, SG]),
                              ALU.add).then_inc(S("s_bias_sum"), 1)
            dve.wait_ge(S("s_bias_sum"), 1)
            dve.tensor_tensor(by_head(logit_c), by_head(logit_c), heads8(temp_b, P, SG), ALU.mult)\
                .then_inc(S("s_logit_w"), 1)
            dve.tensor_scalar(hy_cw, hy_cw, 0.5, None, ALU.mult).then_inc(S("y_halved"), 1)
            dve.tensor_scalar(hy_cb, hy_cb, 0.5, None, ALU.mult).then_inc(S("y_halved"), 1)
            dve.tensor_scalar(hy_small[:, 1, :], hy_small[:, 1, :], 88.0, None, ALU.min).then_inc(S("y_A_min"), 1)
            dve.wait_ge(S("s_logit_w"), 2)
            with dve.Fori(0, NG) as g:
                def sums(i):
                    b = i % 2
                    on_tile(dve, g, "s_exped", i)
                    on_tile(dve, g, "s_rec", i - 2)
                    dve.tensor_reduce(s_sum[:, b, :], by_head(s_exp[:, b, :]), AX.X, ALU.add).then_inc(S("s_summed"), 1)
                    on_tile(dve, g, "s_summed", i)
                    on_tile(dve, g, "s_sw", i - 2)
                    dve.reciprocal(s_rec[:, b, :], s_sum[:, b, :]).then_inc(S("s_rec"), 1)

                for i in range(4):
                    b = i % 2
                    on_tile(dve, g, "s_logits", i)
                    on_tile(dve, g, "s_exped", i - 2)
                    dve.tensor_tensor(s_logit[:, b, :], ps[:, b, :], logit_c, ALU.add).then_inc(S("s_add"), 1)
                    on_tile(dve, g, "s_add", i)
                    on_tile(dve, g, "s_sub", i - 2)
                    dve.tensor_reduce(s_max[:, b, :], by_head(s_logit[:, b, :]), AX.X, ALU.max)\
                        .then_inc(S("s_maxed"), 1)
                    on_tile(dve, g, "s_maxed", i)
                    dve.tensor_tensor(by_head(s_logit[:, b, :]), by_head(s_logit[:, b, :]),
                                      heads8(s_max[:, b, :], P, SG), ALU.subtract).then_inc(S("s_sub"), 1)
                    if i >= 1:
                        sums(i - 1)
                sums(3)
            dve.wait_ge(S("s_norm"), 1)
            dve.tensor_scalar(sn_rec, ps[:, 5, :], 1e-5, None, ALU.add).then_inc(S("s_q"), 1)
            dve.wait_ge(S("s_q"), 1)
            dve.reciprocal(sn_rec, sn_rec).then_inc(S("s_q"), 1)
            dve.wait_ge(S("s_q"), 2)
            dve.tensor_tensor(A_T, ps[:, 2, :], sn_rec, ALU.mult).then_inc(S("s_AT"), 1)
            dve.tensor_tensor(q_rows, ps[:, 5, :], sn_rec, ALU.mult).then_inc(S("s_q"), 1)
            dve.wait_ge(S("s_st"), 1)
            dve.wait_ge(S("s_q"), 3)
            for k in range(4):
                for s in range(2):
                    r = slice(s * 64, s * 64 + 64)
                    c0 = k * P + s * SG
                    dve.scalar_tensor_tensor(st_T[r, k, :], q_rows[r, c0:c0 + SG], bfx_T[r, k:k + 1],
                                             ps[r, 6, c0:c0 + SG], ALU.mult, ALU.add).then_inc(S("s_stT"), 1)
            dve.wait_ge(S("y_dt_in"), after_mamba("y_dt_in", 1))
            two = lambda ap: ap.rearrange("p (s h) -> p s h", s=2)
            dve.tensor_tensor(two(hy_dt[:, 0, :]), two(ps[0:SG, 1, 0:2 * SH]),
                              hy_small[0:SG, 0, :].unsqueeze(1).to_broadcast([SG, 2, SH]), ALU.add)\
                .then_inc(S("y_dt"), 1)
            dve.wait_ge(S("y_dt"), after_mamba("y_dt", 1))
            dve.scalar_tensor_tensor(hy_dt[:, 1, :], hy_dt[:, 0, :], -1.0, hy_dt[:, 0, :], ALU.mult, ALU.max)\
                .then_inc(S("y_dt_abs"), 1)
            dve.wait_ge(S("y_ln"), after_mamba("y_ln", 1))
            dve.scalar_tensor_tensor(hy_dt[:, 4, :], hy_dt[:, 0, :], 0.0, hy_dt[:, 3, :], ALU.max, ALU.add)\
                .then_inc(S("y_dt"), 1)
            dve.wait_ge(S("y_dt"), after_mamba("y_dt", 2))
            dve.wait_ge(S("y_exp"), after_mamba("y_exp", 2))
            dve.scalar_tensor_tensor(two(hy_dt[:, 5, :]), two(hy_dt[:, 4, :]), -1.0,
                                     hy_small[0:SG, 1, :].unsqueeze(1).to_broadcast([SG, 2, SH]),
                                     ALU.mult, ALU.mult).then_inc(S("y_dt"), 1)
            dve.wait_ge(S("y_dt"), after_mamba("y_dt", 3))
            dve.tensor_scalar(hy_dt[:, 5, :], hy_dt[:, 5, :], -1.0e4, None, ALU.max).then_inc(S("y_dt"), 1)
            dve.wait_ge(S("y_dt"), after_mamba("y_dt", 4))
            for s, m in enumerate((tri[0:SG, 0:SG], low[:, :])):
                dve.tensor_tensor(by_head(hy_tdA[:, s, :]), m.unsqueeze(1).to_broadcast([SG, SH, SG]),
                                  heads8(hy_dt[:, 5, s * SH:(s + 1) * SH], SG, SG), ALU.mult).then_inc(S("y_tdA"), 1)
            dve.wait_ge(S("y_clear"), after_mamba("y_clear", 2))
            dve.wait_ge(S("y_halved"), after_mamba("y_halved", 2))
            for k in (2, 0, 1):
                at = {2: 0, 0: 6, 1: 12}[k]
                for q, w in HPARTS:
                    if k == 2:
                        dve.wait_ge(S("y_raw"), after_mamba("y_raw", 1 if q < 4 else 2))
                        dve.tensor_scalar(hc[0:w, q, :], hc_raw[0:w, q, 2:66], hy_cw[0:w, q, 2:3], hy_cb[0:w, q:q + 1],
                                          ALU.mult, ALU.add).then_inc(S("y_tap"), 1)
                    else:
                        dve.wait_ge(S("y_tap"), after_mamba("y_tap", at + q - 5))
                        dve.scalar_tensor_tensor(hc[0:w, q, :], hc_raw[0:w, q, k:k + 64], hy_cw[0:w, q, k:k + 1],
                                                 hc[0:w, q, :], ALU.mult, ALU.add).then_inc(S("y_tap"), 1)
            dve.wait_ge(S("y_tanh"), after_mamba("y_tanh", 1))
            dve.scalar_tensor_tensor(hc[:, 0:4, :], hc_tanh[:, 0:4, :], 1.0, hc[:, 0:4, :], ALU.add, ALU.mult)\
                .then_inc(S("y_conv"), 1)
            dve.wait_ge(S("y_tanh"), after_mamba("y_tanh", 2))
            dve.scalar_tensor_tensor(hc[0:NS, 4:6, :], hc_tanh[0:NS, 4:6, :], 1.0, hc[0:NS, 4:6, :],
                                     ALU.add, ALU.mult).then_inc(S("y_conv"), 1)
            dve.wait_ge(S("y_z_tanh"), after_mamba("y_z_tanh", 1))
            dve.scalar_tensor_tensor(hz, hz, 1.0, ps[0:SG, 0, :], ALU.add, ALU.mult).then_inc(S("y_z"), 1)
            dve.wait_ge(S("y_cb"), after_mamba("y_cb", 1))
            for s, m in enumerate((tri[0:SG, 0:SG], low[:, :])):
                dve.tensor_tensor(hy_cbm[:, s, :], ps[0:SG, 2, 0:SG], m, ALU.mult).then_inc(S("y_cbm"), 1)
            dve.tensor_tensor(hy_fD, ps[0:SG, 2, SG:SG + SH], hy_small[0:SG, 2, :], ALU.add).then_inc(S("y_fD"), 1)
            dve.wait_ge(S("y_cbm"), after_mamba("y_cbm", 2))
            for s in range(2):
                d3 = by_head(hy_dec[:, s, :])
                dve.wait_ge(S("y_dec"), after_mamba("y_dec", s + 1))
                dve.tensor_tensor(d3, d3, hy_cbm[:, s, :].unsqueeze(1).to_broadcast([SG, SH, SG]), ALU.mult)\
                    .then_inc(S("y_dec_cb"), 1)
            m3 = by_head(hy_mix)
            dve.wait_ge(S("y_dec_cb"), after_mamba("y_dec_cb", 1))
            dve.tensor_tensor(m3[:, :, 1:SG], by_head(hy_dec[:, 0, :])[:, :, 0:SG - 1],
                              heads8(hy_dt[:, 4, 0:SH], SG, SG - 1), ALU.mult).then_inc(S("y_mix"), 1)
            dve.wait_ge(S("y_dec_cb"), after_mamba("y_dec_cb", 2))
            d1 = by_head(hy_dec[:, 1, :])
            dve.tensor_tensor(d1, d1, heads8(hy_dt[:, 4, SH:2 * SH], SG, SG), ALU.mult).then_inc(S("y_dec_cb"), 1)
            dve.wait_ge(S("y_dec_cb"), after_mamba("y_dec_cb", 3))
            dve.wait_ge(S("y_mix"), after_mamba("y_mix", 1))
            dve.tensor_tensor(m3[:, :, 0:SG - 1], m3[:, :, 0:SG - 1], d1[:, :, 1:SG], ALU.add)\
                .then_inc(S("y_mix"), 1)
            dve.wait_ge(S("y_rows"), after_mamba("y_rows", 1))
            dve.wait_ge(S("y_fD"), after_mamba("y_fD", 1))
            dve.tensor_tensor(by_head(hy_b), by_head(hx_rows), heads8(hy_fD, SG, SG), ALU.mult).then_inc(S("y_t"), 1)
            dve.wait_ge(S("y_y"), after_mamba("y_y", 1))
            dve.wait_ge(S("y_t"), after_mamba("y_t", 1))
            dve.tensor_tensor(hy_b, hy_b, ps[0:SG, 7, :], ALU.add).then_inc(S("y_t"), 1)
            dve.wait_ge(S("y_t"), after_mamba("y_t", 2))
            dve.wait_ge(S("y_z"), after_mamba("y_z", 1))
            dve.tensor_tensor(hy_a, hy_b, hz, ALU.mult).then_inc(S("y_gated"), 1)
            dve.wait_ge(S("y_rms"), after_mamba("y_rms", 1))
            dve.reciprocal(hy_ss[:, 1:2], hy_ss[:, 0:1]).then_inc(S("y_t"), 1)
            dve.wait_ge(S("y_t"), after_mamba("y_t", 3))
            dve.wait_ge(S("y_gated"), after_mamba("y_gated", 1))
            dve.tensor_scalar(hy_a, hy_a, hy_ss[:, 1:2], 0.5, ALU.mult, ALU.mult).then_inc(S("y_normed"), 1)
            dve.wait_ge(S("y_gT"), after_mamba("y_gT", 1))
            for k in range(4):
                dve.tensor_scalar(yg_T[:, k, :], ps[:, 1, k * SG:(k + 1) * SG], hy_nw[:, k:k + 1], None, ALU.mult)\
                    .then_inc(S("y_gT_w"), 1)
            dve.wait_ge(S("y_o"), after_mamba("y_o", 1))
            dve.wait_ge(S("y_block"), after_mamba("y_block", 1))
            for s in range(2):
                r = slice(s * 64, s * 64 + 64)
                dve.tensor_copy(block_o[r, :, s * SG:(s + 1) * SG],
                                ps[r, 3, 0:256].rearrange("p (k g) -> p k g", k=4)).then_inc(S("y_block"), 1)
            for c in range(NG):
                dve.wait_ge(S("s_out_turned"), c + 1)
                dve.tensor_tensor(x[:, 4 * c:4 * c + 4, :], x[:, 4 * c:4 * c + 4, :],
                                  ps[:, c, :].rearrange("p (i d) -> p i d", d=D), ALU.add)\
                    .then_inc(S("x_updates"), 1)

        def slice_sync(sp, before_x):
            sp.wait_ge(S("x_updates"), before_x)
            for dst, name in ((wx_h, "L3_wx"), (ws_T, "L3_wsT"), (bx_T, "L3_bxT"), (wfx_T, "L3_wfxT"),
                              (bfx_T, "L3_bfxT"), (hy_cw, "L3_cw"), (hy_cb, "L3_cb"), (hy_fcD, "L3_fcDT"),
                              (hy_nw, "L3_nwT"), (before[:, :], "before"), (low[:, :], "low"), (ob_T, "L3_obT"),
                              (wo_T, "L3_woT"), (hy_out, "L3_hyoutT"), (hy_in, "L3_hyinT")):
                sp.dma_start(dst, t[name]).then_inc(S("s_loaded"), 16)
            for dst, name in ((bs_b, "L3_ffn_b_slice"), (temp_b, "L3_temp"), (hy_small[:, 0, :], "L3_ffn_hy_dt_bias"),
                              (hy_small[:, 1, :], "L3_ffn_hy_A_log"), (hy_small[:, 2, :], "L3_ffn_hy_D")):
                sp.dma_start(dst, t[name].partition_broadcast(P)).then_inc(S("s_loaded"), 16)

        NORMS = {"gnn0": 0, "moe0": 1, "gnn1": 2, "mamba": 3, "sage": 4, "moe2": 5, "gnn3": 6, "slice": 7}
        UPDATES = {"gnn0": 3, "moe0": 4, "gnn1": 3, "mamba": NT, "sage": NT, "moe2": 4, "gnn3": 6, "slice": 4}
        need = {}
        total = 16
        for s in STAGES:
            need[s] = total
            if s == "gnn3":
                pass_end["L3"] = total + 3
            total += UPDATES[s]
        x_total = total

        CREDITS = {"h_turned": 4, "hT": 1, "weights": 2, "weights_used": 2, "act_h": RING, "mul_h": RING,
                   "down": RING}
        if "mamba" in STAGES:
            CREDITS |= {name: 2 for name in CHUNKS} | GROUPS
        if "sage" in STAGES:
            CREDITS |= {"g_x": 2}
        if "slice" in STAGES:
            CREDITS |= {name: 2 for name in TILES} | {"h_kept": 1}

        @block.gpsimd
        def _(pool):
            for name, n in CREDITS.items():
                pool.sem_inc(S(name), n)
            for s in STAGES:
                if s == "mamba":
                    add_to_rows(pool, NORMS[s], b_lin, "m_x_bias", "bias_loaded", 1)
                    mamba_pool(pool)
                if s == "slice":
                    slice_pool(pool, NORMS[s])
                if s == "sage":
                    add_to_rows(pool, NORMS[s], sage_b, "g_x_bias", "sage_loaded", 2)

        @block.sync
        def _(sp):
            sp.dma_start(x[:, :, :], t["x"].rearrange("(i p) d -> p i d", p=P)).then_inc(S("x_updates"), 16)
            sp.dma_start(ident[:, :], t["ident"]).then_inc(S("gat_loaded"), 16)
            for l, L in enumerate(("L0", "L1", "L3")):
                sp.dma_start(gat_wT[:, l, :], t[f"{L}_gnn_WT"]).then_inc(S("gat_loaded"), 16)
                sp.dma_start(gat_a[:, l, :], t[f"{L}_gnn_a"]).then_inc(S("gat_loaded"), 16)
            sp.dma_start(value_w[:, 0, 0:D], t["L0_gnn_W"]).then_inc(S("gat_loaded"), 16)
            sp.dma_start(value_w[:, 1, 0:D], t["L1_gnn_W"]).then_inc(S("gat_loaded"), 16)
            sp.dma_start(value_w[:, 2:4, 0:D], t["L3_gnn_wtrans"].rearrange("(s d) o -> d s o", d=D))\
                .then_inc(S("gat_loaded"), 16)
            if "gnn0" in STAGES:
                adj_rows = t["adjT"].rearrange("(j p) n -> j p n", p=P)
                for b in range(2):
                    sp.dma_start(adj_in[:, b, :], adj_rows[b]).then_inc(S(f"adj_landed{b}"), 16)
            sp.dma_start(first[:, :], t["first"].partition_broadcast(P)).then_inc(S("moe_loaded"), 16)
            for m, L in enumerate(("L0", "L2")):
                sp.dma_start(gate_w[:, m, :], t[f"{L}_ffn_Wg"]).then_inc(S("moe_loaded"), 16)
                sp.dma_start(gate_b[:, m, :], t[f"{L}_ffn_bg"].partition_broadcast(P)).then_inc(S("moe_loaded"), 16)
                sp.dma_start(b1_T[L][:, :], t[f"{L}_ffn_b1"]).then_inc(S("moe_loaded"), 16)
                sp.dma_start(b2[:, m, :], t[f"{L}_ffn_b2"]).then_inc(S("moe_loaded"), 16)
            if "gnn0" in STAGES:
                with sp.Fori(1, NT // 2) as jj:
                    for b in range(2):
                        sp.wait_ge(S("adjT"), jj * 2 + (b - 1))
                        sp.dma_start(adj_in[:, b, :], adj_rows[bass.ds(jj * 2 + b, 1)].rearrange("j p n -> p (j n)"))\
                            .then_inc(S(f"adj_landed{b}"), 16)
            if "mamba" in STAGES:
                for dst, name in ((tri, "tri"), (after, "after"), (win_x, "L1_win_x"), (win_zd, "L1_win_zd"),
                                  (conv_w, "L1_conv_w"), (conv_b, "L1_conv_b"), (wout_T, "L1_wout_T"),
                                  (w_lin, "L1_W_lin"), (norm_w, "L1_norm_w")):
                    sp.dma_start(dst[tuple([slice(None)] * len(dst.shape))], t[name]).then_inc(S("mamba_loaded"), 16)
                sp.dma_start(small_in[:, :, :], t["L1_small"].partition_broadcast(P)).then_inc(S("mamba_loaded"), 16)
                sp.dma_start(b_lin[:, :], t["L1_b_lin"].partition_broadcast(P)).then_inc(S("bias_loaded"), 16)
            if "sage" in STAGES:
                sp.dma_start(sage_w[:, :], t["L2_gnn_w"]).then_inc(S("sage_loaded"), 16)
                sp.dma_start(sage_b[:, :], t["L2_gnn_bias"].partition_broadcast(P)).then_inc(S("sage_loaded"), 16)
            for s in STAGES:
                if s == "moe0":
                    moe_sync(sp, "L0", 1)
                if s == "moe2":
                    moe_sync(sp, "L2", 5)
                if s == "slice":
                    slice_sync(sp, need[s])
            sp.wait_ge(S("x_updates"), x_total)
            sp.wait_ge(S("moe_loaded"), 16 * 9)
            sp.dma_start(outs[0].rearrange("(i p) d -> p i d", p=P), x[:, :, :]).then_inc(S("stored"), 16)
            sp.wait_ge(S("stored"), 16)

        @block.vector
        def _(dve):
            gat_setup_vector(dve)
            for s in STAGES:
                norm_vector(dve, NORMS[s], need[s])
                if s[:3] == "gnn":
                    gat_vector(dve, "L" + s[3], NORMS[s])
                if s[:3] == "moe":
                    moe_vector(dve, "L" + s[3], NORMS[s])
                if s == "mamba":
                    mamba_vector(dve, NORMS[s])
                if s == "slice":
                    slice_vector(dve, NORMS[s])
                if s == "sage":
                    sage_vector(dve, NORMS[s])

        @block.scalar
        def _(act):
            for s in STAGES:
                norm_scalar(act, NORMS[s])
                if s[:3] == "gnn":
                    gat_scalar(act, "L" + s[3], NORMS[s])
                if s[:3] == "moe":
                    moe_scalar(act, "L" + s[3], NORMS[s])
                if s == "mamba":
                    mamba_scalar(act, NORMS[s])
                if s == "slice":
                    slice_scalar(act, NORMS[s])

        @block.tensor
        def _(pe):
            gat_setup_tensor(pe)
            for s in STAGES:
                norm_tensor(pe, NORMS[s])
                if s[:3] == "gnn":
                    gat_tensor(pe, "L" + s[3], NORMS[s])
                if s[:3] == "moe":
                    moe_tensor(pe, "L" + s[3], NORMS[s])
                if s == "mamba":
                    mamba_tensor(pe, NORMS[s])
                if s == "slice":
                    slice_tensor(pe, NORMS[s])
                if s == "sage":
                    sage_tensor(pe, NORMS[s])


def kernel(**inputs):
    import numpy as _np
    import concourse.bacc as _bacc
    from concourse import mybir as _mybir
    from concourse.bass_utils import run_bass_kernel_spmd as _run

    a = {k: _np.asarray(v) for k, v in inputs.items()}
    c = _np.ascontiguousarray
    arrays = {
        "x": a["x"], "adjT": c(a["adj"].T),
        "ident": _np.eye(P, dtype=_np.float32), "first": _np.arange(E, 0, -1).astype(_np.float32),
    }
    for L in ("L0", "L1", "L3"):
        arrays[f"{L}_gnn_WT"] = c(a[f"{L}_gnn_W"].T)
        arrays[f"{L}_gnn_a"] = c(a[f"{L}_gnn_a"].reshape(2, D).T)
    arrays["L0_gnn_W"], arrays["L1_gnn_W"] = a["L0_gnn_W"], a["L1_gnn_W"]
    arrays["L3_gnn_wtrans"] = a["L3_gnn_wtrans"]
    arrays["L0_ffn_Wg"], arrays["L2_ffn_Wg"] = a["L0_ffn_Wg"], c(a["L2_ffn_Wg"].T)
    arrays["L0_ffn_W1"], arrays["L2_ffn_W1"] = a["L0_ffn_W1"], c(a["L2_ffn_W1"].transpose(0, 2, 1))
    arrays["L0_ffn_W2"], arrays["L2_ffn_W2"] = a["L0_ffn_W2"], c(a["L2_ffn_W2"].transpose(0, 2, 1))
    for L in ("L0", "L2"):
        arrays[f"{L}_ffn_bg"], arrays[f"{L}_ffn_b2"] = a[f"{L}_ffn_bg"], a[f"{L}_ffn_b2"]
        arrays[f"{L}_ffn_b1"] = c(a[f"{L}_ffn_b1"].reshape(E * HC[L], P).T)
    tri = _np.triu(_np.ones((P, P), _np.float32))
    arrays["tri"], arrays["after"] = tri, c(1 - tri.T) * 0 + _np.tril(_np.ones((P, P), _np.float32), -1)
    win = a["L1_ffn_W_in"]
    arrays["L1_win_x"] = c(win[:, DI:DI + 384])
    arrays["L1_win_zd"] = c(_np.concatenate([win[:, :DI], win[:, DI + 384:]], axis=1))
    cw, cb = _np.zeros((P, 4, 4), _np.float32), _np.zeros((P, 4), _np.float32)
    for q, c0, w in ((0, 0, P), (1, P, P), (2, 2 * P, NS), (3, 2 * P + NS, NS)):
        cw[:w, q], cb[:w, q] = a["L1_ffn_conv_w"][c0:c0 + w], a["L1_ffn_conv_b"][c0:c0 + w]
    arrays["L1_conv_w"], arrays["L1_conv_b"] = cw, cb
    arrays["L1_wout_T"] = c(a["L1_ffn_W_out"].T.reshape(P, 2, P))
    arrays["L1_W_lin"], arrays["L1_b_lin"] = a["L1_ffn_W_lin"], a["L1_ffn_b_lin"]
    arrays["L1_norm_w"] = c(a["L1_ffn_norm_w"].reshape(2, P).T)
    arrays["L1_small"] = _np.stack([a["L1_ffn_dt_bias"], a["L1_ffn_A_log"], a["L1_ffn_D"]])
    arrays["L2_gnn_w"] = c(a["L2_gnn_weight"].reshape(2, D, D).transpose(1, 0, 2).reshape(D, 2 * D))
    arrays["L2_gnn_bias"] = a["L2_gnn_bias"]
    arrays["before"] = c(_np.triu(_np.ones((SG, SG), _np.float32), 1))
    arrays["low"] = c(_np.tril(_np.ones((SG, SG), _np.float32)))
    arrays["L3_wx"] = c(a["L3_ffn_W_x"].reshape(SH, NS, D).transpose(1, 0, 2))
    arrays["L3_wsT"] = c(a["L3_ffn_W_slice"].T)
    arrays["L3_bxT"] = c(a["L3_ffn_b_x"].reshape(SH, NS).T)
    arrays["L3_wfxT"] = c(a["L3_ffn_W_fx"].T)
    arrays["L3_bfxT"] = c(a["L3_ffn_b_fx"].reshape(4, P).T)
    hw, hb = _np.zeros((P, 6, 3), _np.float32), _np.zeros((P, 6), _np.float32)
    for q in range(6):
        c0, w = (q * P, P) if q < 4 else (SI + (q - 4) * NS, NS)
        hw[:w, q], hb[:w, q] = a["L3_ffn_hy_conv_w"][c0:c0 + w], a["L3_ffn_hy_conv_b"][c0:c0 + w]
    arrays["L3_cw"], arrays["L3_cb"] = hw, hb

    def chunks(m):
        return c(m.reshape(4, P, -1).transpose(1, 0, 2))

    arrays["L3_fcDT"] = chunks(a["L3_ffn_hy_fcD_w"].T)
    arrays["L3_nwT"] = c(a["L3_ffn_hy_norm_w"].reshape(4, P).T)
    arrays["L3_hyinT"] = chunks(a["L3_ffn_hy_in_w"].T)
    arrays["L3_hyoutT"] = chunks(a["L3_ffn_hy_out_w"].T)
    arrays["L3_woT"] = chunks(a["L3_ffn_out_w"].T)
    arrays["L3_obT"] = c(a["L3_ffn_out_b"].reshape(P, 1))
    arrays["L3_temp"] = a["L3_ffn_temperature"].reshape(SH)
    for name in ("b_slice", "hy_dt_bias", "hy_A_log", "hy_D"):
        arrays[f"L3_ffn_{name}"] = a[f"L3_ffn_{name}"]
    nc = _bacc.Bacc("TRN2", target_bir_lowering=False, num_devices=1)
    t, ins = {}, {}
    for name, arr in arrays.items():
        ins[f"in_{name}"] = arr
        t[name] = nc.dram_tensor(f"in_{name}", arr.shape, _mybir.dt.from_np(arr.dtype), kind="ExternalInput").ap()
    out_name = OUT
    outs = [nc.dram_tensor(out_name, (N, D), F32, kind="ExternalOutput").ap()]
    program(nc, t, outs)
    r = _run(nc, [ins], core_ids=[0])
    return r.results[0][out_name]


OUT = "out"
```

```python
from contextlib import ExitStack

import numpy as np
import concourse.bass as bass
from concourse import mybir

F32 = mybir.dt.float32
BF16 = mybir.dt.bfloat16
F32R = mybir.dt.float32r
I32 = mybir.dt.int32
ALU = mybir.AluOpType
ACT = mybir.ActivationFunctionType
AX = mybir.AxisListType

P = 128
N = 2048
D = 128
NT = N // P
NG = N // 512
EPS = 1e-5
SLOPE = 0.2
RISE = 1.0 - SLOPE
CLAMP = 75.0 / RISE
E = 8
HC = {"L0": 2, "L2": 4}
VC = D + 1
TPB = 3
NBK = -(-NT // TPB)
RING = 4
LAG = 4
DI = 256
NH = 4
HD = DI // NH
NS = 64
SH = 8
SG = 64
SI = 512
HYP = 2 * SI + 2 * NS + 2 * SH
STAGES = ["gnn0", "moe0", "gnn1", "mamba", "sage", "moe2", "gnn3", "slice"]


def program(nc, t, outs):
    with ExitStack() as ctx:
        def sb(name, shape, dt=F32):
            return ctx.enter_context(nc.sbuf_tensor(name, shape, dt))

        sems = {}
        reused = {}

        def S(name):
            name = reused.get(name, (name,))[0]
            if name not in sems:
                sems[name] = ctx.enter_context(nc.semaphore(name))
            return sems[name]

        x = sb("x", [P, NT, D])
        hT = sb("hT", [P, N])
        adjT = sb("adjT", [P, NT, N], BF16)
        ps = ctx.enter_context(nc.psum_tensor("ps", [P, 8, 512], F32))

        ident = sb("ident", [P, P])
        zeros = sb("zeros", [P, TPB * VC], BF16)
        h_rows = sb("h_rows", [P, 4, D])
        stats = sb("stats", [P, 4, 6])
        mean_var = sb("mean_var", [P, 4, 2])
        std = sb("std", [P, 4])
        rstd = sb("rstd", [P, 4])

        gat_wT = sb("gat_wT", [P, 3, D])
        gat_a = sb("gat_a", [P, 3, 2])
        value_w = sb("value_w", [P, 4, VC])
        score_w = sb("score_w", [P, 3, 2, P])
        s2_bound = sb("s2_bound", [P, 2])
        s2_rel = sb("s2_rel", [P, 2, NT])
        K = sb("K", [P, 2, NT])
        F = sb("F", [P, 2, NT])
        rowrec = sb("rowrec", [P, NT])

        with ExitStack() as beneath:
            def under(name, shape, dt=F32R):
                return beneath.enter_context(nc.sbuf_tensor(name, shape, dt))

            under("big_lower", [P, 4 * N], F32)
            h_parts = under("h_parts", [P, 2, RING, 512])
            hT_parts = under("hT_parts", [P, 2, N])
            w_parts = under("w_parts", [P, 2, 2, 2, 512])
        big = sb("big", [P, 8 * N])
        R = big[:, 0:2 * N].rearrange("p (s n) -> p s n", s=2)
        T = big[:, 2 * N:4 * N].rearrange("p (s n) -> p s n", s=2)
        PR = big[:, 4 * N:6 * N].rearrange("p (s n) -> p s n", s=2)
        adj_in = big[:, 6 * N:8 * N].bitcast(I32).rearrange("p (s n) -> p s n", s=2)
        G = sb("G", [P, 2, NT, VC])
        rows_a = T[:, 0, :].rearrange("p (i d) -> p i d", d=D)
        rows_b = T[:, 1, :].rearrange("p (i d) -> p i d", d=D)
        rows_c = R[:, 0, :].rearrange("p (i d) -> p i d", d=D)

        comb_b = big[:, 0:2 * N].rearrange("p (s n) -> p s n", s=2)
        act_h = big[:, 2 * N:3 * N].rearrange("p (r n) -> p r n", r=RING)
        out_T = big[:, 3 * N:4 * N].rearrange("p (c n) -> p c n", c=NG)
        comb8 = big[0:E, 3 * N:4 * N]
        expert_in = sb("expert_in", [P, 2048])
        w1_e = expert_in[:, 0:1024].rearrange("p (s h) -> p s h", s=2)
        w2_e = expert_in[:, 1024:2048].rearrange("p (s k d) -> p s k d", s=2, d=P)
        gate_w = sb("gate_w", [P, 2, E])
        gate_b = sb("gate_b", [P, 2, E])
        first = sb("first", [P, E])
        b1_T = {"L0": sb("b1_T0", [P, E * 2]), "L2": sb("b1_T2", [P, E * 4])}
        b2 = sb("b2", [E, 2, D])
        top = sb("top", [P, 8, NT, E])
        topm = sb("topm", [P, 8, NT])
        comb = sb("comb", [P, E, NT])
        comb_T = sb("comb_T", [P, P])
        comb_dram = {L: nc.dram_tensor(f"comb_{L}", [E, N], F32, kind="Internal").ap() for L in ("L0", "L2")}

        o = [0]

        def part(n, rows=P):
            o[0] += n
            assert o[0] <= 8 * N
            return big[0:rows, o[0] - n:o[0]]

        conv_raw = part(4 * 516).rearrange("p (q n) -> p q n", q=4)
        conv = part(4 * 512).rearrange("p (q n) -> p q n", q=4)
        z_gate = part(NT * DI).rearrange("p (i d) -> p i d", d=DI)
        y_rows = part(NT * D).rearrange("p (i d) -> p i d", d=D)
        xb_rows = part(4 * 320).rearrange("p (i d) -> p i d", d=320)
        cb_masked = part(4 * P).rearrange("p (i l) -> p i l", i=4)
        mixm = part(2 * 512).rearrange("p (b n) -> p b n", b=2)
        x_dt = part(2 * DI).rearrange("p (b n) -> p b n", b=2)
        x_decayed = part(2 * DI).rearrange("p (b n) -> p b n", b=2)
        x_skip = part(2 * DI).rearrange("p (b n) -> p b n", b=2)
        y_gated = part(2 * DI).rearrange("p (b n) -> p b n", b=2)
        y_T = part(2 * DI).rearrange("p (b n) -> p b n", b=2)
        state = part(2 * DI, 64).rearrange("p (b n) -> p b n", b=2)
        Gf = G[:, :, :, :].rearrange("p s i c -> p (s i c)")
        conv_tanh = Gf[:, 0:2048].rearrange("p (q n) -> p q n", q=4)
        tri_dA = Gf[:, 2048:3072].rearrange("p (b n) -> p b n", b=2)
        decay = Gf[:, 3072:4096].rearrange("p (b n) -> p b n", b=2)
        conv_out = expert_in[:, :].rearrange("p (q n) -> p q n", q=4)
        y_a = sb("y_a", [P, DI])
        y_b = sb("y_b", [P, DI])
        z_tanh = sb("z_tanh", [P, 2, DI])
        y_square = sb("y_square", [P, DI])
        tri = sb("tri", [P, P])
        after = sb("after", [P, P])
        ones = sb("ones", [P, P])
        win_x = sb("win_x", [P, 384])
        win_zd = sb("win_zd", [P, DI + NH])
        conv_w = sb("conv_w", [P, 4, 4])
        conv_b = sb("conv_b", [P, 4])
        small_in = sb("small_in", [P, 3, NH])
        wout_T = sb("wout_T", [P, 2, P])
        w_lin = sb("w_lin", [P, P])
        norm_w = sb("norm_w", [P, 2])
        b_lin = sb("b_lin", [P, D])
        w_proj = sb("w_proj", [P, 2, P])
        dts = sb("dts", [P, 6, NT * NH])
        exp_A = sb("exp_A", [P, NH])
        carry = sb("carry", [P, 2, NT * NH])
        sumsq = sb("sumsq", [P, NT])

        sage_w = sb("sage_w", [P, 2 * D])
        sage_b = sb("sage_b", [P, D])
        sage_y = big[:, 0:NT * 200].bitcast(BF16)[:, 0:NT * 386].rearrange("p (i c) -> p i c", c=386)
        sage_r = big[:, NT * 200:NT * 200 + N].rearrange("p (i d) -> p i d", d=D)
        sage_sum = sb("sage_sum", [P, 2, D])
        sage_rec = sb("sage_rec", [P, 2])

        adj_words = adjT[:, :, :].rearrange("p i n -> p (i n)").bitcast(F32)
        a_o = [0]

        def in_adj(n, rows=P):
            a_o[0] += n
            assert a_o[0] <= NT * N // 2
            return adj_words[0:rows, a_o[0] - n:a_o[0]]

        wx_h = in_adj(SH * D, NS).rearrange("p (h d) -> p h d", h=SH)
        ws_T = in_adj(SG, NS)
        bx_T = in_adj(SH, NS)
        bs_b = in_adj(SG)
        temp_b = in_adj(SH)
        wfx_T = in_adj(SI)
        bfx_T = in_adj(4)
        hy_in = in_adj(4 * HYP).rearrange("p (k n) -> p k n", k=4)
        hy_cw = in_adj(6 * 3).rearrange("p (q k) -> p q k", q=6)
        hy_cb = in_adj(6)
        hy_small = in_adj(4 * SH).rearrange("p (q h) -> p q h", q=4)
        hy_fcD = in_adj(4 * SH).rearrange("p (k h) -> p k h", k=4)
        hy_nw = in_adj(4)
        hy_out = in_adj(4 * SI).rearrange("p (k n) -> p k n", k=4)
        wo_T = in_adj(4 * D).rearrange("p (k d) -> p k d", k=4)
        ob_T = in_adj(1)
        logit_w = in_adj(SI)
        logit_c = in_adj(SI)
        A_T = in_adj(SI)
        q_rows = in_adj(SI)
        sn_rec = in_adj(SI)
        st_T = in_adj(4 * SG).rearrange("p (k g) -> p k g", k=4)
        block_o = in_adj(4 * P).rearrange("p (k g) -> p k g", k=4)
        slice_w = in_adj(4 * D).rearrange("p (k d) -> p k d", k=4)
        hc_raw = in_adj(6 * 66).rearrange("p (q l) -> p q l", q=6)
        hc = in_adj(6 * SG).rearrange("p (q l) -> p q l", q=6)
        hc_tanh = in_adj(6 * SG).rearrange("p (q l) -> p q l", q=6)
        yg_T = in_adj(4 * SG).rearrange("p (k g) -> p k g", k=4)
        hx_rows = in_adj(SI, SG)
        hy_a = in_adj(SI, SG)
        hy_cbm = in_adj(2 * SG, SG).rearrange("p (s l) -> p s l", s=2)
        hy_dt = in_adj(6 * 2 * SH, SG).rearrange("p (q h) -> p q h", q=6)
        hy_fD = in_adj(SH, SG)
        hy_ss = in_adj(2, SG)
        sw_T = big[:, 0:4 * N].rearrange("p (k n) -> p k n", k=4)
        s_out_T = big[:, 4 * N:5 * N].rearrange("p (c n) -> p c n", c=NG)
        o5 = 5 * N
        s_logit = big[:, o5:o5 + 1024].rearrange("p (b n) -> p b n", b=2)
        s_exp = big[:, o5 + 1024:o5 + 2048].rearrange("p (b n) -> p b n", b=2)
        s_sw = big[:, o5 + 2048:o5 + 3072].rearrange("p (b n) -> p b n", b=2)
        s_acc = big[:, o5 + 3072:o5 + 3584]
        s_hT = big[:, o5 + 3584:o5 + 4096]
        s_h = big[:, o5 + 4096:o5 + 4608].rearrange("p (i d) -> p i d", d=D)
        h_all = Gf[:, 0:N].rearrange("p (i d) -> p i d", d=D)
        hz, hy_b, hy_mix = (Gf[0:SG, N + q * SI:N + (q + 1) * SI] for q in range(3))
        hy_tdA, hy_dec = s_logit[0:SG], s_exp[0:SG]
        s_max = sb("s_max", [P, 2, SH])
        s_sum = sb("s_sum", [P, 2, SH])
        s_rec = sb("s_rec", [P, 2, SH])
        before = sb("before", [SG, SG])
        low = sb("low", [SG, SG])

        x_count = [16]
        ndbg = [0]

        def bank_rows(b0, b1, c0, c1):
            return ps[:, b0:b1, 0:TPB * VC].rearrange("p b (k c) -> p b k c", c=VC)[:, :, :, c0:c1]

        def tiles3(ap, b0, b1):
            return ap[:, TPB * b0:TPB * b1, :].rearrange("p (b k) d -> p b k d", k=TPB)

        FULL = NT // TPB

        block = ctx.enter_context(nc.Block())
        plan = []

        def norm_vector(dve, n, need):
            dve.wait_ge(S("x_updates"), need)
            with dve.Fori(0, NG) as g:
                k = g * 4 + (16 * n)
                for i in range(4):
                    dve.bn_stats(stats[:, i, :], x[:, bass.ds(g * 4 + i, 1), :]).then_inc(S("stats"), 1)
                dve.wait_ge(S("stats"), k + 4)
                dve.sem_inc(S("stats_seen"), 1)
                for i in range(4):
                    dve.bn_aggr(mean_var[:, i, :], stats[:, i, :]).then_inc(S("mean_var"), 1)
                dve.wait_ge(S("std"), g + (4 * n + 1))
                dve.reciprocal(rstd[:, :], std[:, :]).then_inc(S("rstd"), 1)
                dve.wait_ge(S("rstd"), g + (4 * n + 1))
                dve.wait_ge(S("h_turned"), k + 1)
                if n == 7:
                    dve.wait_ge(S("h_kept"), g + 1)
                for i in range(4):
                    dve.tensor_scalar(h_rows[:, i, :], x[:, bass.ds(g * 4 + i, 1), :], mean_var[:, i, 0:1],
                                      rstd[:, i:i + 1], ALU.subtract, ALU.mult).then_inc(S("h_rows"), 1)
                dve.wait_ge(S("h_rows"), k + 4)

        def norm_scalar(act, n):
            with act.Fori(0, NG) as g:
                act.wait_ge(S("mean_var"), g * 4 + (16 * n + 4))
                act.activation(std[:, :], mean_var[:, :, 1], ACT.Sqrt, bias=EPS).then_inc(S("std"), 1)
                act.wait_ge(S("h_turned"), g * 4 + (16 * n + 4 + 4))
                act.copy(hT[:, bass.ts(g, 512)], ps[:, 6, :]).then_inc(S("hT"), 1)

        def norm_tensor(pe, n):
            with pe.Fori(0, NG) as g:
                pe.wait_ge(S("h_rows"), g * 4 + (16 * n + 4))
                pe.wait_ge(S("hT"), g + (4 * n + 1))
                for i in range(4):
                    pe.transpose(ps[:, 6, i * P:(i + 1) * P], h_rows[:, i, :], ident[:, :]).then_inc(S("h_turned"), 1)

        def hT_ready(eng, n):
            eng.wait_ge(S("hT"), 4 * n + 4 + 1)

        GAT = {"L0": 0, "L1": 1, "L3": 2}
        VAL = {"L0": [0], "L1": [1], "L3": [2, 3]}

        def gat_setup_tensor(pe):
            pe.wait_ge(S("gat_loaded"), 16 * 10)
            for l in range(3):
                pe.matmul(ps[:, 7, 2 * l:2 * l + 2], gat_wT[:, l, :], gat_a[:, l, :], start=True, stop=True)\
                    .then_inc(S("score_vec"), 1)

        def gat_setup_vector(dve):
            dve.memset(zeros[:, :], 0.0).then_inc(S("zeros"), 1)
            dve.wait_ge(S("score_vec"), 3)
            dve.wait_ge(S("gat_loaded"), 16 * 10)
            for l in range(3):
                for s in range(2):
                    dve.tensor_copy(score_w[:, l, s, :], ps[:, 7, 2 * l + s:2 * l + s + 1].to_broadcast([P, P]))\
                        .then_inc(S("score_w"), 1)
            for v, l in enumerate((0, 1, 2, 2)):
                dve.tensor_copy(value_w[:, v, D:VC], ps[:, 7, 2 * l + 1:2 * l + 2]).then_inc(S("score_w"), 1)

        def gat_tensor(pe, L, n):
            l = GAT[L]
            pe.wait_ge(S("score_w"), 10)
            hT_ready(pe, n)
            for s in range(2):
                for c in range(NG):
                    pe.matmul(ps[:, 4 * s + c, :], score_w[:, l, s, :], hT[:, c * 512:(c + 1) * 512],
                              start=True, stop=True).then_inc(S("scores"), 1)
            for sign, v in enumerate(VAL[L]):
                if sign == 0:
                    pe.wait_ge(S("clamped"), clamp_end[L])
                else:
                    pe.wait_ge(S("x_updates"), pass_end[L])
                for i in range(NT):
                    pe.matmul(ps[:, i // TPB, (i % TPB) * VC:(i % TPB + 1) * VC], hT[:, i * P:(i + 1) * P],
                              value_w[:, v, :], start=True, stop=True).then_inc(S("values"), 1)
                pe.wait_ge(S("G"), 3 * (v + 1))
                pe.wait_ge(S("zeros"), 1)
                for b in range(NBK):
                    w = VC * (TPB if b < FULL else NT - FULL * TPB)
                    pe.matmul(ps[:, b, 0:w], zeros[:, 0:P], zeros[:, 0:w], start=True, stop=False,
                              skip_group_check=True).then_inc(S("cleared"), 1)
                pe.wait_ge(S("cleared"), NBK * (v + 1))
                with pe.Fori(0, NT // 2) as jj:
                    for b in range(2):
                        pe.wait_ge(S("weights"), jj * 2 + (NT * v + b + 1 + 2))
                        for i in range(NT):
                            mm = pe.matmul(ps[:, i // TPB, (i % TPB) * VC:(i % TPB + 1) * VC],
                                           PR[:, b, i * P:(i + 1) * P], G[:, sign, bass.ds(jj * 2 + b, 1), :],
                                           start=False, stop=False, skip_group_check=True)
                        mm.then_inc(S("weights_used"), 1)

        def gat_scalar(act, L, n):
            for sign, v in enumerate(VAL[L]):
                s = (1.0, -1.0)[sign]
                act.wait_ge(S("clamped"), clamp_end[L] - (len(VAL[L]) - 1) * (1 - sign))
                act.activation(R[:, sign, :], R[:, sign, :], ACT.Exp, scale=s * RISE).then_inc(S("R"), 1)
                act.wait_ge(S("s2_rel"), 2 * (v + 1))
                act.activation(K[:, sign, :], s2_rel[:, sign, :], ACT.Exp, scale=s * RISE).then_inc(S("KF"), 1)
                act.activation(F[:, sign, :], s2_rel[:, sign, :], ACT.Exp, scale=s * SLOPE).then_inc(S("KF"), 1)
                if sign == 0:
                    act.wait_ge(S("R"), v + 1)
                    act.wait_ge(S("KF"), 2 * v + 2)
                    k = VNUM[v]
                    with act.Fori(0, NT // 2) as jj:
                        for b in range(2):
                            act.wait_ge(S("weights"), jj * 2 + (NT * v + b + 1))
                            act.activation(T[:, b, :], R[:, 0, :], ACT.Relu, bias=-1.0,
                                           scale=K[:, 0, bass.ds(jj * 2 + b, 1)]).then_inc(S("T"), 1)
                if L == "L0" or sign == 1:
                    for q in range(3):
                        act.wait_ge(S("elu_in"), 3 * ELU[L] + q + 1)
                        lo, hi = PIECES[q]
                        act.activation(rows_b[:, lo:hi, :], rows_b[:, lo:hi, :], ACT.Exp).then_inc(S("elu_exp"), 1)

        VNUM = [0, 1, 2, 3]
        ELU = {"L0": 0, "L3": 1}
        PIECES = [(0, 9), (9, 15), (15, 16)]
        clamp_end = {"L0": 1, "L1": 2, "L3": 5}
        pass_end = {}

        def rows_of(q, c0, c1):
            lo, hi = PIECES[q]
            if hi <= FULL * TPB:
                return bank_rows(lo // TPB, hi // TPB, c0, c1)
            return ps[:, FULL:FULL + 1, c0:c1]

        def match(ap, q):
            lo, hi = PIECES[q]
            if hi <= FULL * TPB:
                return ap[:, lo:hi, :].rearrange("p (b k) d -> p b k d", k=TPB)
            return ap[:, lo:hi, :]

        def match1(ap, q, w):
            lo, hi = PIECES[q]
            if hi <= FULL * TPB:
                return ap[:, lo:hi].rearrange("p (b k) -> p b k", k=TPB).unsqueeze(3)\
                    .to_broadcast([P, (hi - lo) // TPB, TPB, w])
            return ap[:, lo:hi].unsqueeze(2).to_broadcast([P, hi - lo, w])

        def gat_vector(dve, L, n):
            l = GAT[L]
            base = clamp_end[L] - (1 if len(VAL[L]) == 1 else 3)
            dve.wait_ge(S("scores"), 8 * (l + 1))
            dve.tensor_reduce(s2_bound[:, 0:1], ps[:, 4:8, :], AX.XY, ALU.max).then_inc(S("bound"), 1)
            dve.wait_ge(S("bound"), l + 1)
            dve.tensor_scalar(R[:, 0, :], ps[:, 0:4, :], s2_bound[:, 0:1], CLAMP, ALU.add, ALU.min)\
                .then_inc(S("clamped"), 1)
            if L == "L3":
                dve.tensor_reduce(s2_bound[:, 1:2], ps[:, 4:8, :], AX.XY, ALU.min).then_inc(S("bound"), 1)
                dve.wait_ge(S("bound"), l + 2)
                dve.tensor_scalar(R[:, 1, :], ps[:, 0:4, :], s2_bound[:, 1:2], -CLAMP, ALU.add, ALU.max)\
                    .then_inc(S("clamped"), 1)
                dve.wait_ge(S("clamped"), base + 2)
                dve.tensor_scalar(R[:, 1, :], R[:, 1, :], CLAMP, None, ALU.min).then_inc(S("clamped"), 1)
            for sign, v in enumerate(VAL[L]):
                dve.wait_ge(S("values"), NT * (v + 1))
                dve.tensor_scalar(s2_rel[:, sign, 0:15].rearrange("p (b k) -> p b k", k=TPB),
                                  bank_rows(0, FULL, D, VC).squeeze(3) if False else
                                  ps[:, 0:FULL, 0:TPB * VC].rearrange("p b (k c) -> p b k c", c=VC)[:, :, :, D],
                                  s2_bound[:, sign:sign + 1], None, ALU.subtract).then_inc(S("s2_rel"), 1)
                dve.tensor_scalar(s2_rel[:, sign, 15:16], ps[:, FULL, D:VC], s2_bound[:, sign:sign + 1], None,
                                  ALU.subtract).then_inc(S("s2_rel"), 1)
                dve.wait_ge(S("KF"), 2 * v + 2)
                dve.tensor_copy(G[:, sign, :, D], F[:, sign, :]).then_inc(S("G"), 1)
                for b0, b1 in ((0, FULL), (FULL, NBK)):
                    if b1 == FULL:
                        o = G[:, sign, 0:15, 0:D].rearrange("p (b k) d -> p b k d", k=TPB)
                        i0 = bank_rows(0, FULL, 0, D)
                        i1 = F[:, sign, 0:15].rearrange("p (b k) -> p b k", k=TPB).unsqueeze(3).to_broadcast(
                            [P, FULL, TPB, D])
                        dve.tensor_tensor(o, i0, i1, ALU.mult).then_inc(S("G"), 1)
                    else:
                        dve.tensor_scalar(G[:, sign, 15, 0:D], ps[:, FULL, 0:D], F[:, sign, 15:16], None, ALU.mult)\
                            .then_inc(S("G"), 1)
                dve.wait_ge(S("R"), v + 1)
                with dve.Fori(0, NT // 2) as jj:
                    for b in range(2):
                        j = jj * 2 + b
                        if L == "L0":
                            dve.wait_ge(S(f"adj_landed{b}"), jj * 16 + 16)
                            dve.tensor_copy(adjT[:, bass.ds(j, 1), :], adj_in[:, b, :]).then_inc(S("adjT"), 1)
                        if sign == 0:
                            dve.wait_ge(S("T"), j + (NT * TNUM[v] + 1))
                        else:
                            dve.wait_ge(S("weights"), j + (NT * v + 1))
                            dve.tensor_scalar(T[:, b, :], R[:, 1, :], K[:, 1, bass.ds(j, 1)], 1.0, ALU.mult,
                                              ALU.min).then_inc(S("T_neg"), 1)
                            dve.wait_ge(S("T_neg"), j + 1)
                        dve.wait_ge(S("weights_used"), j + (NT * v + 1))
                        if L == "L0":
                            dve.wait_ge(S("adjT"), j + 1)
                        if sign == 0:
                            dve.scalar_tensor_tensor(PR[:, b, :], T[:, b, :], 1.0, adjT[:, bass.ds(j, 1), :],
                                                     ALU.add, ALU.mult).then_inc(S("weights"), 1)
                        else:
                            dve.tensor_tensor(PR[:, b, :], T[:, b, :], adjT[:, bass.ds(j, 1), :], ALU.mult)\
                                .then_inc(S("weights"), 1)
                dve.wait_ge(S("weights_used"), NT * (v + 1) + 2)
                for q in range(3):
                    lo, hi = PIECES[q]
                    cols = ps[:, lo // TPB:hi // TPB, 0:TPB * VC].rearrange("p b (k c) -> p b k c", c=VC)[:, :, :, D] \
                        if q < 2 else ps[:, FULL, D:VC]
                    o = rowrec[:, lo:hi].rearrange("p (b k) -> p b k", k=TPB) if q < 2 else rowrec[:, lo:hi]
                    dve.reciprocal(o, cols).then_inc(S("rowrec"), 1)
                dve.wait_ge(S("rowrec"), 3 * (v + 1))
                if L == "L3" and sign == 0:
                    for q in range(3):
                        dve.tensor_tensor(match(rows_c, q), rows_of(q, 0, D), match1(rowrec, q, D), ALU.mult)\
                            .then_inc(S("x_updates"), 1)
                    continue
                for q in range(3):
                    dve.tensor_tensor(match(rows_a, q), rows_of(q, 0, D), match1(rowrec, q, D), ALU.mult)\
                        .then_inc(S("att_rows"), 1)
                a0 = ATT[L] * 3
                for q in range(3):
                    lo, hi = PIECES[q]
                    dve.wait_ge(S("att_rows"), a0 + q + 1)
                    if L == "L1":
                        dve.tensor_tensor(x[:, lo:hi, :], x[:, lo:hi, :], rows_a[:, lo:hi, :], ALU.add)\
                            .then_inc(S("x_updates"), 1)
                        continue
                    if sign == 1:
                        dve.tensor_tensor(rows_a[:, lo:hi, :], rows_c[:, lo:hi, :], rows_a[:, lo:hi, :],
                                          ALU.subtract).then_inc(S("att_diff"), 1)
                        dve.wait_ge(S("att_diff"), q + 1)
                    dve.tensor_scalar(rows_b[:, lo:hi, :], rows_a[:, lo:hi, :], 0.0, None, ALU.min)\
                        .then_inc(S("elu_in"), 1)
                if L == "L1":
                    continue
                for q in range(3):
                    lo, hi = PIECES[q]
                    dve.wait_ge(S("elu_exp"), 3 * ELU[L] + q + 1)
                    dve.scalar_tensor_tensor(rows_a[:, lo:hi, :], rows_a[:, lo:hi, :], 0.0, rows_b[:, lo:hi, :],
                                             ALU.max, ALU.add).then_inc(S("elu_sum"), 1)
                    dve.wait_ge(S("elu_sum"), 3 * ELU[L] + q + 1)
                    dve.scalar_tensor_tensor(x[:, lo:hi, :], rows_a[:, lo:hi, :], -1.0, x[:, lo:hi, :],
                                             ALU.add, ALU.add).then_inc(S("x_updates"), 1)

        TNUM = [0, 1, 2]
        ATT = {"L0": 0, "L1": 1, "L3": 2}

        MOE = {"L0": 0, "L2": 1}
        ITEMS = {L: NG * HC[L] for L in HC}
        BASE = {"L0": 0, "L2": E * ITEMS["L0"]}

        def moe_items(L):
            out = []
            for s in range(2):
                for c in range(NG):
                    for k in range(HC[L]):
                        out.append((len(out), s, c, k))
            return out

        def moe_tensor(pe, L, n):
            m, items, base = MOE[L], moe_items(L), BASE[L]
            per = len(items)
            hT_ready(pe, n)
            pe.wait_ge(S("moe_loaded"), 16 * 9)
            for i in range(NT):
                mm = pe.matmul(ps[:, 0, i * E:(i + 1) * E], hT[:, i * P:(i + 1) * P], gate_w[:, m, :],
                               start=True, stop=True)
            mm.then_inc(S("gates"), 1)

            def thrice(out, w, xs, done, **flags):
                for step, (p, q) in enumerate(((0, 0), (0, 1), (1, 0))):
                    mm = pe.matmul(out, w[p], xs[q], start=flags["first"] and step == 0,
                                   stop=flags["first"] and step == 2, skip_group_check=not flags["first"])
                mm.then_inc(S(done), 1)

            def up(jj, item, extra=0):
                i, s, c, k = item
                at = jj * per + (base + i + extra)
                if (c, k) == (0, 0):
                    pe.wait_ge(S("w_lo"), jj * 4 + (2 * (E * m + s + 1) + (4 if extra else 0)))
                pe.wait_ge(S("act_h"), at + 1)
                thrice(ps[:, 4 + i % RING, :], [w_parts[:, s, 0, q, k * P:(k + 1) * P] for q in range(2)],
                       [hT_parts[:, q, c * 512:(c + 1) * 512] for q in range(2)], "up", first=True)

            def down(jj, item):
                i, s, c, k = item
                pe.wait_ge(S("h_lo"), jj * per + (base + i + 1 + RING))
                thrice(ps[:, c, :], [w_parts[:, s, 1, q, k * P:(k + 1) * P] for q in range(2)],
                       [h_parts[:, q, i % RING, :] for q in range(2)], "down", first=False)

            pe.wait_ge(S("hT_lo"), NG * (m + 1))
            for i in range(LAG):
                up(0, items[i])
            pe.wait_ge(S("comb"), m + 1)
            pe.transpose(ps[:, 1, 0:P], comb[:, :, :].rearrange("p e i -> p (e i)"), ident[:, :])\
                .then_inc(S("comb_turned"), 1)
            pe.wait_ge(S("comb8"), 16 * (m + 1))
            pe.wait_ge(S("comb_T"), m + 1)
            for c in range(NG):
                mm = pe.matmul(ps[:, c, :], b2[:, m, :], comb8[:, c * 512:(c + 1) * 512], start=True, stop=False,
                               skip_group_check=True)
            mm.then_inc(S("b2_in"), 1)
            pe.wait_ge(S("b2_in"), m + 1)
            with pe.Fori(0, E // 2 - 1) as jj:
                for i in range(per):
                    if i + LAG < per:
                        up(jj, items[i + LAG])
                    else:
                        up(jj, items[i + LAG - per], per)
                    down(jj, items[i])
            for i in range(per):
                if i + LAG < per:
                    up(E // 2 - 1, items[i + LAG])
                down(E // 2 - 1, items[i])
            for c in range(NG):
                pe.wait_ge(S("out_T"), NG * m + c + 1)
                for i in range(4):
                    mm = pe.transpose(ps[:, 4 + c, i * P:(i + 1) * P], out_T[:, c, i * P:(i + 1) * P], ident[:, :])
                mm.then_inc(S("out_turned"), 1)

        def moe_scalar(act, L, n):
            m, items, base = MOE[L], moe_items(L), BASE[L]
            per = len(items)
            act.wait_ge(S("moe_loaded"), 16 * 9)
            if L == "L2":
                act.wait_ge(S("top"), 2 * RANK_STEPS + 1)
                act.activation(topm[:, 4, :], topm[:, 4, :], ACT.Exp).then_inc(S("top_exp"), 1)
            with act.Fori(0, E // 2) as jj:
                def high(i):
                    at = jj * per + (base + i)
                    act.wait_ge(S("prod"), at + 1)
                    act.wait_ge(S("down"), at + 1)
                    act.copy(h_parts[:, 0, i % RING, :], act_h[:, i % RING, :]).then_inc(S("h_hi"), 1)

                for i, s, c, k in items:
                    at = jj * per + (base + i)
                    act.wait_ge(S("up"), at + 1)
                    act.wait_ge(S("h_lo"), at + 1)
                    act.sem_inc(S("act_seen"), 1)
                    act.activation(act_h[:, i % RING, :], ps[:, 4 + i % RING, :], ACT.Gelu if L == "L0" else ACT.Relu,
                                   bias=b1_T[L][:, bass.ds(jj * (2 * HC[L]) + (s * HC[L] + k), 1)])\
                        .then_inc(S("act_h"), 1)
                    if i:
                        high(i - 1)
                high(per - 1)
            act.wait_ge(S("down"), BASE[L] + E * ITEMS[L] + RING)
            for c in range(NG):
                act.copy(out_T[:, c, :], ps[:, c, :]).then_inc(S("out_T"), 1)

        RANK_STEPS = 11

        def moe_vector(dve, L, n):
            m, items, base = MOE[L], moe_items(L), BASE[L]
            per = len(items)
            count = [RANK_STEPS * m]

            def step(ins):
                ins.then_inc(S("top"), 1)
                count[0] += 1
                dve.wait_ge(S("top"), count[0])

            def over_e(ap):
                return ap.unsqueeze(2).to_broadcast([P, NT, E])

            def over_i(ap):
                return ap.unsqueeze(1).to_broadcast([P, NT, E])

            sc, key, oh1, oh2, sc2 = (top[:, q, :, :] for q in range(5))
            m1, m2, k1 = (topm[:, q, :] for q in range(3))
            dve.wait_ge(S("moe_loaded"), 16 * 9)
            dve.wait_ge(S("gates"), m + 1)
            step(dve.tensor_tensor(sc, ps[:, 0, 0:NT * E].rearrange("p (i e) -> p i e", e=E),
                                   over_i(gate_b[:, m, :]), ALU.add))
            step(dve.tensor_reduce(m1, sc, AX.X, ALU.max))
            step(dve.tensor_tensor(key, sc, over_e(m1), ALU.is_equal))
            step(dve.tensor_tensor(key, key, over_i(first[:, :]), ALU.mult))
            step(dve.tensor_reduce(k1, key, AX.X, ALU.max))
            step(dve.tensor_tensor(oh1, key, over_e(k1), ALU.is_equal))
            step(dve.scalar_tensor_tensor(sc2, oh1, -3.0e38, sc, ALU.mult, ALU.add))
            step(dve.tensor_reduce(m2, sc2, AX.X, ALU.max))
            step(dve.tensor_tensor(key, sc2, over_e(m2), ALU.is_equal))
            step(dve.tensor_tensor(key, key, over_i(first[:, :]), ALU.mult))
            step(dve.tensor_reduce(k1, key, AX.X, ALU.max))
            by_e = comb[:, :, :].rearrange("p e i -> p i e")
            if L == "L0":
                dve.tensor_tensor(oh2, key, over_e(k1), ALU.is_equal).then_inc(S("oh2"), 1)
                dve.wait_ge(S("oh2"), 1)
                dve.tensor_tensor(by_e, oh1, oh2, ALU.add).then_inc(S("comb"), 1)
            else:
                p1, p2 = topm[:, 5, :], topm[:, 6, :]
                step(dve.tensor_tensor(topm[:, 4, :], m2, m1, ALU.subtract))

                step(dve.tensor_tensor(oh2, key, over_e(k1), ALU.is_equal))
                dve.wait_ge(S("top_exp"), 1)
                step(dve.tensor_scalar(p1, topm[:, 4, :], 1.0, None, ALU.add))
                step(dve.reciprocal(p1, p1))
                step(dve.tensor_tensor(p2, topm[:, 4, :], p1, ALU.mult))
                dve.tensor_tensor(oh1, oh1, over_e(p1), ALU.mult).then_inc(S("oh2"), 1)
                dve.tensor_tensor(oh2, oh2, over_e(p2), ALU.mult).then_inc(S("oh2"), 1)
                dve.wait_ge(S("oh2"), 3)
                dve.tensor_tensor(by_e, oh1, oh2, ALU.add).then_inc(S("comb"), 1)
            dve.wait_ge(S("comb_turned"), m + 1)
            dve.tensor_copy(comb_T[:, :], ps[:, 1, 0:P]).then_inc(S("comb_T"), 1)
            with dve.Fori(0, E // 2) as jj:
                def low_part(i):
                    dve.wait_ge(S("h_hi"), jj * per + (base + i + 1))
                    dve.tensor_tensor(h_parts[:, 1, i % RING, :], act_h[:, i % RING, :], h_parts[:, 0, i % RING, :],
                                      ALU.subtract).then_inc(S("h_lo"), 1)

                for i, s, c, k in items:
                    at = jj * per + (base + i)
                    if (c, k) == (0, 0):
                        dve.wait_ge(S(f"comb_b{s}"), jj * 16 + 16 * (4 * m + 1))
                    dve.wait_ge(S("act_h"), at + 1 + RING)
                    dve.tensor_tensor(act_h[:, i % RING, :], act_h[:, i % RING, :],
                                      comb_b[:, s, c * 512:(c + 1) * 512], ALU.mult).then_inc(S("prod"), 1)
                    if i:
                        low_part(i - 1)
                low_part(per - 1)
            for c in range(NG):
                dve.wait_ge(S("out_turned"), NG * m + c + 1)
                dve.tensor_tensor(x[:, 4 * c:4 * c + 4, :], x[:, 4 * c:4 * c + 4, :],
                                  ps[:, 4 + c, :].rearrange("p (i d) -> p i d", d=D), ALU.add)\
                    .then_inc(S("x_updates"), 1)

        def moe_pool(pool, L, n):
            m, base, H = MOE[L], BASE[L], HC[L] * P
            for c in range(NG):
                cols = slice(c * 512, (c + 1) * 512)
                pool.wait_ge(S("hT"), 4 * n + c + 1 + 1)
                pool.tensor_copy(hT_parts[:, 0, cols], hT[:, cols]).then_inc(S("hT_hi"), 1)
                pool.wait_ge(S("hT_hi"), NG * m + c + 1)
                pool.tensor_tensor(hT_parts[:, 1, cols], hT[:, cols], hT_parts[:, 0, cols], ALU.subtract)\
                    .then_inc(S("hT_lo"), 1)

            def split(jj, s):
                pool.wait_ge(S(f"expert_w{s}"), jj * 32 + 32 + 32 * 4 * m)
                pool.sem_inc(S("split_seen"), 1)
                for w, raw in enumerate((w1_e[:, s, 0:H], w2_e[:, s, :, :].rearrange("p k d -> p (k d)")[:, 0:H])):
                    pool.tensor_copy(w_parts[:, s, w, 0, 0:H], raw).then_inc(S("w_hi"), 1)
                    pool.wait_ge(S("w_hi"), jj * 4 + (2 * (E * m + s) + w + 1))
                    pool.tensor_tensor(w_parts[:, s, w, 1, 0:H], raw, w_parts[:, s, w, 0, 0:H], ALU.subtract)\
                        .then_inc(S("w_lo"), 1)

            for s in range(2):
                split(0, s)
            with pool.Fori(1, E // 2) as jj:
                for s in range(2):
                    pool.wait_ge(S("down"), (jj * 2 + s) * ITEMS[L] + (base - ITEMS[L] + RING))
                    split(jj, s)

        def moe_sync(sp, L, n):
            m, base = MOE[L], BASE[L]
            H = HC[L] * P
            w1, w2 = t[f"{L}_ffn_W1"], t[f"{L}_ffn_W2"]

            def weights(e, s):
                sp.dma_start(w1_e[:, s, 0:H], w1[bass.ds(e, 1), :, :].rearrange("e d h -> d (e h)"))\
                    .then_inc(S(f"expert_w{s}"), 16)
                sp.dma_start(w2_e[:, s, 0:HC[L], :],
                             w2[bass.ds(e, 1), :, :].rearrange("e (k p) d -> p (e k) d", p=P))\
                    .then_inc(S(f"expert_w{s}"), 16)

            def mix(e, s):
                sp.dma_start(comb_b[:, s, :],
                             comb_dram[L][bass.ds(e, 1), :].to_broadcast([P, N])).then_inc(S(f"comb_b{s}"), 16)

            for s in range(2):
                if m:
                    sp.wait_ge(S("w_lo"), 2 * E)
                    if "sage" in need:
                        sp.wait_ge(S("x_updates"), need["sage"])
                weights(s, s)
            sp.wait_ge(S("comb_T"), m + 1)
            sp.dma_start(comb_dram[L].rearrange("e (i n) -> (e i) n", n=P), comb_T[:, :]).then_inc(S("comb_out"), 16)
            sp.wait_ge(S("comb_out"), 16 * (m + 1))
            sp.dma_start(comb8, comb_dram[L][:, :]).then_inc(S("comb8"), 16)
            for s in range(2):
                mix(s, s)
            with sp.Fori(1, E // 2) as jj:
                for s in range(2):
                    e = jj * 2 + s
                    sp.wait_ge(S("prod"), e * ITEMS[L] + (base - ITEMS[L]))
                    mix(e, s)
                    sp.wait_ge(S("w_lo"), e * 2 + 2 * (E * m - 1))
                    weights(e, s)

        PARTS = [(0, 0, P), (1, P, P), (2, 2 * P, NS), (3, 2 * P + NS, NS)]
        HALO = 3

        def on_chunk(eng, g, name, k):
            eng.wait_ge(S(name), g * 4 + (k + 1 + 2))

        CHUNKS = ["m_turned", "m_rows", "m_tri_dA", "m_segsum", "m_decay", "m_mix", "m_x_dt", "m_x_decayed",
                  "m_x_skip", "m_y_parts", "m_state_new", "m_state", "m_y_sum", "m_y_skip", "m_y_gated",
                  "m_yT_turned", "m_yT", "m_out", "m_y_rows", "m_square"]

        FIRST = -1

        def mamba_groups(eng, body):
            with eng.Fori(0, NG - 1) as g:
                body(g, False)
            body(NG - 1, True)

        def mamba_tensor(pe, n):
            pe.wait_ge(S("mamba_loaded"), 16 * 10)
            hT_ready(pe, n)
            for k in range(2):
                mm = pe.matmul(ps[:, 5, k * P:(k + 1) * P], wout_T[:, k, :], w_lin[:, :], start=True, stop=True)
            mm.then_inc(S("m_proj"), 1)
            pe.wait_ge(S("m_halved"), 3)
            for i in range(NT):
                if i >= 4:
                    pe.wait_ge(S("m_z_gate"), i - 3)
                    pe.wait_ge(S("m_dt_raw"), i - 3)
                pe.matmul(ps[:, i % 4, 0:DI + NH], hT[:, i * P:(i + 1) * P], win_zd[:, :], start=True, stop=True)\
                    .then_inc(S("m_zd"), 1)

            def conv_in(g, q):
                if not (g is FIRST and q == 0):
                    pe.wait_ge(S("m_conv_seed"), g * 4 + (4 + q))
                    pe.sem_inc(S("m_seed_seen"), 1)
                _, c0, w = PARTS[q]
                pe.matmul(ps[0:w, 5, :], win_x[:, c0:c0 + w], hT[:, bass.ts(g + 1, 512)], start=True, stop=True)\
                    .then_inc(S("m_conv_in"), 1)

            def turn(g, i):
                pe.wait_ge(S("m_conv"), g * 4 + (4 + 3))
                on_chunk(pe, g, "m_rows", i + 3)
                for q in range(2):
                    pe.transpose(ps[:, 4, q * P:(q + 1) * P], conv_out[:, q, i * P:(i + 1) * P], ident[:, :])
                pe.transpose(ps[:, 4, DI:DI + NS], conv_out[0:NS, 2, i * P:(i + 1) * P], ident[0:NS, 0:NS])\
                    .then_inc(S("m_turned"), 1)

            def segsum(g, i):
                on_chunk(pe, g, "m_tri_dA", i)
                on_chunk(pe, g, "m_decay", i - 1)
                pe.matmul(ps[:, 7, :], after[:, :], tri_dA[:, i % 2, :], start=True, stop=True)\
                    .then_inc(S("m_segsum"), 1)

            def front(g):
                turn(g, 0)
                turn(g, 1)
                pe.wait_ge(S("m_conv"), g * 4 + (4 + 4))
                if g is not FIRST:
                    pe.wait_ge(S("m_cb_masked"), g + 1)
                for i in range(4):
                    mm = pe.matmul(ps[:, 6, i * P:(i + 1) * P], conv_out[0:NS, 2, i * P:(i + 1) * P],
                                   conv_out[0:NS, 3, i * P:(i + 1) * P], start=True, stop=True)
                mm.then_inc(S("m_cb"), 1)
                turn(g, 2)
                turn(g, 3)

            pe.wait_ge(S("m_clear"), 5)
            for q in range(4):
                conv_in(FIRST, q)
            pe.wait_ge(S("m_dA"), 1)
            pe.matmul(ps[:, 4, 0:64], tri[:, :], dts[:, 4, :], start=True, stop=True)
            pe.matmul(ps[:, 4, 64:128], ones[:, :], dts[:, 4, :], start=True, stop=True).then_inc(S("m_cum"), 1)
            segsum(0, 0)
            pe.wait_ge(S("m_carry"), 1)
            front(FIRST)

            def body(g, last):
                def tail(i):
                    on_chunk(pe, g, "m_y_gated", i)
                    on_chunk(pe, g, "m_y_rows", i - 1)
                    for k in range(2):
                        mm = pe.transpose(ps[:, 3, k * P:(k + 1) * P], y_gated[:, i % 2, k * P:(k + 1) * P],
                                          ident[:, :])
                    mm.then_inc(S("m_yT_turned"), 1)
                    on_chunk(pe, g, "m_yT", i)
                    for k in range(2):
                        mm = pe.matmul(ps[:, 3, DI:DI + D], y_T[:, i % 2, k * P:(k + 1) * P], w_proj[:, k, :],
                                       start=(k == 0), stop=(k == 1))
                    mm.then_inc(S("m_out"), 1)

                for i in range(4):
                    if not (last and i == 3):
                        segsum(g, i + 1)
                    on_chunk(pe, g, "m_state", i - 1)
                    on_chunk(pe, g, "m_y_sum", i - 2)
                    pe.matmul(ps[:, i % 2, DI:2 * DI], conv_out[0:NS, 3, i * P:(i + 1) * P], state[:, i % 2, :],
                              start=True, stop=True)
                    on_chunk(pe, g, "m_mix", i)
                    on_chunk(pe, g, "m_x_dt", i)
                    for h in range(NH):
                        mm = pe.matmul(ps[:, i % 2, h * HD:(h + 1) * HD], mixm[:, i % 2, h * P:(h + 1) * P],
                                       x_dt[:, i % 2, h * HD:(h + 1) * HD], start=True, stop=True)
                    mm.then_inc(S("m_y_parts"), 1)
                    on_chunk(pe, g, "m_x_decayed", i)
                    pe.matmul(ps[0:NS, 2, 0:DI], xb_rows[:, i, DI:DI + NS], x_decayed[:, i % 2, :],
                              start=True, stop=True).then_inc(S("m_state_new"), 1)
                    if not last:
                        conv_in(g, i)
                    if i >= 1:
                        tail(i - 1)
                if not last:
                    front(g)
                tail(3)

            mamba_groups(pe, body)

        def mamba_scalar(act, n):
            act.wait_ge(S("mamba_loaded"), 16 * 10)
            act.activation(exp_A[:, :], small_in[:, 1, :], ACT.Exp).then_inc(S("m_expA"), 1)
            for i in range(NT):
                act.wait_ge(S("m_zd"), i + 1)
                if i >= 2:
                    act.wait_ge(S("m_z_gate"), i - 1)
                act.activation(z_tanh[:, i % 2, :], ps[:, i % 4, 0:DI], ACT.Tanh).then_inc(S("m_z_tanh"), 1)
            act.wait_ge(S("m_dt_abs"), 1)
            act.activation(dts[:, 2, :], dts[:, 1, :], ACT.Exp, scale=-1.0).then_inc(S("m_dt_exp"), 1)
            act.wait_ge(S("m_dt_exp"), 1)
            act.activation(dts[:, 5, :], dts[:, 2, :], ACT.Ln, bias=1.0).then_inc(S("m_dt_ln"), 1)

            def seed(g, q):
                _, c0, w = PARTS[q]
                if g is not FIRST:
                    act.wait_ge(S("m_conv_tap"), g * 12 + 3 * (q + 1))
                    act.copy(conv_raw[:, q, 0:HALO], conv_raw[:, q, 512:512 + HALO]).then_inc(S("m_halo"), 1)
                    act.wait_ge(S("m_halo"), g * 4 + (q + 1))
                    act.wait_ge(S("m_conv"), g * 4 + (q + 1))
                act.wait_ge(S("m_conv_in"), g * 4 + (4 + q + 1))
                act.copy(conv_raw[0:w, q, HALO:HALO + 512], ps[0:w, 5, :]).then_inc(S("m_conv_raw"), 1)
                act.activation(conv[0:w, q, :], ps[0:w, 5, :], ACT.Identity, bias=conv_b[0:w, q:q + 1],
                               scale=conv_w[0:w, q, HALO:HALO + 1]).then_inc(S("m_conv_seed"), 1)

            def tanh(g, q):
                w = PARTS[q][2]
                act.wait_ge(S("m_conv_tap"), g * 12 + (12 + 3 * (q + 1)))
                act.activation(conv_tanh[0:w, q, :], conv[0:w, q, :], ACT.Tanh).then_inc(S("m_conv_tanh"), 1)

            def decays(g, i):
                on_chunk(act, g, "m_segsum", i)
                on_chunk(act, g, "m_mix", i - 2)
                on_chunk(act, g, "m_x_decayed", i - 2)
                act.activation(decay[:, i % 2, :], ps[:, 7, :], ACT.Exp).then_inc(S("m_decay"), 1)

            def rows(g):
                for i in range(4):
                    on_chunk(act, g, "m_turned", i + 4)
                    if g is not FIRST:
                        on_chunk(act, g, "m_state_new", i)
                        on_chunk(act, g, "m_x_skip", i)
                    act.copy(xb_rows[:, i, :], ps[:, 4, 0:DI + NS]).then_inc(S("m_rows"), 1)

            for q in range(4):
                seed(FIRST, q)
            act.wait_ge(S("m_cum"), 1)
            act.activation(carry[:, :, :], ps[:, 4, 0:128].rearrange("p (s n) -> p s n", s=2), ACT.Exp)\
                .then_inc(S("m_carry"), 1)
            decays(0, 0)
            for q in range(4):
                tanh(FIRST, q)
            rows(FIRST)

            def body(g, last):
                def tail(i, between=None):
                    on_chunk(act, g, "m_yT_turned", i)
                    on_chunk(act, g, "m_out", i - 2)
                    act.copy(y_T[:, i % 2, :], ps[:, 3, 0:DI]).then_inc(S("m_yT"), 1)
                    on_chunk(act, g, "m_square", i - 1)
                    act.activation(y_square[:, :], y_gated[:, i % 2, :], ACT.Square,
                                   accum_out=sumsq[:, bass.ds(g * 4 + i, 1)]).then_inc(S("m_square"), 1)
                    on_chunk(act, g, "m_out", i)
                    act.copy(y_rows[:, bass.ds(g * 4 + i, 1), :], ps[:, 3, DI:DI + D]).then_inc(S("m_y_rows"), 1)

                for i in range(4):
                    if not (last and i == 3):
                        decays(g, i + 1)
                    if not last:
                        seed(g, i)
                    if i >= 1:
                        tail(i - 1)
                    if not last:
                        tanh(g, i)
                if not last:
                    rows(g)
                tail(3)

            mamba_groups(act, body)
            act.wait_ge(S("m_square"), NT + 2)
            act.activation(sumsq[:, :], sumsq[:, :], ACT.Sqrt, scale=1.0 / DI, bias=EPS).then_inc(S("m_rms"), 1)

        def mamba_pool(pool):
            pool.wait_ge(S("m_dA"), 1)

            def heads(g, ap, c, w):
                return ap[:, bass.ds(g * 16 + c * NH, NH)].unsqueeze(2).to_broadcast([P, NH, w])

            def tri_times(g, i):
                on_chunk(pool, g, "m_segsum", i - 2)
                pool.tensor_tensor(tri_dA[:, i % 2, :].rearrange("p (h l) -> p h l", h=NH),
                                   tri[:, :].unsqueeze(1).to_broadcast([P, NH, P]), heads(g, dts[:, 4, :], i, P),
                                   ALU.mult).then_inc(S("m_tri_dA"), 1)

            def body(g, last):
                for i in range(4):
                    if not (last and i == 3):
                        tri_times(g, i + 1)
                    on_chunk(pool, g, "m_rows", i)
                    on_chunk(pool, g, "m_y_parts", i - 2)
                    on_chunk(pool, g, "m_x_decayed", i - 2)
                    x3 = xb_rows[:, i, 0:DI].rearrange("p (h d) -> p h d", h=NH)
                    pool.tensor_tensor(x_dt[:, i % 2, :].rearrange("p (h d) -> p h d", h=NH), x3,
                                       heads(g, dts[:, 3, :], i, HD), ALU.mult).then_inc(S("m_x_dt"), 1)
                    on_chunk(pool, g, "m_y_skip", i - 2)
                    pool.tensor_tensor(x_skip[:, i % 2, :].rearrange("p (h d) -> p h d", h=NH), x3,
                                       small_in[:, 2, :].unsqueeze(2).to_broadcast([P, NH, HD]), ALU.mult)\
                        .then_inc(S("m_x_skip"), 1)
                    on_chunk(pool, g, "m_x_dt", i)
                    on_chunk(pool, g, "m_decay", i)
                    on_chunk(pool, g, "m_state_new", i - 2)
                    last_row = decay[:, i % 2, :].rearrange("p (h l) -> p h l", h=NH)[:, :, P - 1]
                    pool.tensor_tensor(x_decayed[:, i % 2, :].rearrange("p (h d) -> p h d", h=NH),
                                       x_dt[:, i % 2, :].rearrange("p (h d) -> p h d", h=NH),
                                       last_row.unsqueeze(2).to_broadcast([P, NH, HD]), ALU.mult)\
                        .then_inc(S("m_x_decayed"), 1)

            tri_times(0, 0)
            mamba_groups(pool, body)

        def mamba_vector(dve, n):
            dve.wait_ge(S("mamba_loaded"), 16 * 10)
            dve.tensor_scalar(win_zd[:, 0:DI], win_zd[:, 0:DI], 0.5, None, ALU.mult).then_inc(S("m_halved"), 1)
            dve.tensor_scalar(conv_w[:, :, :], conv_w[:, :, :], 0.5, None, ALU.mult).then_inc(S("m_halved"), 1)
            dve.tensor_scalar(conv_b[:, :], conv_b[:, :], 0.5, None, ALU.mult).then_inc(S("m_halved"), 1)
            dve.memset(ones[:, :], 1.0).then_inc(S("m_clear"), 1)
            dve.memset(conv_raw[:, :, :], 0.0).then_inc(S("m_clear"), 1)
            dve.memset(state[:, :], 0.0).then_inc(S("m_clear"), 1)
            dve.wait_ge(S("m_proj"), 1)
            for k in range(2):
                dve.tensor_scalar(w_proj[:, k, :], ps[:, 5, k * P:(k + 1) * P], norm_w[:, k:k + 1], None, ALU.mult)\
                    .then_inc(S("m_clear"), 1)
            dve.wait_ge(S("m_clear"), 5)
            for i in range(NT):
                dve.wait_ge(S("m_z_tanh"), i + 1)
                dve.tensor_copy(dts[:, 0, i * NH:(i + 1) * NH], ps[:, i % 4, DI:DI + NH]).then_inc(S("m_dt_raw"), 1)
                dve.scalar_tensor_tensor(z_gate[:, i, :], z_tanh[:, i % 2, :], 1.0, ps[:, i % 4, 0:DI],
                                         ALU.add, ALU.mult).then_inc(S("m_z_gate"), 1)
            dt3 = [dts[:, q, :].rearrange("p (c h) -> p c h", h=NH) for q in range(6)]
            dve.wait_ge(S("m_dt_raw"), NT)
            dve.tensor_tensor(dt3[0], dt3[0], small_in[:, 0, :].unsqueeze(1).to_broadcast([P, NT, NH]), ALU.add)\
                .then_inc(S("m_dt_bias"), 1)
            dve.wait_ge(S("m_dt_bias"), 1)
            dve.scalar_tensor_tensor(dts[:, 1, :], dts[:, 0, :], -1.0, dts[:, 0, :], ALU.mult, ALU.max)\
                .then_inc(S("m_dt_abs"), 1)
            dve.wait_ge(S("m_dt_ln"), 1)
            dve.scalar_tensor_tensor(dts[:, 3, :], dts[:, 0, :], 0.0, dts[:, 5, :], ALU.max, ALU.add)\
                .then_inc(S("m_dt_bias"), 1)
            dve.wait_ge(S("m_dt_bias"), 2)
            dve.wait_ge(S("m_expA"), 1)
            dve.scalar_tensor_tensor(dt3[4], dt3[3], -1.0, exp_A[:, :].unsqueeze(1).to_broadcast([P, NT, NH]),
                                     ALU.mult, ALU.mult).then_inc(S("m_dA"), 1)

            def tap(g, q, k):
                w = PARTS[q][2]
                if k == 0:
                    dve.wait_ge(S("m_conv_seed"), g * 4 + (4 + q + 1))
                else:
                    dve.wait_ge(S("m_conv_tap"), g * 12 + (12 + 3 * q + k))
                dve.scalar_tensor_tensor(conv[0:w, q, :], conv_raw[0:w, q, k:k + 512], conv_w[0:w, q, k:k + 1],
                                         conv[0:w, q, :], ALU.mult, ALU.add).then_inc(S("m_conv_tap"), 1)

            def silu(g, q):
                w = PARTS[q][2]
                dve.wait_ge(S("m_conv_tanh"), g * 4 + (4 + q + 1))
                if g is not FIRST:
                    if q == 0:
                        on_chunk(dve, g, "m_turned", 3)
                    if q == 2:
                        dve.wait_ge(S("m_cb"), g + 1)
                    if q == 3:
                        on_chunk(dve, g, "m_y_parts", 3)
                dve.scalar_tensor_tensor(conv_out[0:w, q, :], conv_tanh[0:w, q, :], 1.0, conv[0:w, q, :],
                                         ALU.add, ALU.mult).then_inc(S("m_conv"), 1)

            def masked(g):
                dve.wait_ge(S("m_cb"), g + 2)
                dve.tensor_tensor(cb_masked[:, :, :], ps[:, 6, :].rearrange("p (i l) -> p i l", i=4),
                                  tri[:, :].unsqueeze(1).to_broadcast([P, 4, P]), ALU.mult)\
                    .then_inc(S("m_cb_masked"), 1)
                dve.wait_ge(S("m_cb_masked"), g + 2)

            def mix(g, i):
                on_chunk(dve, g, "m_decay", i)
                on_chunk(dve, g, "m_y_parts", i - 2)
                dve.tensor_tensor(mixm[:, i % 2, :].rearrange("p (h l) -> p h l", h=NH),
                                  decay[:, i % 2, :].rearrange("p (h l) -> p h l", h=NH),
                                  cb_masked[:, i % 4, :].unsqueeze(1).to_broadcast([P, NH, P]), ALU.mult)\
                    .then_inc(S("m_mix"), 1)

            for q in range(4):
                for k in range(HALO):
                    tap(FIRST, q, k)
            for q in range(4):
                silu(FIRST, q)
            masked(FIRST)
            mix(0, 0)
            dve.wait_ge(S("m_carry"), 1)

            def body(g, last):
                def heads(ap, rows, c, w):
                    return ap[0:rows, bass.ds(g * 16 + c * NH, NH)].unsqueeze(2).to_broadcast([rows, NH, w])

                for i in range(4):
                    b = i % 2
                    if i < 3:
                        mix(g, i + 1)
                    on_chunk(dve, g, "m_state", i - 1)
                    on_chunk(dve, g, "m_y_parts", i - 1)
                    dve.tensor_tensor(state[:, 1 - b, :].rearrange("p (h d) -> p h d", h=NH),
                                      state[:, b, :].rearrange("p (h d) -> p h d", h=NH),
                                      heads(carry[:, 1, :], NS, i, HD), ALU.mult).then_inc(S("m_state_aged"), 1)
                    on_chunk(dve, g, "m_y_parts", i)
                    on_chunk(dve, g, "m_y_sum", i - 1)
                    dve.tensor_tensor(y_a[:, :].rearrange("p (h d) -> p h d", h=NH),
                                      ps[:, b, DI:2 * DI].rearrange("p (h d) -> p h d", h=NH),
                                      heads(carry[:, 0, :], P, i, HD), ALU.mult).then_inc(S("m_y_a"), 1)
                    on_chunk(dve, g, "m_state_new", i)
                    dve.wait_ge(S("m_state_aged"), g * 4 + (i + 1))
                    dve.tensor_tensor(state[:, 1 - b, :], state[:, 1 - b, :], ps[0:NS, 2, 0:DI], ALU.add)\
                        .then_inc(S("m_state"), 1)
                    dve.wait_ge(S("m_y_a"), g * 4 + (i + 1))
                    on_chunk(dve, g, "m_y_skip", i - 1)
                    dve.tensor_tensor(y_b[:, :], y_a[:, :], ps[:, b, 0:DI], ALU.add).then_inc(S("m_y_sum"), 1)
                    if not last:
                        tap(g, i, 0)
                    on_chunk(dve, g, "m_y_sum", i)
                    on_chunk(dve, g, "m_x_skip", i)
                    on_chunk(dve, g, "m_yT_turned", i - 2)
                    on_chunk(dve, g, "m_square", i - 2)
                    dve.tensor_tensor(y_b[:, :], y_b[:, :], x_skip[:, b, :], ALU.add).then_inc(S("m_y_skip"), 1)
                    if not last:
                        tap(g, i, 1)
                    on_chunk(dve, g, "m_y_skip", i)
                    dve.tensor_tensor(y_gated[:, b, :], y_b[:, :], z_gate[:, bass.ds(g * 4 + i, 1), :], ALU.mult)\
                        .then_inc(S("m_y_gated"), 1)
                    if not last:
                        tap(g, i, 2)
                        if i:
                            silu(g, i - 1)
                if not last:
                    silu(g, 3)
                    masked(g)
                    mix(g, 4)

            mamba_groups(dve, body)
            dve.wait_ge(S("m_rms"), 1)
            dve.reciprocal(sumsq[:, :], sumsq[:, :]).then_inc(S("m_rms_inv"), 1)
            dve.wait_ge(S("m_y_rows"), NT + 2)
            dve.wait_ge(S("m_x_bias"), 1)
            dve.wait_ge(S("m_rms_inv"), 1)
            for i in range(NT):
                dve.scalar_tensor_tensor(x[:, i, :], y_rows[:, i, :], sumsq[:, i:i + 1], x[:, i, :],
                                         ALU.mult, ALU.add).then_inc(S("x_updates"), 1)

        def add_to_rows(pool, n, bias, name, loaded, count):
            hT_ready(pool, n)
            pool.wait_ge(S(loaded), 16 * count)
            pool.tensor_tensor(x[:, :, :], x[:, :, :], bias[:, :].unsqueeze(1).to_broadcast([P, NT, D]), ALU.add)\
                .then_inc(S(name), 1)

        PW = 3 * D + 1

        def sage_tensor(pe, n):
            pe.wait_ge(S("sage_loaded"), 16 * 2)
            hT_ready(pe, n)
            for i in range(NT):
                pe.matmul(ps[:, i // 2, (i % 2) * 2 * D:(i % 2 + 1) * 2 * D], hT[:, i * P:(i + 1) * P], sage_w[:, :],
                          start=True, stop=True).then_inc(S("g_in"), 1)
            pe.wait_ge(S("g_y"), 5 * NG + 1)
            with pe.Fori(0, NT // 2) as ii:
                for b in range(2):
                    pe.wait_ge(S("g_x"), ii * 2 + (b + 1 + NG))
                    for j in range(NT):
                        mm = pe.matmul(ps[:, b, 0:PW], adjT[:, j, bass.ds(ii * 2 * P + b * P, P)],
                                       sage_y[:, j, 0:PW], start=(j == 0), stop=(j == NT - 1))
                    mm.then_inc(S("g_sums"), 1)

        def sage_vector(dve, n):
            dve.wait_ge(S("g_x_bias"), 1)
            dve.memset(sage_y[:, :, 3 * D:PW], 1.0).then_inc(S("g_y"), 1)
            for c in range(NG):
                a = slice(4 * c, 4 * c + 4)
                psy = ps[:, 2 * c:2 * c + 2, :].rearrange("p b (k d) -> p b k d", k=2)
                four = lambda ap: ap.rearrange("p (b k) d -> p b k d", k=2)
                dve.wait_ge(S("g_in"), 4 * c + 4)
                k = 1 + 5 * c
                dve.tensor_copy(four(sage_y[:, a, 0:D]), psy[:, :, :, 0:D]).then_inc(S("g_y"), 1)
                dve.wait_ge(S("g_y"), k + 1)
                dve.tensor_tensor(four(sage_r[:, a, :]), psy[:, :, :, 0:D], four(sage_y[:, a, 0:D]), ALU.subtract)\
                    .then_inc(S("g_y"), 1)
                dve.wait_ge(S("g_y"), k + 2)
                dve.tensor_copy(sage_y[:, a, D:2 * D], sage_r[:, a, :]).then_inc(S("g_y"), 1)
                dve.wait_ge(S("g_y"), k + 3)
                dve.tensor_tensor(sage_r[:, a, :], sage_r[:, a, :], sage_y[:, a, D:2 * D], ALU.subtract)\
                    .then_inc(S("g_y"), 1)
                dve.wait_ge(S("g_y"), k + 4)
                dve.tensor_copy(sage_y[:, a, 2 * D:3 * D], sage_r[:, a, :]).then_inc(S("g_y"), 1)
            for c in range(NG):
                psy = ps[:, 2 * c:2 * c + 2, :].rearrange("p b (k d) -> p b k d", k=4)
                x4 = x[:, 4 * c:4 * c + 4, :].rearrange("p (b k) d -> p b k d", k=2)
                dve.tensor_tensor(x4, x4, ps[:, 2 * c:2 * c + 2, :].rearrange("p b (k s d) -> p b k s d", k=2, s=2)
                                  [:, :, :, 1, :], ALU.add).then_inc(S("g_x"), 1)
            with dve.Fori(0, NT // 2) as ii:
                for b in range(2):
                    at = ii * 2 + b
                    dve.wait_ge(S("g_sums"), at + 1)
                    dve.reciprocal(sage_rec[:, b:b + 1], ps[:, b, 3 * D:PW]).then_inc(S("g_rec"), 1)
                    dve.tensor_reduce(sage_sum[:, b, :], ps[:, b, 0:3 * D].rearrange("p (s d) -> p d s", s=3), AX.X,
                                      ALU.add).then_inc(S("g_x"), 1)
                    dve.wait_ge(S("g_rec"), at + 1)
                    dve.wait_ge(S("g_x"), at + (NG + 2 + 1))
                    dve.scalar_tensor_tensor(x[:, bass.ds(at, 1), :], sage_sum[:, b, :], sage_rec[:, b:b + 1],
                                             x[:, bass.ds(at, 1), :], ALU.mult, ALU.add)\
                        .then_inc(S("x_updates"), 1)

        def on_tile(eng, g, name, k):
            eng.wait_ge(S(name), g * 4 + (k + 1 + 2))

        last = {name: NT + 2 for name in CHUNKS} | {
            "m_conv_in": 4 * NG, "m_conv_raw": 4 * NG, "m_conv_seed": 4 * NG, "m_conv_tap": 12 * NG,
            "m_conv_tanh": 4 * NG, "m_conv": 4 * NG, "m_cb": NG, "m_cb_masked": NG, "m_halo": 4 * (NG - 1),
            "m_zd": NT, "m_z_tanh": NT, "m_z_gate": NT, "m_dt_raw": NT, "m_dt_bias": 2, "m_dt_abs": 1,
                 "m_dt_exp": 1, "m_dt_ln": 1, "m_dA": 1, "m_cum": 1, "m_carry": 1, "m_y_a": NT, "m_state_aged": NT}
        signals = """y_A_min y_block y_cb y_cbm y_clear y_conv y_conv_in y_dec y_dec_cb y_dt y_dt_abs y_dt_in y_exp y_fD y_gT y_gT_w y_gated y_halved y_ln y_mix y_normed y_o y_q y_raw y_rms y_rows y_slice_w y_spans y_ss y_t y_tanh y_tap y_tdA y_turned y_y y_z y_z_in y_z_tanh""".split()
        reused.update({y: (m, last[m]) for y, m in zip(signals, sorted(last), strict=False)})

        def after_mamba(name, count):
            return reused[name][1] + count

        TILES = ["s_logits", "s_add", "s_maxed", "s_sub", "s_exped", "s_summed", "s_rec", "s_sw", "s_acc", "s_A",
                 "s_turned", "s_swT"]
        S_LOADED = 16 * 20
        HPARTS = [(0, P), (1, P), (2, P), (3, P), (4, NS), (5, NS)]

        def heads8(ap, rows, w):
            return ap.unsqueeze(2).to_broadcast([rows, SH, w])

        def by_head(ap):
            return ap.rearrange("p (h g) -> p h g", h=SH)

        def slice_tensor(pe, n):
            pe.wait_ge(S("s_loaded"), S_LOADED)
            for h in range(SH):
                pe.matmul(ps[:, 0, h * SG:(h + 1) * SG], wx_h[:, h, :], ws_T, start=True, stop=True)
            for h in range(SH):
                mm = pe.matmul(ps[:, 1, h * SG:(h + 1) * SG], bx_T[:, h:h + 1].to_broadcast([NS, P]), ws_T,
                               start=True, stop=True)
            mm.then_inc(S("s_weights"), 1)
            pe.wait_ge(S("s_logit_w"), 2)
            pe.wait_ge(S("zeros"), 1)
            for w in range(0, SI, 256):
                mm = pe.matmul(ps[:, 2, w:w + 256], zeros[:, 0:P], zeros[:, 0:256], start=(w == 0), stop=False,
                               skip_group_check=True)
            mm.then_inc(S("s_cleared"), 1)
            pe.wait_ge(S("s_cleared"), 1)
            with pe.Fori(0, NG) as g:
                def logits(i):
                    on_tile(pe, g, "s_add", i - 2)
                    pe.matmul(ps[:, i % 2, :], s_hT[:, i * P:(i + 1) * P], logit_w, start=True, stop=True)\
                        .then_inc(S("s_logits"), 1)

                pe.wait_ge(S("s_staged"), g * 2 + 2)
                logits(0)
                for i in range(4):
                    if i < 3:
                        logits(i + 1)
                    on_tile(pe, g, "s_sw", i)
                    pe.matmul(ps[:, 2, :], s_h[:, i, :], s_sw[:, i % 2, :], start=False, stop=False,
                              skip_group_check=True).then_inc(S("s_A"), 1)
                    on_tile(pe, g, "s_swT", i - 2)
                    for k in range(4):
                        mm = pe.transpose(ps[:, 3 + i % 2, k * P:(k + 1) * P], s_sw[:, i % 2, k * P:(k + 1) * P],
                                          ident[:, :])
                    mm.then_inc(S("s_turned"), 1)
            pe.wait_ge(S("s_acc"), NT + 2)
            pe.matmul(ps[:, 5, :], ones[:, :], s_acc, start=True, stop=True).then_inc(S("s_norm"), 1)
            pe.wait_ge(S("s_AT"), 1)
            for k in range(4):
                mm = pe.matmul(ps[:, 6, k * P:(k + 1) * P], wfx_T[:, k * P:(k + 1) * P], A_T[:, k * P:(k + 1) * P],
                               start=True, stop=True)
            mm.then_inc(S("s_st"), 1)
            pe.wait_ge(S("s_stT"), 8)
            pe.wait_ge(S("s_swT"), NT + 2)
            for k in range(4):
                mm = pe.matmul(ps[0:SG, 1, 0:2 * SH], st_T[:, k, :], hy_in[:, k, SI * 2 + 2 * NS:HYP],
                               start=(k == 0), stop=(k == 3))
            mm.then_inc(S("y_dt_in"), 1)
            for q, w in HPARTS:
                c0 = SI + q * P if q < 4 else 2 * SI + (q - 4) * NS
                for k in range(4):
                    mm = pe.matmul(ps[0:w, 3, q * SG:(q + 1) * SG], hy_in[:, k, c0:c0 + w], st_T[:, k, :],
                                   start=(k == 0), stop=(k == 3))
            mm.then_inc(S("y_conv_in"), 1)
            for k in range(4):
                mm = pe.matmul(ps[0:SG, 0, :], st_T[:, k, :], hy_in[:, k, 0:SI], start=(k == 0), stop=(k == 3))
            mm.then_inc(S("y_z_in"), 1)
            pe.wait_ge(S("y_tdA"), after_mamba("y_tdA", 2))
            pe.wait_ge(S("s_loaded"), S_LOADED)
            pe.matmul(ps[0:SG, 4, :], after[0:SG, 0:SG], hy_tdA[:, 0, :], start=True, stop=True)\
                .then_inc(S("y_spans"), 1)
            pe.matmul(ps[0:SG, 5, :], before[:, :], hy_tdA[:, 1, :], start=True, stop=True).then_inc(S("y_spans"), 1)
            pe.wait_ge(S("y_conv"), after_mamba("y_conv", 2))
            pe.matmul(ps[0:SG, 2, 0:SG], hc[0:NS, 4, :], hc[0:NS, 5, :], start=True, stop=True)
            for k in range(4):
                mm = pe.matmul(ps[0:SG, 2, SG:SG + SH], hc[:, k, :], hy_fcD[:, k, :], start=(k == 0), stop=(k == 3))
            mm.then_inc(S("y_cb"), 1)
            for k in range(4):
                mm = pe.transpose(ps[0:SG, 6, k * P:(k + 1) * P], hc[:, k, :], ident[:, :])
            mm.then_inc(S("y_turned"), 1)
            pe.wait_ge(S("y_mix"), after_mamba("y_mix", 2))
            pe.wait_ge(S("y_rows"), after_mamba("y_rows", 1))
            for h in range(SH):
                mm = pe.matmul(ps[0:SG, 7, h * SG:(h + 1) * SG], hy_mix[:, h * SG:(h + 1) * SG],
                               hx_rows[:, h * SG:(h + 1) * SG], start=True, stop=True)
            mm.then_inc(S("y_y"), 1)
            pe.wait_ge(S("y_normed"), after_mamba("y_normed", 1))
            for k in range(4):
                mm = pe.transpose(ps[:, 1, k * SG:(k + 1) * SG], hy_a[:, k * P:(k + 1) * P], ident[0:SG, 0:SG])
            mm.then_inc(S("y_gT"), 1)
            pe.wait_ge(S("y_gT_w"), after_mamba("y_gT_w", 4))
            for c in range(4):
                for k in range(4):
                    mm = pe.matmul(ps[:, 3, c * SG:(c + 1) * SG], hy_out[:, k, c * P:(c + 1) * P], yg_T[:, k, :],
                                   start=(k == 0), stop=(k == 3))
            mm.then_inc(S("y_o"), 1)
            pe.wait_ge(S("y_block"), after_mamba("y_block", 3))
            for c in range(4):
                mm = pe.matmul(ps[:, 2, c * P:(c + 1) * P], block_o[:, c, :], wo_T[:, c, :], start=True, stop=True)
            mm.then_inc(S("y_q"), 1)
            pe.wait_ge(S("y_slice_w"), after_mamba("y_slice_w", 1))
            for c in range(NG):
                for k in range(4):
                    mm = pe.matmul(ps[:, 4 + c, :], slice_w[:, k, :], sw_T[:, k, c * 512:(c + 1) * 512],
                                   start=(k == 0), stop=(k == 3))
                mm.then_inc(S("s_mixed"), 1)
            for c in range(NG):
                pe.wait_ge(S("s_out_T"), c + 1)
                for i in range(4):
                    mm = pe.transpose(ps[:, c, i * P:(i + 1) * P], s_out_T[:, c, i * P:(i + 1) * P], ident[:, :])
                mm.then_inc(S("s_out_turned"), 1)

        def slice_scalar(act, n):
            with act.Fori(0, NG) as g:
                def copy_out(i):
                    on_tile(act, g, "s_turned", i)
                    act.copy(sw_T[:, :, bass.ds(g * 512 + i * P, P)],
                             ps[:, 3 + i % 2, :].rearrange("p (k n) -> p k n", k=4)).then_inc(S("s_swT"), 1)

                for i in range(4):
                    on_tile(act, g, "s_sub", i)
                    on_tile(act, g, "s_sw", i - 2)
                    act.activation(s_exp[:, i % 2, :], s_logit[:, i % 2, :], ACT.Exp).then_inc(S("s_exped"), 1)
                    if i >= 1:
                        copy_out(i - 1)
                copy_out(3)
            act.wait_ge(S("y_dt_abs"), after_mamba("y_dt_abs", 1))
            act.activation(hy_dt[:, 2, :], hy_dt[:, 1, :], ACT.Exp, scale=-1.0).then_inc(S("y_exp"), 1)
            act.wait_ge(S("y_A_min"), after_mamba("y_A_min", 1))
            act.activation(hy_small[0:SG, 1, :], hy_small[0:SG, 1, :], ACT.Exp).then_inc(S("y_exp"), 1)
            act.wait_ge(S("y_exp"), after_mamba("y_exp", 2))
            act.activation(hy_dt[:, 3, :], hy_dt[:, 2, :], ACT.Ln, bias=1.0).then_inc(S("y_ln"), 1)
            act.wait_ge(S("y_conv_in"), after_mamba("y_conv_in", 1))
            act.wait_ge(S("y_clear"), after_mamba("y_clear", 2))
            act.copy(hc_raw[:, 0:4, 2:66], ps[:, 3, 0:256].rearrange("p (q l) -> p q l", q=4)).then_inc(S("y_raw"), 1)
            act.copy(hc_raw[0:NS, 4:6, 2:66], ps[0:NS, 3, 256:384].rearrange("p (q l) -> p q l", q=2))\
                .then_inc(S("y_raw"), 1)
            act.wait_ge(S("y_tap"), after_mamba("y_tap", 18))
            act.activation(hc_tanh[:, 0:4, :], hc[:, 0:4, :], ACT.Tanh).then_inc(S("y_tanh"), 1)
            act.activation(hc_tanh[0:NS, 4:6, :], hc[0:NS, 4:6, :], ACT.Tanh).then_inc(S("y_tanh"), 1)
            act.wait_ge(S("y_z_in"), after_mamba("y_z_in", 1))
            act.activation(hz, ps[0:SG, 0, :], ACT.Tanh, scale=0.5).then_inc(S("y_z_tanh"), 1)
            for s in range(2):
                act.wait_ge(S("y_spans"), after_mamba("y_spans", s + 1))
                act.activation(hy_dec[:, s, :], ps[0:SG, 4 + s, :], ACT.Exp).then_inc(S("y_dec"), 1)
            act.wait_ge(S("y_turned"), after_mamba("y_turned", 1))
            act.copy(hx_rows, ps[0:SG, 6, :]).then_inc(S("y_rows"), 1)
            act.wait_ge(S("y_gated"), after_mamba("y_gated", 1))
            act.activation(hy_b, hy_a, ACT.Square, scale=0.5, accum_out=hy_ss[:, 0:1]).then_inc(S("y_ss"), 1)
            act.wait_ge(S("y_ss"), after_mamba("y_ss", 1))
            act.activation(hy_ss[:, 0:1], hy_ss[:, 0:1], ACT.Sqrt, scale=1.0 / SI, bias=EPS).then_inc(S("y_rms"), 1)
            act.wait_ge(S("y_q"), after_mamba("y_q", 1))
            act.copy(slice_w.rearrange("p k d -> p (k d)"), ps[:, 2, :]).then_inc(S("y_slice_w"), 1)
            for c in range(NG):
                act.wait_ge(S("s_mixed"), c + 1)
                act.activation(s_out_T[:, c, :], ps[:, 4 + c, :], ACT.Identity, bias=ob_T).then_inc(S("s_out_T"), 1)

        def slice_pool(pool, n):
            with pool.Fori(0, NG) as g:
                pool.wait_ge(S("h_rows"), g * 4 + (16 * n + 4))
                pool.tensor_copy(h_all[:, bass.ds(g * 4, 4), :], h_rows[:, :, :]).then_inc(S("h_kept"), 1)
            hT_ready(pool, n)
            with pool.Fori(0, NG) as g:
                on_tile(pool, g, "s_logits", -1)
                pool.tensor_copy(s_hT, hT[:, bass.ts(g, 512)]).then_inc(S("s_staged"), 1)
                on_tile(pool, g, "s_A", -1)
                pool.wait_ge(S("h_kept"), NG + 1)
                pool.tensor_copy(s_h, h_all[:, bass.ds(g * 4, 4), :]).then_inc(S("s_staged"), 1)
                for i in range(4):
                    b = i % 2
                    on_tile(pool, g, "s_rec", i)
                    on_tile(pool, g, "s_turned", i - 2)
                    on_tile(pool, g, "s_acc", i - 2)
                    pool.tensor_tensor(by_head(s_sw[:, b, :]), by_head(s_exp[:, b, :]), heads8(s_rec[:, b, :], P, SG),
                                       ALU.mult).then_inc(S("s_sw"), 1)
                    on_tile(pool, g, "s_sw", i)
                    on_tile(pool, g, "s_acc", i - 1)
                    pool.tensor_tensor(s_acc, s_acc, s_sw[:, b, :], ALU.add).then_inc(S("s_acc"), 1)

        def slice_vector(dve, n):
            dve.memset(s_acc, 0.0).then_inc(S("s_zeroed"), 1)
            dve.memset(ones[:, :], 1.0).then_inc(S("s_zeroed"), 1)
            dve.memset(block_o[:, :, :], 0.0).then_inc(S("y_block"), 1)
            dve.memset(hc_raw[:, :, :], 0.0).then_inc(S("y_clear"), 1)
            dve.memset(hy_mix, 0.0).then_inc(S("y_clear"), 1)
            dve.wait_ge(S("s_loaded"), S_LOADED)
            dve.wait_ge(S("s_zeroed"), 2)
            dve.tensor_scalar(temp_b, temp_b, 1e-6, None, ALU.max).then_inc(S("s_temp"), 1)
            dve.wait_ge(S("s_temp"), 1)
            dve.reciprocal(temp_b, temp_b).then_inc(S("s_temp"), 1)
            dve.wait_ge(S("s_weights"), 1)
            dve.wait_ge(S("s_temp"), 2)
            dve.tensor_tensor(by_head(logit_w), by_head(ps[:, 0, :]), heads8(temp_b, P, SG), ALU.mult)\
                .then_inc(S("s_logit_w"), 1)
            dve.tensor_tensor(by_head(logit_c), by_head(ps[:, 1, :]), bs_b.unsqueeze(1).to_broadcast([P, SH, SG]),
                              ALU.add).then_inc(S("s_bias_sum"), 1)
            dve.wait_ge(S("s_bias_sum"), 1)
            dve.tensor_tensor(by_head(logit_c), by_head(logit_c), heads8(temp_b, P, SG), ALU.mult)\
                .then_inc(S("s_logit_w"), 1)
            dve.tensor_scalar(hy_cw, hy_cw, 0.5, None, ALU.mult).then_inc(S("y_halved"), 1)
            dve.tensor_scalar(hy_cb, hy_cb, 0.5, None, ALU.mult).then_inc(S("y_halved"), 1)
            dve.tensor_scalar(hy_small[:, 1, :], hy_small[:, 1, :], 88.0, None, ALU.min).then_inc(S("y_A_min"), 1)
            dve.wait_ge(S("s_logit_w"), 2)
            with dve.Fori(0, NG) as g:
                def sums(i):
                    b = i % 2
                    on_tile(dve, g, "s_exped", i)
                    on_tile(dve, g, "s_rec", i - 2)
                    dve.tensor_reduce(s_sum[:, b, :], by_head(s_exp[:, b, :]), AX.X, ALU.add).then_inc(S("s_summed"), 1)
                    on_tile(dve, g, "s_summed", i)
                    on_tile(dve, g, "s_sw", i - 2)
                    dve.reciprocal(s_rec[:, b, :], s_sum[:, b, :]).then_inc(S("s_rec"), 1)

                for i in range(4):
                    b = i % 2
                    on_tile(dve, g, "s_logits", i)
                    on_tile(dve, g, "s_exped", i - 2)
                    dve.tensor_tensor(s_logit[:, b, :], ps[:, b, :], logit_c, ALU.add).then_inc(S("s_add"), 1)
                    on_tile(dve, g, "s_add", i)
                    on_tile(dve, g, "s_sub", i - 2)
                    dve.tensor_reduce(s_max[:, b, :], by_head(s_logit[:, b, :]), AX.X, ALU.max)\
                        .then_inc(S("s_maxed"), 1)
                    on_tile(dve, g, "s_maxed", i)
                    dve.tensor_tensor(by_head(s_logit[:, b, :]), by_head(s_logit[:, b, :]),
                                      heads8(s_max[:, b, :], P, SG), ALU.subtract).then_inc(S("s_sub"), 1)
                    if i >= 1:
                        sums(i - 1)
                sums(3)
            dve.wait_ge(S("s_norm"), 1)
            dve.tensor_scalar(sn_rec, ps[:, 5, :], 1e-5, None, ALU.add).then_inc(S("s_q"), 1)
            dve.wait_ge(S("s_q"), 1)
            dve.reciprocal(sn_rec, sn_rec).then_inc(S("s_q"), 1)
            dve.wait_ge(S("s_q"), 2)
            dve.tensor_tensor(A_T, ps[:, 2, :], sn_rec, ALU.mult).then_inc(S("s_AT"), 1)
            dve.tensor_tensor(q_rows, ps[:, 5, :], sn_rec, ALU.mult).then_inc(S("s_q"), 1)
            dve.wait_ge(S("s_st"), 1)
            dve.wait_ge(S("s_q"), 3)
            for k in range(4):
                for s in range(2):
                    r = slice(s * 64, s * 64 + 64)
                    c0 = k * P + s * SG
                    dve.scalar_tensor_tensor(st_T[r, k, :], q_rows[r, c0:c0 + SG], bfx_T[r, k:k + 1],
                                             ps[r, 6, c0:c0 + SG], ALU.mult, ALU.add).then_inc(S("s_stT"), 1)
            dve.wait_ge(S("y_dt_in"), after_mamba("y_dt_in", 1))
            two = lambda ap: ap.rearrange("p (s h) -> p s h", s=2)
            dve.tensor_tensor(two(hy_dt[:, 0, :]), two(ps[0:SG, 1, 0:2 * SH]),
                              hy_small[0:SG, 0, :].unsqueeze(1).to_broadcast([SG, 2, SH]), ALU.add)\
                .then_inc(S("y_dt"), 1)
            dve.wait_ge(S("y_dt"), after_mamba("y_dt", 1))
            dve.scalar_tensor_tensor(hy_dt[:, 1, :], hy_dt[:, 0, :], -1.0, hy_dt[:, 0, :], ALU.mult, ALU.max)\
                .then_inc(S("y_dt_abs"), 1)
            dve.wait_ge(S("y_ln"), after_mamba("y_ln", 1))
            dve.scalar_tensor_tensor(hy_dt[:, 4, :], hy_dt[:, 0, :], 0.0, hy_dt[:, 3, :], ALU.max, ALU.add)\
                .then_inc(S("y_dt"), 1)
            dve.wait_ge(S("y_dt"), after_mamba("y_dt", 2))
            dve.wait_ge(S("y_exp"), after_mamba("y_exp", 2))
            dve.scalar_tensor_tensor(two(hy_dt[:, 5, :]), two(hy_dt[:, 4, :]), -1.0,
                                     hy_small[0:SG, 1, :].unsqueeze(1).to_broadcast([SG, 2, SH]),
                                     ALU.mult, ALU.mult).then_inc(S("y_dt"), 1)
            dve.wait_ge(S("y_dt"), after_mamba("y_dt", 3))
            dve.tensor_scalar(hy_dt[:, 5, :], hy_dt[:, 5, :], -1.0e4, None, ALU.max).then_inc(S("y_dt"), 1)
            dve.wait_ge(S("y_dt"), after_mamba("y_dt", 4))
            for s, m in enumerate((tri[0:SG, 0:SG], low[:, :])):
                dve.tensor_tensor(by_head(hy_tdA[:, s, :]), m.unsqueeze(1).to_broadcast([SG, SH, SG]),
                                  heads8(hy_dt[:, 5, s * SH:(s + 1) * SH], SG, SG), ALU.mult).then_inc(S("y_tdA"), 1)
            dve.wait_ge(S("y_clear"), after_mamba("y_clear", 2))
            dve.wait_ge(S("y_halved"), after_mamba("y_halved", 2))
            for k in (2, 0, 1):
                at = {2: 0, 0: 6, 1: 12}[k]
                for q, w in HPARTS:
                    if k == 2:
                        dve.wait_ge(S("y_raw"), after_mamba("y_raw", 1 if q < 4 else 2))
                        dve.tensor_scalar(hc[0:w, q, :], hc_raw[0:w, q, 2:66], hy_cw[0:w, q, 2:3], hy_cb[0:w, q:q + 1],
                                          ALU.mult, ALU.add).then_inc(S("y_tap"), 1)
                    else:
                        dve.wait_ge(S("y_tap"), after_mamba("y_tap", at + q - 5))
                        dve.scalar_tensor_tensor(hc[0:w, q, :], hc_raw[0:w, q, k:k + 64], hy_cw[0:w, q, k:k + 1],
                                                 hc[0:w, q, :], ALU.mult, ALU.add).then_inc(S("y_tap"), 1)
            dve.wait_ge(S("y_tanh"), after_mamba("y_tanh", 1))
            dve.scalar_tensor_tensor(hc[:, 0:4, :], hc_tanh[:, 0:4, :], 1.0, hc[:, 0:4, :], ALU.add, ALU.mult)\
                .then_inc(S("y_conv"), 1)
            dve.wait_ge(S("y_tanh"), after_mamba("y_tanh", 2))
            dve.scalar_tensor_tensor(hc[0:NS, 4:6, :], hc_tanh[0:NS, 4:6, :], 1.0, hc[0:NS, 4:6, :],
                                     ALU.add, ALU.mult).then_inc(S("y_conv"), 1)
            dve.wait_ge(S("y_z_tanh"), after_mamba("y_z_tanh", 1))
            dve.scalar_tensor_tensor(hz, hz, 1.0, ps[0:SG, 0, :], ALU.add, ALU.mult).then_inc(S("y_z"), 1)
            dve.wait_ge(S("y_cb"), after_mamba("y_cb", 1))
            for s, m in enumerate((tri[0:SG, 0:SG], low[:, :])):
                dve.tensor_tensor(hy_cbm[:, s, :], ps[0:SG, 2, 0:SG], m, ALU.mult).then_inc(S("y_cbm"), 1)
            dve.tensor_tensor(hy_fD, ps[0:SG, 2, SG:SG + SH], hy_small[0:SG, 2, :], ALU.add).then_inc(S("y_fD"), 1)
            dve.wait_ge(S("y_cbm"), after_mamba("y_cbm", 2))
            for s in range(2):
                d3 = by_head(hy_dec[:, s, :])
                dve.wait_ge(S("y_dec"), after_mamba("y_dec", s + 1))
                dve.tensor_tensor(d3, d3, hy_cbm[:, s, :].unsqueeze(1).to_broadcast([SG, SH, SG]), ALU.mult)\
                    .then_inc(S("y_dec_cb"), 1)
            m3 = by_head(hy_mix)
            dve.wait_ge(S("y_dec_cb"), after_mamba("y_dec_cb", 1))
            dve.tensor_tensor(m3[:, :, 1:SG], by_head(hy_dec[:, 0, :])[:, :, 0:SG - 1],
                              heads8(hy_dt[:, 4, 0:SH], SG, SG - 1), ALU.mult).then_inc(S("y_mix"), 1)
            dve.wait_ge(S("y_dec_cb"), after_mamba("y_dec_cb", 2))
            d1 = by_head(hy_dec[:, 1, :])
            dve.tensor_tensor(d1, d1, heads8(hy_dt[:, 4, SH:2 * SH], SG, SG), ALU.mult).then_inc(S("y_dec_cb"), 1)
            dve.wait_ge(S("y_dec_cb"), after_mamba("y_dec_cb", 3))
            dve.wait_ge(S("y_mix"), after_mamba("y_mix", 1))
            dve.tensor_tensor(m3[:, :, 0:SG - 1], m3[:, :, 0:SG - 1], d1[:, :, 1:SG], ALU.add)\
                .then_inc(S("y_mix"), 1)
            dve.wait_ge(S("y_rows"), after_mamba("y_rows", 1))
            dve.wait_ge(S("y_fD"), after_mamba("y_fD", 1))
            dve.tensor_tensor(by_head(hy_b), by_head(hx_rows), heads8(hy_fD, SG, SG), ALU.mult).then_inc(S("y_t"), 1)
            dve.wait_ge(S("y_y"), after_mamba("y_y", 1))
            dve.wait_ge(S("y_t"), after_mamba("y_t", 1))
            dve.tensor_tensor(hy_b, hy_b, ps[0:SG, 7, :], ALU.add).then_inc(S("y_t"), 1)
            dve.wait_ge(S("y_t"), after_mamba("y_t", 2))
            dve.wait_ge(S("y_z"), after_mamba("y_z", 1))
            dve.tensor_tensor(hy_a, hy_b, hz, ALU.mult).then_inc(S("y_gated"), 1)
            dve.wait_ge(S("y_rms"), after_mamba("y_rms", 1))
            dve.reciprocal(hy_ss[:, 1:2], hy_ss[:, 0:1]).then_inc(S("y_t"), 1)
            dve.wait_ge(S("y_t"), after_mamba("y_t", 3))
            dve.wait_ge(S("y_gated"), after_mamba("y_gated", 1))
            dve.tensor_scalar(hy_a, hy_a, hy_ss[:, 1:2], 0.5, ALU.mult, ALU.mult).then_inc(S("y_normed"), 1)
            dve.wait_ge(S("y_gT"), after_mamba("y_gT", 1))
            for k in range(4):
                dve.tensor_scalar(yg_T[:, k, :], ps[:, 1, k * SG:(k + 1) * SG], hy_nw[:, k:k + 1], None, ALU.mult)\
                    .then_inc(S("y_gT_w"), 1)
            dve.wait_ge(S("y_o"), after_mamba("y_o", 1))
            dve.wait_ge(S("y_block"), after_mamba("y_block", 1))
            for s in range(2):
                r = slice(s * 64, s * 64 + 64)
                dve.tensor_copy(block_o[r, :, s * SG:(s + 1) * SG],
                                ps[r, 3, 0:256].rearrange("p (k g) -> p k g", k=4)).then_inc(S("y_block"), 1)
            for c in range(NG):
                dve.wait_ge(S("s_out_turned"), c + 1)
                dve.tensor_tensor(x[:, 4 * c:4 * c + 4, :], x[:, 4 * c:4 * c + 4, :],
                                  ps[:, c, :].rearrange("p (i d) -> p i d", d=D), ALU.add)\
                    .then_inc(S("x_updates"), 1)

        def slice_sync(sp, before_x):
            sp.wait_ge(S("x_updates"), before_x)
            for dst, name in ((wx_h, "L3_wx"), (ws_T, "L3_wsT"), (bx_T, "L3_bxT"), (wfx_T, "L3_wfxT"),
                              (bfx_T, "L3_bfxT"), (hy_cw, "L3_cw"), (hy_cb, "L3_cb"), (hy_fcD, "L3_fcDT"),
                              (hy_nw, "L3_nwT"), (before[:, :], "before"), (low[:, :], "low"), (ob_T, "L3_obT"),
                              (wo_T, "L3_woT"), (hy_out, "L3_hyoutT"), (hy_in, "L3_hyinT")):
                sp.dma_start(dst, t[name]).then_inc(S("s_loaded"), 16)
            for dst, name in ((bs_b, "L3_ffn_b_slice"), (temp_b, "L3_temp"), (hy_small[:, 0, :], "L3_ffn_hy_dt_bias"),
                              (hy_small[:, 1, :], "L3_ffn_hy_A_log"), (hy_small[:, 2, :], "L3_ffn_hy_D")):
                sp.dma_start(dst, t[name].partition_broadcast(P)).then_inc(S("s_loaded"), 16)

        NORMS = {"gnn0": 0, "moe0": 1, "gnn1": 2, "mamba": 3, "sage": 4, "moe2": 5, "gnn3": 6, "slice": 7}
        UPDATES = {"gnn0": 3, "moe0": 4, "gnn1": 3, "mamba": NT, "sage": NT, "moe2": 4, "gnn3": 6, "slice": 4}
        need = {}
        total = 16
        for s in STAGES:
            need[s] = total
            if s == "gnn3":
                pass_end["L3"] = total + 3
            total += UPDATES[s]
        x_total = total

        CREDITS = {"h_turned": 4, "hT": 1, "weights": 2, "weights_used": 2, "act_h": RING, "h_lo": RING,
                   "down": RING}
        if "mamba" in STAGES:
            CREDITS |= {name: 2 for name in CHUNKS}
        if "sage" in STAGES:
            CREDITS |= {"g_x": 2}
        if "slice" in STAGES:
            CREDITS |= {name: 2 for name in TILES} | {"h_kept": 1}

        @block.gpsimd
        def _(pool):
            for name, n in CREDITS.items():
                pool.sem_inc(S(name), n)
            for s in STAGES:
                if s[:3] == "moe":
                    moe_pool(pool, "L" + s[3], NORMS[s])
                if s == "mamba":
                    add_to_rows(pool, NORMS[s], b_lin, "m_x_bias", "bias_loaded", 1)
                    mamba_pool(pool)
                if s == "slice":
                    slice_pool(pool, NORMS[s])
                if s == "sage":
                    add_to_rows(pool, NORMS[s], sage_b, "g_x_bias", "sage_loaded", 2)

        @block.sync
        def _(sp):
            sp.dma_start(x[:, :, :], t["x"].rearrange("(i p) d -> p i d", p=P)).then_inc(S("x_updates"), 16)
            sp.dma_start(ident[:, :], t["ident"]).then_inc(S("gat_loaded"), 16)
            for l, L in enumerate(("L0", "L1", "L3")):
                sp.dma_start(gat_wT[:, l, :], t[f"{L}_gnn_WT"]).then_inc(S("gat_loaded"), 16)
                sp.dma_start(gat_a[:, l, :], t[f"{L}_gnn_a"]).then_inc(S("gat_loaded"), 16)
            sp.dma_start(value_w[:, 0, 0:D], t["L0_gnn_W"]).then_inc(S("gat_loaded"), 16)
            sp.dma_start(value_w[:, 1, 0:D], t["L1_gnn_W"]).then_inc(S("gat_loaded"), 16)
            sp.dma_start(value_w[:, 2:4, 0:D], t["L3_gnn_wtrans"].rearrange("(s d) o -> d s o", d=D))\
                .then_inc(S("gat_loaded"), 16)
            if "gnn0" in STAGES:
                adj_rows = t["adjT"].rearrange("(j p) n -> j p n", p=P)
                for b in range(2):
                    sp.dma_start(adj_in[:, b, :], adj_rows[b]).then_inc(S(f"adj_landed{b}"), 16)
            sp.dma_start(first[:, :], t["first"].partition_broadcast(P)).then_inc(S("moe_loaded"), 16)
            for m, L in enumerate(("L0", "L2")):
                sp.dma_start(gate_w[:, m, :], t[f"{L}_ffn_Wg"]).then_inc(S("moe_loaded"), 16)
                sp.dma_start(gate_b[:, m, :], t[f"{L}_ffn_bg"].partition_broadcast(P)).then_inc(S("moe_loaded"), 16)
                sp.dma_start(b1_T[L][:, :], t[f"{L}_ffn_b1"]).then_inc(S("moe_loaded"), 16)
                sp.dma_start(b2[:, m, :], t[f"{L}_ffn_b2"]).then_inc(S("moe_loaded"), 16)
            if "gnn0" in STAGES:
                with sp.Fori(1, NT // 2) as jj:
                    for b in range(2):
                        sp.wait_ge(S("adjT"), jj * 2 + (b - 1))
                        sp.dma_start(adj_in[:, b, :], adj_rows[bass.ds(jj * 2 + b, 1)].rearrange("j p n -> p (j n)"))\
                            .then_inc(S(f"adj_landed{b}"), 16)
            if "mamba" in STAGES:
                for dst, name in ((tri, "tri"), (after, "after"), (win_x, "L1_win_x"), (win_zd, "L1_win_zd"),
                                  (conv_w, "L1_conv_w"), (conv_b, "L1_conv_b"), (wout_T, "L1_wout_T"),
                                  (w_lin, "L1_W_lin"), (norm_w, "L1_norm_w")):
                    sp.dma_start(dst[tuple([slice(None)] * len(dst.shape))], t[name]).then_inc(S("mamba_loaded"), 16)
                sp.dma_start(small_in[:, :, :], t["L1_small"].partition_broadcast(P)).then_inc(S("mamba_loaded"), 16)
                sp.dma_start(b_lin[:, :], t["L1_b_lin"].partition_broadcast(P)).then_inc(S("bias_loaded"), 16)
            if "sage" in STAGES:
                sp.dma_start(sage_w[:, :], t["L2_gnn_w"]).then_inc(S("sage_loaded"), 16)
                sp.dma_start(sage_b[:, :], t["L2_gnn_bias"].partition_broadcast(P)).then_inc(S("sage_loaded"), 16)
            for s in STAGES:
                if s == "moe0":
                    moe_sync(sp, "L0", 1)
                if s == "moe2":
                    moe_sync(sp, "L2", 5)
                if s == "slice":
                    slice_sync(sp, need[s])
            sp.wait_ge(S("x_updates"), x_total)
            sp.wait_ge(S("moe_loaded"), 16 * 9)
            sp.dma_start(outs[0].rearrange("(i p) d -> p i d", p=P), x[:, :, :]).then_inc(S("stored"), 16)
            sp.wait_ge(S("stored"), 16)

        @block.vector
        def _(dve):
            gat_setup_vector(dve)
            for s in STAGES:
                norm_vector(dve, NORMS[s], need[s])
                if s[:3] == "gnn":
                    gat_vector(dve, "L" + s[3], NORMS[s])
                if s[:3] == "moe":
                    moe_vector(dve, "L" + s[3], NORMS[s])
                if s == "mamba":
                    mamba_vector(dve, NORMS[s])
                if s == "slice":
                    slice_vector(dve, NORMS[s])
                if s == "sage":
                    sage_vector(dve, NORMS[s])

        @block.scalar
        def _(act):
            for s in STAGES:
                norm_scalar(act, NORMS[s])
                if s[:3] == "gnn":
                    gat_scalar(act, "L" + s[3], NORMS[s])
                if s[:3] == "moe":
                    moe_scalar(act, "L" + s[3], NORMS[s])
                if s == "mamba":
                    mamba_scalar(act, NORMS[s])
                if s == "slice":
                    slice_scalar(act, NORMS[s])

        @block.tensor
        def _(pe):
            gat_setup_tensor(pe)
            for s in STAGES:
                norm_tensor(pe, NORMS[s])
                if s[:3] == "gnn":
                    gat_tensor(pe, "L" + s[3], NORMS[s])
                if s[:3] == "moe":
                    moe_tensor(pe, "L" + s[3], NORMS[s])
                if s == "mamba":
                    mamba_tensor(pe, NORMS[s])
                if s == "slice":
                    slice_tensor(pe, NORMS[s])
                if s == "sage":
                    sage_tensor(pe, NORMS[s])


def kernel(**inputs):
    import numpy as _np
    import concourse.bacc as _bacc
    from concourse import mybir as _mybir
    from concourse.bass_utils import run_bass_kernel_spmd as _run

    a = {k: _np.asarray(v) for k, v in inputs.items()}
    c = _np.ascontiguousarray
    arrays = {
        "x": a["x"], "adjT": c(a["adj"].T),
        "ident": _np.eye(P, dtype=_np.float32), "first": _np.arange(E, 0, -1).astype(_np.float32),
    }
    for L in ("L0", "L1", "L3"):
        arrays[f"{L}_gnn_WT"] = c(a[f"{L}_gnn_W"].T)
        arrays[f"{L}_gnn_a"] = c(a[f"{L}_gnn_a"].reshape(2, D).T)
    arrays["L0_gnn_W"], arrays["L1_gnn_W"] = a["L0_gnn_W"], a["L1_gnn_W"]
    arrays["L3_gnn_wtrans"] = a["L3_gnn_wtrans"]
    arrays["L0_ffn_Wg"], arrays["L2_ffn_Wg"] = a["L0_ffn_Wg"], c(a["L2_ffn_Wg"].T)
    arrays["L0_ffn_W1"], arrays["L2_ffn_W1"] = a["L0_ffn_W1"], c(a["L2_ffn_W1"].transpose(0, 2, 1))
    arrays["L0_ffn_W2"], arrays["L2_ffn_W2"] = a["L0_ffn_W2"], c(a["L2_ffn_W2"].transpose(0, 2, 1))
    for L in ("L0", "L2"):
        arrays[f"{L}_ffn_bg"], arrays[f"{L}_ffn_b2"] = a[f"{L}_ffn_bg"], a[f"{L}_ffn_b2"]
        arrays[f"{L}_ffn_b1"] = c(a[f"{L}_ffn_b1"].reshape(E * HC[L], P).T)
    tri = _np.triu(_np.ones((P, P), _np.float32))
    arrays["tri"], arrays["after"] = tri, c(1 - tri.T) * 0 + _np.tril(_np.ones((P, P), _np.float32), -1)
    win = a["L1_ffn_W_in"]
    arrays["L1_win_x"] = c(win[:, DI:DI + 384])
    arrays["L1_win_zd"] = c(_np.concatenate([win[:, :DI], win[:, DI + 384:]], axis=1))
    cw, cb = _np.zeros((P, 4, 4), _np.float32), _np.zeros((P, 4), _np.float32)
    for q, c0, w in ((0, 0, P), (1, P, P), (2, 2 * P, NS), (3, 2 * P + NS, NS)):
        cw[:w, q], cb[:w, q] = a["L1_ffn_conv_w"][c0:c0 + w], a["L1_ffn_conv_b"][c0:c0 + w]
    arrays["L1_conv_w"], arrays["L1_conv_b"] = cw, cb
    arrays["L1_wout_T"] = c(a["L1_ffn_W_out"].T.reshape(P, 2, P))
    arrays["L1_W_lin"], arrays["L1_b_lin"] = a["L1_ffn_W_lin"], a["L1_ffn_b_lin"]
    arrays["L1_norm_w"] = c(a["L1_ffn_norm_w"].reshape(2, P).T)
    arrays["L1_small"] = _np.stack([a["L1_ffn_dt_bias"], a["L1_ffn_A_log"], a["L1_ffn_D"]])
    arrays["L2_gnn_w"] = c(a["L2_gnn_weight"].reshape(2, D, D).transpose(1, 0, 2).reshape(D, 2 * D))
    arrays["L2_gnn_bias"] = a["L2_gnn_bias"]
    arrays["before"] = c(_np.triu(_np.ones((SG, SG), _np.float32), 1))
    arrays["low"] = c(_np.tril(_np.ones((SG, SG), _np.float32)))
    arrays["L3_wx"] = c(a["L3_ffn_W_x"].reshape(SH, NS, D).transpose(1, 0, 2))
    arrays["L3_wsT"] = c(a["L3_ffn_W_slice"].T)
    arrays["L3_bxT"] = c(a["L3_ffn_b_x"].reshape(SH, NS).T)
    arrays["L3_wfxT"] = c(a["L3_ffn_W_fx"].T)
    arrays["L3_bfxT"] = c(a["L3_ffn_b_fx"].reshape(4, P).T)
    hw, hb = _np.zeros((P, 6, 3), _np.float32), _np.zeros((P, 6), _np.float32)
    for q in range(6):
        c0, w = (q * P, P) if q < 4 else (SI + (q - 4) * NS, NS)
        hw[:w, q], hb[:w, q] = a["L3_ffn_hy_conv_w"][c0:c0 + w], a["L3_ffn_hy_conv_b"][c0:c0 + w]
    arrays["L3_cw"], arrays["L3_cb"] = hw, hb

    def chunks(m):
        return c(m.reshape(4, P, -1).transpose(1, 0, 2))

    arrays["L3_fcDT"] = chunks(a["L3_ffn_hy_fcD_w"].T)
    arrays["L3_nwT"] = c(a["L3_ffn_hy_norm_w"].reshape(4, P).T)
    arrays["L3_hyinT"] = chunks(a["L3_ffn_hy_in_w"].T)
    arrays["L3_hyoutT"] = chunks(a["L3_ffn_hy_out_w"].T)
    arrays["L3_woT"] = chunks(a["L3_ffn_out_w"].T)
    arrays["L3_obT"] = c(a["L3_ffn_out_b"].reshape(P, 1))
    arrays["L3_temp"] = a["L3_ffn_temperature"].reshape(SH)
    for name in ("b_slice", "hy_dt_bias", "hy_A_log", "hy_D"):
        arrays[f"L3_ffn_{name}"] = a[f"L3_ffn_{name}"]
    nc = _bacc.Bacc("TRN2", target_bir_lowering=False, num_devices=1)
    t, ins = {}, {}
    for name, arr in arrays.items():
        ins[f"in_{name}"] = arr
        t[name] = nc.dram_tensor(f"in_{name}", arr.shape, _mybir.dt.from_np(arr.dtype), kind="ExternalInput").ap()
    out_name = OUT
    outs = [nc.dram_tensor(out_name, (N, D), F32, kind="ExternalOutput").ap()]
    program(nc, t, outs)
    r = _run(nc, [ins], core_ids=[0])
    return r.results[0][out_name]


OUT = "out"
```

```python
from contextlib import ExitStack

import numpy as np
import concourse.bass as bass
from concourse import mybir

F32 = mybir.dt.float32
BF16 = mybir.dt.bfloat16
F32R = mybir.dt.float32r
I32 = mybir.dt.int32
ALU = mybir.AluOpType
ACT = mybir.ActivationFunctionType
AX = mybir.AxisListType

P = 128
N = 2048
D = 128
NT = N // P
NG = N // 512
EPS = 1e-5
SLOPE = 0.2
RISE = 1.0 - SLOPE
CLAMP = 75.0 / RISE
E = 8
HC = {"L0": 2, "L2": 4}
VC = D + 1
TPB = 3
NBK = -(-NT // TPB)
RING = 4
LAG = 4
DI = 256
NH = 4
HD = DI // NH
NS = 64
SH = 8
SG = 64
SI = 512
HYP = 2 * SI + 2 * NS + 2 * SH
STAGES = ["gnn0", "moe0", "gnn1", "mamba", "sage", "moe2", "gnn3", "slice"]


def program(nc, t, outs):
    with ExitStack() as ctx:
        def sb(name, shape, dt=F32):
            return ctx.enter_context(nc.sbuf_tensor(name, shape, dt))

        sems = {}
        reused = {}

        def S(name):
            name = reused.get(name, (name,))[0]
            if name not in sems:
                sems[name] = ctx.enter_context(nc.semaphore(name))
            return sems[name]

        x = sb("x", [P, NT, D])
        hT = sb("hT", [P, N])
        adjT = sb("adjT", [P, NT, N], BF16)
        ps = ctx.enter_context(nc.psum_tensor("ps", [P, 8, 512], F32))

        ident = sb("ident", [P, P])
        zeros = sb("zeros", [P, TPB * VC], BF16)
        stats = sb("stats", [P, NT, 6])
        mean_var = sb("mean_var", [P, NT, 2])
        std = sb("std", [P, NT])
        rstd = sb("rstd", [P, NT])

        gat_wT = sb("gat_wT", [P, 3, D])
        gat_a = sb("gat_a", [P, 3, 2])
        value_w = sb("value_w", [P, 4, VC])
        score_w = sb("score_w", [P, 3, 2, P])
        s2_bound = sb("s2_bound", [P, 2])
        s2_rel = sb("s2_rel", [P, 2, NT])
        K = sb("K", [P, 2, NT])
        F = sb("F", [P, 2, NT])
        rowrec = sb("rowrec", [P, NT])

        with ExitStack() as beneath:
            def under(name, shape, dt=F32R):
                return beneath.enter_context(nc.sbuf_tensor(name, shape, dt))

            under("big_lower", [P, 4 * N], F32)
            h_parts = under("h_parts", [P, 2, RING, 512])
            hT_parts = under("hT_parts", [P, 2, N])
            w_parts = under("w_parts", [P, 2, 2, 2, 512])
        big = sb("big", [P, 8 * N])
        R = big[:, 0:2 * N].rearrange("p (s n) -> p s n", s=2)
        T = big[:, 2 * N:4 * N].rearrange("p (s n) -> p s n", s=2)
        PR = big[:, 4 * N:6 * N].rearrange("p (s n) -> p s n", s=2)
        adj_in = big[:, 6 * N:8 * N].bitcast(I32).rearrange("p (s n) -> p s n", s=2)
        G = sb("G", [P, 2, NT, VC])
        rows_a = T[:, 0, :].rearrange("p (i d) -> p i d", d=D)
        rows_b = T[:, 1, :].rearrange("p (i d) -> p i d", d=D)
        rows_c = R[:, 0, :].rearrange("p (i d) -> p i d", d=D)
        h_rows = big[:, 0:N].rearrange("p (i d) -> p i d", d=D)
        comb_b = big[:, 0:2 * N].rearrange("p (s n) -> p s n", s=2)
        act_h = big[:, 2 * N:3 * N].rearrange("p (r n) -> p r n", r=RING)
        out_T = big[:, 3 * N:4 * N].rearrange("p (c n) -> p c n", c=NG)
        comb8 = big[0:E, 3 * N:4 * N]
        expert_in = sb("expert_in", [P, 2048])
        w1_e = expert_in[:, 0:1024].rearrange("p (s h) -> p s h", s=2)
        w2_e = expert_in[:, 1024:2048].rearrange("p (s k d) -> p s k d", s=2, d=P)
        gate_w = sb("gate_w", [P, 2, E])
        gate_b = sb("gate_b", [P, 2, E])
        first = sb("first", [P, E])
        b1_T = {"L0": sb("b1_T0", [P, E * 2]), "L2": sb("b1_T2", [P, E * 4])}
        b2 = sb("b2", [E, 2, D])
        top = sb("top", [P, 8, NT, E])
        topm = sb("topm", [P, 8, NT])
        comb = sb("comb", [P, E, NT])
        comb_T = sb("comb_T", [P, P])
        comb_dram = {L: nc.dram_tensor(f"comb_{L}", [E, N], F32, kind="Internal").ap() for L in ("L0", "L2")}

        o = [0]

        def part(n, rows=P):
            o[0] += n
            assert o[0] <= 8 * N
            return big[0:rows, o[0] - n:o[0]]

        conv_raw = part(4 * 516).rearrange("p (q n) -> p q n", q=4)
        conv = part(4 * 512).rearrange("p (q n) -> p q n", q=4)
        z_gate = part(NT * DI).rearrange("p (i d) -> p i d", d=DI)
        y_rows = part(NT * D).rearrange("p (i d) -> p i d", d=D)
        xb_rows = part(4 * 320).rearrange("p (i d) -> p i d", d=320)
        cb_masked = part(4 * P).rearrange("p (i l) -> p i l", i=4)
        mixm = part(2 * 512).rearrange("p (b n) -> p b n", b=2)
        x_dt = part(2 * DI).rearrange("p (b n) -> p b n", b=2)
        x_decayed = part(2 * DI).rearrange("p (b n) -> p b n", b=2)
        x_skip = part(2 * DI).rearrange("p (b n) -> p b n", b=2)
        y_gated = part(2 * DI).rearrange("p (b n) -> p b n", b=2)
        y_T = part(2 * DI).rearrange("p (b n) -> p b n", b=2)
        state = part(2 * DI, 64).rearrange("p (b n) -> p b n", b=2)
        Gf = G[:, :, :, :].rearrange("p s i c -> p (s i c)")
        conv_tanh = Gf[:, 0:2048].rearrange("p (q n) -> p q n", q=4)
        tri_dA = Gf[:, 2048:3072].rearrange("p (b n) -> p b n", b=2)
        decay = Gf[:, 3072:4096].rearrange("p (b n) -> p b n", b=2)
        conv_out = expert_in[:, :].rearrange("p (q n) -> p q n", q=4)
        y_a = sb("y_a", [P, DI])
        y_b = sb("y_b", [P, DI])
        z_tanh = sb("z_tanh", [P, 2, DI])
        y_square = sb("y_square", [P, DI])
        tri = sb("tri", [P, P])
        after = sb("after", [P, P])
        ones = sb("ones", [P, P])
        win_x = sb("win_x", [P, 384])
        win_zd = sb("win_zd", [P, DI + NH])
        conv_w = sb("conv_w", [P, 4, 4])
        conv_b = sb("conv_b", [P, 4])
        small_in = sb("small_in", [P, 3, NH])
        wout_T = sb("wout_T", [P, 2, P])
        w_lin = sb("w_lin", [P, P])
        norm_w = sb("norm_w", [P, 2])
        b_lin = sb("b_lin", [P, D])
        w_proj = sb("w_proj", [P, 2, P])
        dts = sb("dts", [P, 6, NT * NH])
        exp_A = sb("exp_A", [P, NH])
        carry = sb("carry", [P, 2, NT * NH])
        sumsq = sb("sumsq", [P, NT])

        sage_w = sb("sage_w", [P, 2 * D])
        sage_b = sb("sage_b", [P, D])
        sage_y = big[:, 0:NT * 200].bitcast(BF16)[:, 0:NT * 386].rearrange("p (i c) -> p i c", c=386)
        sage_r = big[:, NT * 200:NT * 200 + N].rearrange("p (i d) -> p i d", d=D)
        sage_sum = sb("sage_sum", [P, 2, D])
        sage_rec = sb("sage_rec", [P, 2])

        adj_words = adjT[:, :, :].rearrange("p i n -> p (i n)").bitcast(F32)
        a_o = [0]

        def in_adj(n, rows=P):
            a_o[0] += n
            assert a_o[0] <= NT * N // 2
            return adj_words[0:rows, a_o[0] - n:a_o[0]]

        wx_h = expert_in[0:NS, 0:SH * D].rearrange("p (h d) -> p h d", h=SH)
        o6 = SH * D
        ws_T, bx_T = expert_in[0:NS, o6:o6 + SG], expert_in[0:NS, o6 + SG:o6 + SG + SH]
        o6 += SG + SH
        bs_b, temp_b = expert_in[:, o6:o6 + SG], expert_in[:, o6 + SG:o6 + SG + SH]
        wfx_T = in_adj(SI)
        bfx_T = in_adj(4)
        hy_in = in_adj(4 * HYP).rearrange("p (k n) -> p k n", k=4)
        hy_cw = in_adj(6 * 3).rearrange("p (q k) -> p q k", q=6)
        hy_cb = in_adj(6)
        hy_small = in_adj(4 * SH).rearrange("p (q h) -> p q h", q=4)
        hy_fcD = in_adj(4 * SH).rearrange("p (k h) -> p k h", k=4)
        hy_nw = in_adj(4)
        hy_out = in_adj(4 * SI).rearrange("p (k n) -> p k n", k=4)
        wo_T = in_adj(4 * D).rearrange("p (k d) -> p k d", k=4)
        ob_b = in_adj(D)
        logit_w = in_adj(SI)
        logit_c = in_adj(SI)
        A_T = in_adj(SI)
        q_rows = in_adj(SI)
        sn_rec = in_adj(SI)
        st_T = in_adj(4 * SG).rearrange("p (k g) -> p k g", k=4)
        block_o = in_adj(4 * P).rearrange("p (k g) -> p k g", k=4)
        slice_w = in_adj(4 * D).rearrange("p (k d) -> p k d", k=4)
        hc_raw = in_adj(6 * 66).rearrange("p (q l) -> p q l", q=6)
        hc = in_adj(6 * SG).rearrange("p (q l) -> p q l", q=6)
        hc_tanh = in_adj(6 * SG).rearrange("p (q l) -> p q l", q=6)
        yg_T = in_adj(4 * SG).rearrange("p (k g) -> p k g", k=4)
        hx_rows = in_adj(SI, SG)
        hy_a = in_adj(SI, SG)
        hy_cbm = in_adj(2 * SG, SG).rearrange("p (s l) -> p s l", s=2)
        hy_dt = in_adj(6 * 2 * SH, SG).rearrange("p (q h) -> p q h", q=6)
        hy_fD = in_adj(SH, SG)
        hy_ss = in_adj(2, SG)
        sw_T = big[:, 0:4 * N].rearrange("p (k n) -> p k n", k=4)
        o5 = 5 * N
        s_logit = big[:, o5:o5 + 1024].rearrange("p (b n) -> p b n", b=2)
        s_exp = big[:, o5 + 1024:o5 + 2048].rearrange("p (b n) -> p b n", b=2)
        s_sw = big[:, o5 + 2048:o5 + 3072].rearrange("p (b n) -> p b n", b=2)
        s_acc = big[:, o5 + 3072:o5 + 3584]
        s_hT = big[:, o5 + 3584:o5 + 4096].rearrange("p (i n) -> p i n", n=P)
        s_h = big[:, o5 + 4096:o5 + 4608].rearrange("p (i d) -> p i d", d=D)
        h_all = Gf[:, 0:N].rearrange("p (i d) -> p i d", d=D)
        hz, hy_b, hy_mix = (Gf[0:SG, N + q * SI:N + (q + 1) * SI] for q in range(3))
        hy_tdA, hy_dec = s_logit[0:SG], s_exp[0:SG]
        s_max = sb("s_max", [P, 2, SH])
        s_sum = sb("s_sum", [P, 2, SH])
        s_rec = sb("s_rec", [P, 2, SH])
        before = sb("before", [SG, SG])
        low = sb("low", [SG, SG])

        def bank_rows(b0, b1, c0, c1):
            return ps[:, b0:b1, 0:TPB * VC].rearrange("p b (k c) -> p b k c", c=VC)[:, :, :, c0:c1]

        def value_cols(c):
            return ps[:, 0:FULL, 0:TPB * VC].rearrange("p b (k c) -> p b k c", c=VC)[:, :, :, c]

        FULL = NT // TPB

        block = ctx.enter_context(nc.Block())

        def norm_rows(n):
            return h_all if n == 7 else h_rows

        def norm_vector(dve, n, need):
            dve.wait_ge(S("x_updates"), need)
            for i in range(NT):
                dve.bn_stats(stats[:, i, :], x[:, i, :]).then_inc(S("stats"), 1)
            for i in range(NT):
                dve.wait_ge(S("stats"), NT * n + i + 1)
                dve.bn_aggr(mean_var[:, i, :], stats[:, i, :]).then_inc(S("mean_var"), 1)
            if n == 0:
                gat_setup_vector(dve)
            dve.wait_ge(S("std"), n + 1)
            dve.reciprocal(rstd[:, :], std[:, :]).then_inc(S("rstd"), 1)
            dve.wait_ge(S("rstd"), n + 1)
            for i in range(NT):
                dve.tensor_scalar(norm_rows(n)[:, i, :], x[:, i, :], mean_var[:, i, 0:1], rstd[:, i:i + 1],
                                  ALU.subtract, ALU.mult).then_inc(S("h_rows"), 1)

        def norm_scalar(act, n):
            act.wait_ge(S("mean_var"), NT * (n + 1))
            act.activation(std[:, :], mean_var[:, :, 1], ACT.Sqrt, bias=EPS).then_inc(S("std"), 1)
            for g in range(NG):
                act.wait_ge(S("h_turned"), NT * n + 4 * (g + 1))
                act.copy(hT[:, g * 512:(g + 1) * 512], ps[:, 6 + g % 2, :]).then_inc(S("hT"), 1)

        def norm_tensor(pe, n):
            for g in range(NG):
                if g >= 2:
                    pe.wait_ge(S("hT"), NG * n + g - 1)
                for i in range(4):
                    pe.wait_ge(S("h_rows"), NT * n + 4 * g + i + 1)
                    pe.transpose(ps[:, 6 + g % 2, i * P:(i + 1) * P], norm_rows(n)[:, 4 * g + i, :], ident[:, :])\
                        .then_inc(S("h_turned"), 1)

        def hT_ready(eng, n, c=NG - 1):
            eng.wait_ge(S("hT"), NG * n + c + 1)

        GAT = {"L0": 0, "L1": 1, "L3": 2}
        VAL = {"L0": [0], "L1": [1], "L3": [2, 3]}

        def gat_setup_tensor(pe):
            pe.wait_ge(S("gat_loaded"), 16 * 10)
            for l in range(3):
                pe.matmul(ps[:, 7, 2 * l:2 * l + 2], gat_wT[:, l, :], gat_a[:, l, :], start=True, stop=True)\
                    .then_inc(S("score_vec"), 1)

        def gat_setup_vector(dve):
            dve.memset(zeros[:, :], 0.0).then_inc(S("zeros"), 1)
            dve.wait_ge(S("score_vec"), 3)
            dve.wait_ge(S("gat_loaded"), 16 * 10)
            for l in range(3):
                for s in range(2):
                    dve.tensor_copy(score_w[:, l, s, :], ps[:, 7, 2 * l + s:2 * l + s + 1].to_broadcast([P, P]))\
                        .then_inc(S("score_w"), 1)
            for v, l in enumerate((0, 1, 2, 2)):
                dve.tensor_copy(value_w[:, v, D:VC], ps[:, 7, 2 * l + 1:2 * l + 2]).then_inc(S("score_w"), 1)

        def gat_tensor(pe, L, n):
            l = GAT[L]
            pe.wait_ge(S("score_w"), 10)

            def score(s, c, bank):
                pe.matmul(ps[:, bank, :], score_w[:, l, s, :], hT[:, c * 512:(c + 1) * 512],
                          start=True, stop=True).then_inc(S("scores"), 1)

            def value(v, i, bank, k):
                pe.matmul(ps[:, bank, k * VC:(k + 1) * VC], hT[:, i * P:(i + 1) * P],
                          value_w[:, v, :], start=True, stop=True).then_inc(S("values"), 1)

            for c in range(NG):
                hT_ready(pe, n, c)
                score(1, c, 4 + c)
            for i in range(4 * TPB):
                value(VAL[L][0], i, i // TPB, i % TPB)
            pe.wait_ge(S("bound"), bound_end[L])
            for c in range(2):
                score(0, c, 6 + c)
            for i in range(4 * TPB, NT):
                value(VAL[L][0], i, i // TPB, i % TPB)
            pe.wait_ge(S("clamped"), 2 * l + 1)
            if L == "L3":
                pe.wait_ge(S("cut"), 1)
            for c in range(2):
                score(0, 2 + c, 6 + c)
            if L == "L3":
                pe.wait_ge(S("clamped"), 2 * l + 2)
                pe.wait_ge(S("cut"), 2)
                for i in range(NT):
                    if i and i % (2 * TPB) == 0:
                        pe.wait_ge(S("values_kept"), i // (2 * TPB))
                    value(VAL[L][1], i, 6 + i // TPB % 2, i % TPB)
            for sign, v in enumerate(VAL[L]):
                if sign == 0:
                    pe.wait_ge(S("G"), 3 * (v + 1))
                else:
                    pe.wait_ge(S("x_updates"), pass_end[L])
                    pe.wait_ge(S("G_neg"), 2)
                pe.wait_ge(S("zeros"), 1)
                for b in range(NBK):
                    w = VC * (TPB if b < FULL else NT - FULL * TPB)
                    pe.matmul(ps[:, b, 0:w], zeros[:, 0:P], zeros[:, 0:w], start=True, stop=False,
                              skip_group_check=True).then_inc(S("cleared"), 1)
                pe.wait_ge(S("cleared"), NBK * (v + 1))
                with pe.Fori(0, NT // 2) as jj:
                    for b in range(2):
                        pe.wait_ge(S("weights"), jj * 2 + (NT * v + b + 1 + 2))
                        for i in range(NT):
                            mm = pe.matmul(ps[:, i // TPB, (i % TPB) * VC:(i % TPB + 1) * VC],
                                           PR[:, b, i * P:(i + 1) * P], G[:, sign, bass.ds(jj * 2 + b, 1), :],
                                           start=False, stop=False, skip_group_check=True)
                        mm.then_inc(S("weights_used"), 1)

        def gat_scalar(act, L, n):
            for sign, v in enumerate(VAL[L]):
                l = GAT[L]
                if sign == 0:
                    act.wait_ge(S("clamped"), 2 * l + 1)
                    act.activation(R[:, 0, 0:N // 2], R[:, 0, 0:N // 2], ACT.Exp, scale=RISE).then_inc(S("R"), 1)
                    act.wait_ge(S("s2_rel"), 2 * (v + 1))
                    act.activation(K[:, 0, :], s2_rel[:, 0, :], ACT.Exp, scale=RISE).then_inc(S("KF"), 1)
                    act.activation(F[:, 0, :], s2_rel[:, 0, :], ACT.Exp, scale=SLOPE).then_inc(S("KF"), 1)
                    act.wait_ge(S("clamped"), 2 * l + 2)
                    act.activation(R[:, 0, N // 2:N], R[:, 0, N // 2:N], ACT.Exp, scale=RISE).then_inc(S("R"), 1)
                def relu(jj, b):
                    act.wait_ge(S("weights"), jj * 2 + (NT * v + b + 1))
                    act.activation(T[:, b, :], R[:, 0, :], ACT.Relu, bias=-1.0,
                                   scale=K[:, 0, bass.ds(jj * 2 + b, 1)]).then_inc(S("T"), 1)

                if sign == 0:
                    act.wait_ge(S("R"), 2 * (l + 1))
                    act.wait_ge(S("KF"), 2 * v + 2)
                if L == "L3" and sign == 0:
                    for b in range(2):
                        relu(0, b)
                    act.wait_ge(S("s2_rel"), 2 * (v + 1) + 1)
                    act.activation(K[:, 1, :], s2_rel[:, 1, :], ACT.Exp, scale=-RISE).then_inc(S("KF"), 1)
                    act.activation(F[:, 1, :], s2_rel[:, 1, :], ACT.Exp, scale=-SLOPE).then_inc(S("KF"), 1)
                    act.wait_ge(S("clamped_neg"), 2)
                    act.activation(R[:, 1, :], R[:, 1, :], ACT.Exp, scale=-RISE).then_inc(S("R"), 1)
                if sign == 0:
                    with act.Fori(1 if L == "L3" else 0, NT // 2) as jj:
                        for b in range(2):
                            relu(jj, b)
                if L == "L0" or sign == 1:
                    for q in range(3):
                        if L == "L0":
                            act.wait_ge(S("att_rows"), ATT[L] * 3 + q + 1)
                        else:
                            act.wait_ge(S("att_diff"), q + 1)
                        lo, hi = PIECES[q]
                        act.activation(rows_b[:, lo:hi, :], rows_a[:, lo:hi, :], ACT.Relu, scale=-1.0)\
                            .then_inc(S("elu_in"), 1)
                        act.wait_ge(S("elu_in"), 3 * ELU[L] + q + 1)
                        act.activation(rows_b[:, lo:hi, :], rows_b[:, lo:hi, :], ACT.Exp, scale=-1.0)\
                            .then_inc(S("elu_exp"), 1)

        ELU = {"L0": 0, "L3": 1}
        PIECES = [(0, 9), (9, 15), (15, 16)]
        bound_end = {"L0": 1, "L1": 2, "L3": 4}
        pass_end = {}

        def rows_of(q, c0, c1):
            lo, hi = PIECES[q]
            if hi <= FULL * TPB:
                return bank_rows(lo // TPB, hi // TPB, c0, c1)
            return ps[:, FULL:FULL + 1, c0:c1]

        def match(ap, q):
            lo, hi = PIECES[q]
            if hi <= FULL * TPB:
                return ap[:, lo:hi, :].rearrange("p (b k) d -> p b k d", k=TPB)
            return ap[:, lo:hi, :]

        def match1(ap, q, w):
            lo, hi = PIECES[q]
            if hi <= FULL * TPB:
                return ap[:, lo:hi].rearrange("p (b k) -> p b k", k=TPB).unsqueeze(3)\
                    .to_broadcast([P, (hi - lo) // TPB, TPB, w])
            return ap[:, lo:hi].unsqueeze(2).to_broadcast([P, hi - lo, w])

        def gat_vector(dve, L, n):
            l = GAT[L]
            halves = [(slice(0, N // 2), 0), (slice(N // 2, N), 1)]
            dve.wait_ge(S("scores"), 8 * l + 4)
            dve.tensor_reduce(s2_bound[:, 0:1], ps[:, 4:8, :], AX.XY, ALU.max).then_inc(S("bound"), 1)
            if L == "L3":
                dve.tensor_reduce(s2_bound[:, 1:2], ps[:, 4:8, :], AX.XY, ALU.min).then_inc(S("bound"), 1)
            dve.wait_ge(S("bound"), bound_end[L])

            def clamp(half):
                cols, c = halves[half]
                dve.wait_ge(S("scores"), 8 * l + 6 + 2 * c)
                dve.tensor_scalar(R[:, 0, cols], ps[:, 6:8, :], s2_bound[:, 0:1], CLAMP, ALU.add, ALU.min)\
                    .then_inc(S("clamped"), 1)
                if L == "L3":
                    dve.tensor_scalar(R[:, 1, cols], ps[:, 6:8, :], s2_bound[:, 1:2], -CLAMP, ALU.add, ALU.max)\
                        .then_inc(S("cut"), 1)

            clamp(0)
            v0 = VAL[L][0]
            dve.wait_ge(S("values"), NT * (v0 + 1))
            dve.tensor_scalar(s2_rel[:, 0, 0:15].rearrange("p (b k) -> p b k", k=TPB), value_cols(D),
                              s2_bound[:, 0:1], None, ALU.subtract).then_inc(S("s2_rel"), 1)
            dve.tensor_scalar(s2_rel[:, 0, 15:16], ps[:, FULL, D:VC], s2_bound[:, 0:1], None,
                              ALU.subtract).then_inc(S("s2_rel"), 1)
            clamp(1)
            for sign, v in enumerate(VAL[L]):
                if sign == 1:
                    negative(dve, 0, 1)
                    with dve.Fori(1, NT // 2) as jj:
                        for b in range(2):
                            negative(dve, jj, b)
                    finish(dve, L, sign, v)
                    continue

                def masked(jj, b):
                    j = jj * 2 + b
                    if L == "L0":
                        dve.wait_ge(S(f"adj_landed{b}"), jj * 16 + 16)
                        dve.tensor_copy(adjT[:, bass.ds(j, 1), :], adj_in[:, b, :]).then_inc(S("adjT"), 1)
                    dve.wait_ge(S("T"), j + (NT * TNUM[v] + 1))
                    dve.wait_ge(S("weights_used"), j + (NT * v + 1))
                    if L == "L0":
                        dve.wait_ge(S("adjT"), j + 1)
                    dve.scalar_tensor_tensor(PR[:, b, :], T[:, b, :], 1.0, adjT[:, bass.ds(j, 1), :],
                                             ALU.add, ALU.mult).then_inc(S("weights"), 1)

                dve.wait_ge(S("KF"), 2 * v + 2)
                dve.tensor_copy(G[:, sign, :, D], F[:, sign, :]).then_inc(S("G"), 1)
                for b0, b1 in ((0, FULL), (FULL, NBK)):
                    if b1 == FULL:
                        o = G[:, sign, 0:15, 0:D].rearrange("p (b k) d -> p b k d", k=TPB)
                        i0 = bank_rows(0, FULL, 0, D)
                        i1 = F[:, sign, 0:15].rearrange("p (b k) -> p b k", k=TPB).unsqueeze(3).to_broadcast(
                            [P, FULL, TPB, D])
                        dve.tensor_tensor(o, i0, i1, ALU.mult).then_inc(S("G"), 1)
                    else:
                        dve.tensor_scalar(G[:, sign, 15, 0:D], ps[:, FULL, 0:D], F[:, sign, 15:16], None, ALU.mult)\
                            .then_inc(S("G"), 1)
                if L == "L3":
                    for k in range(3):
                        i0, i1 = 2 * TPB * k, min(2 * TPB * (k + 1), NT)
                        dve.wait_ge(S("values"), NT * (v + 1) + i1)
                        if i1 - i0 == 2 * TPB:
                            dve.tensor_copy(G[:, 1, i0:i1, :].rearrange("p (b k) c -> p b k c", k=TPB),
                                            bank_rows(6, 8, 0, VC)).then_inc(S("values_kept"), 1)
                        else:
                            dve.tensor_copy(G[:, 1, i0:i1 - 1, :], bank_rows(6, 7, 0, VC).squeeze(1))\
                                .then_inc(S("values_kept"), 1)
                            dve.tensor_copy(G[:, 1, i1 - 1, :], ps[:, 7, 0:VC]).then_inc(S("values_kept"), 1)
                        if k < 2:
                            masked(0, k)
                    dve.wait_ge(S("cut"), 2)
                    for cols, _ in halves:
                        dve.tensor_scalar(R[:, 1, cols], R[:, 1, cols], CLAMP, None, ALU.min)\
                            .then_inc(S("clamped_neg"), 1)
                    dve.wait_ge(S("values_kept"), 4)
                    dve.tensor_scalar(s2_rel[:, 1, :], G[:, 1, :, D], s2_bound[:, 1:2], None, ALU.subtract)\
                        .then_inc(S("s2_rel"), 1)
                with dve.Fori(1 if L == "L3" else 0, NT // 2) as jj:
                    for b in range(2):
                        masked(jj, b)
                if L == "L3":
                    dve.wait_ge(S("R"), 7)
                    negative(dve, 0, 0)
                finish(dve, L, sign, v)

        def negative(dve, jj, b):
            v = VAL["L3"][1]
            j = jj * 2 + b
            dve.wait_ge(S("weights"), j + (NT * v + 1))
            dve.tensor_scalar(T[:, b, :], R[:, 1, :], K[:, 1, bass.ds(j, 1)], 1.0, ALU.mult,
                              ALU.min).then_inc(S("T_neg"), 1)
            dve.wait_ge(S("T_neg"), j + 1)
            dve.wait_ge(S("weights_used"), j + (NT * v + 1))
            dve.tensor_tensor(PR[:, b, :], T[:, b, :], adjT[:, bass.ds(j, 1), :], ALU.mult)\
                .then_inc(S("weights"), 1)

        def finish(dve, L, sign, v):
            dve.wait_ge(S("weights_used"), NT * (v + 1) + 2)
            for q in range(3):
                lo, hi = PIECES[q]
                cols = ps[:, lo // TPB:hi // TPB, 0:TPB * VC].rearrange("p b (k c) -> p b k c", c=VC)[:, :, :, D] \
                    if q < 2 else ps[:, FULL, D:VC]
                o = rowrec[:, lo:hi].rearrange("p (b k) -> p b k", k=TPB) if q < 2 else rowrec[:, lo:hi]
                dve.reciprocal(o, cols).then_inc(S("rowrec"), 1)
            dve.wait_ge(S("rowrec"), 3 * (v + 1))
            if L == "L3" and sign == 0:
                for q in range(3):
                    dve.tensor_tensor(match(rows_c, q), rows_of(q, 0, D), match1(rowrec, q, D), ALU.mult)\
                        .then_inc(S("x_updates"), 1)
                return
            for q in range(3):
                dve.tensor_tensor(match(rows_a, q), rows_of(q, 0, D), match1(rowrec, q, D), ALU.mult)\
                    .then_inc(S("att_rows"), 1)
            a0 = ATT[L] * 3
            for q in range(3):
                lo, hi = PIECES[q]
                dve.wait_ge(S("att_rows"), a0 + q + 1)
                if L == "L1":
                    dve.tensor_tensor(x[:, lo:hi, :], x[:, lo:hi, :], rows_a[:, lo:hi, :], ALU.add)\
                        .then_inc(S("x_updates"), 1)
                    continue
                if sign == 1:
                    dve.tensor_tensor(rows_a[:, lo:hi, :], rows_c[:, lo:hi, :], rows_a[:, lo:hi, :],
                                      ALU.subtract).then_inc(S("att_diff"), 1)
            if L == "L1":
                return
            for q in range(3):
                lo, hi = PIECES[q]
                if sign == 1:
                    dve.wait_ge(S("att_diff"), q + 1)
                dve.scalar_tensor_tensor(x[:, lo:hi, :], rows_a[:, lo:hi, :], 0.0, x[:, lo:hi, :],
                                         ALU.max, ALU.add).then_inc(S("elu_sum"), 1)
            for q in range(3):
                lo, hi = PIECES[q]
                dve.wait_ge(S("elu_exp"), 3 * ELU[L] + q + 1)
                dve.wait_ge(S("elu_sum"), 3 * ELU[L] + q + 1)
                dve.scalar_tensor_tensor(x[:, lo:hi, :], rows_b[:, lo:hi, :], -1.0, x[:, lo:hi, :],
                                         ALU.add, ALU.add).then_inc(S("x_updates"), 1)

        TNUM = [0, 1, 2]
        ATT = {"L0": 0, "L1": 1, "L3": 2}

        MOE = {"L0": 0, "L2": 1}
        ITEMS = {L: NG * HC[L] for L in HC}
        BASE = {"L0": 0, "L2": E * ITEMS["L0"]}

        def moe_items(L):
            out = []
            for s in range(2):
                for c in range(NG):
                    for k in range(HC[L]):
                        out.append((len(out), s, c, k))
            return out

        def moe_tensor(pe, L, n):
            m, items, base = MOE[L], moe_items(L), BASE[L]
            per = len(items)
            pe.wait_ge(S("moe_loaded"), 16 * 9)
            for i in range(NT):
                if i % 4 == 0:
                    hT_ready(pe, n, i // 4)
                mm = pe.matmul(ps[:, 0, i * E:(i + 1) * E], hT[:, i * P:(i + 1) * P], gate_w[:, m, :],
                               start=True, stop=True)
            mm.then_inc(S("gates"), 1)

            def thrice(out, w, xs, done, **flags):
                for step, (p, q) in enumerate(((0, 0), (0, 1), (1, 0))):
                    mm = pe.matmul(out, w[p], xs[q], start=flags["first"] and step == 0,
                                   stop=flags["first"] and step == 2, skip_group_check=not flags["first"])
                mm.then_inc(S(done), 1)

            def up(jj, item, extra=0):
                i, s, c, k = item
                at = jj * per + (base + i + extra)
                if (c, k) == (0, 0):
                    pe.wait_ge(S("w_lo"), jj * 4 + (2 * (E * m + s + 1) + (4 if extra else 0)))
                pe.wait_ge(S("act_h"), at + 1)
                thrice(ps[:, 4 + i % RING, :], [w_parts[:, s, 0, q, k * P:(k + 1) * P] for q in range(2)],
                       [hT_parts[:, q, c * 512:(c + 1) * 512] for q in range(2)], "up", first=True)

            def down(jj, item):
                i, s, c, k = item
                pe.wait_ge(S("h_lo"), jj * per + (base + i + 1 + RING))
                thrice(ps[:, c, :], [w_parts[:, s, 1, q, k * P:(k + 1) * P] for q in range(2)],
                       [h_parts[:, q, i % RING, :] for q in range(2)], "down", first=False)

            pe.wait_ge(S("hT_lo"), NG * (m + 1))
            for i in range(LAG):
                up(0, items[i])
            pe.wait_ge(S("comb"), m + 1)
            pe.transpose(ps[:, 3, 0:P], comb[:, :, :].rearrange("p e i -> p (e i)"), ident[:, :])\
                .then_inc(S("mixing"), 1)
            for c in range(NG):
                if c == 3:
                    pe.wait_ge(S("comb_T"), m + 1)
                for i in range(4):
                    weight = comb[:, 0, 4 * c + i:4 * c + i + 1]
                    mm = pe.matmul(ps[:, c, i * P:(i + 1) * P], weight.to_broadcast([P, P]), ident[:, :],
                                   start=True, stop=True)
                mm.then_inc(S("mixing"), 1)
            pe.wait_ge(S("zeros"), 1)
            for c in range(NG):
                pe.wait_ge(S("first_mix"), NG * m + c + 1)
                for h in range(2):
                    mm = pe.matmul(ps[:, c, h * 256:(h + 1) * 256], zeros[:, 0:P], zeros[:, 0:256],
                                   start=True, stop=False, skip_group_check=True)
                mm.then_inc(S("mixing"), 1)
            pe.wait_ge(S("mixing"), MIXING * m + 9)
            with pe.Fori(0, E // 2 - 1) as jj:
                for i in range(per):
                    if i + LAG < per:
                        up(jj, items[i + LAG])
                    else:
                        up(jj, items[i + LAG - per], per)
                    down(jj, items[i])
            for i in range(per):
                if i + LAG < per:
                    up(E // 2 - 1, items[i + LAG])
                down(E // 2 - 1, items[i])
                s, c, k = items[i][1:]
                if (s, k) == (1, HC[L] - 1):
                    pe.wait_ge(S("comb8"), 16 * (m + 1))
                    pe.matmul(ps[:, c, :], b2[:, m, :], comb8[:, c * 512:(c + 1) * 512], start=False, stop=False,
                              skip_group_check=True).then_inc(S("mixing"), 1)
            for c in range(NG):
                pe.wait_ge(S("out_T"), NG * m + c + 1)
                for i in range(4):
                    mm = pe.transpose(ps[:, 4 + c, i * P:(i + 1) * P], out_T[:, c, i * P:(i + 1) * P], ident[:, :])
                mm.then_inc(S("out_turned"), 1)

        def moe_scalar(act, L, n):
            m, items, base = MOE[L], moe_items(L), BASE[L]
            per = len(items)
            for c in range(NG):
                hT_ready(act, n, c)
                cols = slice(c * 512, (c + 1) * 512)
                act.copy(hT_parts[:, 0, cols], hT[:, cols]).then_inc(S("hT_hi"), 1)
            act.wait_ge(S("moe_loaded"), 16 * 9)
            if L == "L2":
                act.wait_ge(S("top"), 2 * RANK_STEPS + 1)
                act.activation(topm[:, 4, :], topm[:, 4, :], ACT.Exp).then_inc(S("top_exp"), 1)
            with act.Fori(0, E // 2) as jj:
                def high(i):
                    at = jj * per + (base + i)
                    act.wait_ge(S("prod"), at + 1)
                    act.wait_ge(S("down"), at + 1)
                    act.copy(h_parts[:, 0, i % RING, :], act_h[:, i % RING, :]).then_inc(S("h_hi"), 1)

                for i, s, c, k in items:
                    at = jj * per + (base + i)
                    act.wait_ge(S("up"), at + 1)
                    act.wait_ge(S("h_lo"), at + 1)
                    act.sem_inc(S("seen"), 1)
                    act.activation(act_h[:, i % RING, :], ps[:, 4 + i % RING, :], ACT.Gelu if L == "L0" else ACT.Relu,
                                   bias=b1_T[L][:, bass.ds(jj * (2 * HC[L]) + (s * HC[L] + k), 1)])\
                        .then_inc(S("act_h"), 1)
                    if i:
                        high(i - 1)
                high(per - 1)
            for c in range(NG):
                act.wait_ge(S("mixing"), MIXING * m + 10 + c)
                act.copy(out_T[:, c, :], ps[:, c, :]).then_inc(S("out_T"), 1)

        MIXING = 13
        RANK_STEPS = 11

        def moe_vector(dve, L, n):
            m, items, base = MOE[L], moe_items(L), BASE[L]
            per = len(items)
            count = [RANK_STEPS * m]

            def step(ins):
                ins.then_inc(S("top"), 1)
                count[0] += 1
                dve.wait_ge(S("top"), count[0])

            def over_e(ap):
                return ap.unsqueeze(2).to_broadcast([P, NT, E])

            def over_i(ap):
                return ap.unsqueeze(1).to_broadcast([P, NT, E])

            sc, key, oh1, oh2, sc2 = (top[:, q, :, :] for q in range(5))
            m1, m2, k1 = (topm[:, q, :] for q in range(3))
            for c in range(NG):
                cols = slice(c * 512, (c + 1) * 512)
                dve.wait_ge(S("hT_hi"), NG * m + c + 1)
                dve.tensor_tensor(hT_parts[:, 1, cols], hT[:, cols], hT_parts[:, 0, cols], ALU.subtract)\
                    .then_inc(S("hT_lo"), 1)
            dve.wait_ge(S("moe_loaded"), 16 * 9)
            dve.wait_ge(S("gates"), m + 1)
            step(dve.tensor_tensor(sc, ps[:, 0, 0:NT * E].rearrange("p (i e) -> p i e", e=E),
                                   over_i(gate_b[:, m, :]), ALU.add))
            step(dve.tensor_reduce(m1, sc, AX.X, ALU.max))
            step(dve.tensor_tensor(key, sc, over_e(m1), ALU.is_equal))
            step(dve.tensor_tensor(key, key, over_i(first[:, :]), ALU.mult))
            step(dve.tensor_reduce(k1, key, AX.X, ALU.max))
            step(dve.tensor_tensor(oh1, key, over_e(k1), ALU.is_equal))
            step(dve.scalar_tensor_tensor(sc2, oh1, -3.0e38, sc, ALU.mult, ALU.add))
            step(dve.tensor_reduce(m2, sc2, AX.X, ALU.max))
            step(dve.tensor_tensor(key, sc2, over_e(m2), ALU.is_equal))
            step(dve.tensor_tensor(key, key, over_i(first[:, :]), ALU.mult))
            step(dve.tensor_reduce(k1, key, AX.X, ALU.max))
            by_e = comb[:, :, :].rearrange("p e i -> p i e")
            if L == "L0":
                dve.tensor_tensor(oh2, key, over_e(k1), ALU.is_equal).then_inc(S("oh2"), 1)
                dve.wait_ge(S("oh2"), 1)
                dve.tensor_tensor(by_e, oh1, oh2, ALU.add).then_inc(S("comb"), 1)
            else:
                p1, p2 = topm[:, 5, :], topm[:, 6, :]
                step(dve.tensor_tensor(topm[:, 4, :], m2, m1, ALU.subtract))

                step(dve.tensor_tensor(oh2, key, over_e(k1), ALU.is_equal))
                dve.wait_ge(S("top_exp"), 1)
                step(dve.tensor_scalar(p1, topm[:, 4, :], 1.0, None, ALU.add))
                step(dve.reciprocal(p1, p1))
                step(dve.tensor_tensor(p2, topm[:, 4, :], p1, ALU.mult))
                dve.tensor_tensor(oh1, oh1, over_e(p1), ALU.mult).then_inc(S("oh2"), 1)
                dve.tensor_tensor(oh2, oh2, over_e(p2), ALU.mult).then_inc(S("oh2"), 1)
                dve.wait_ge(S("oh2"), 3)
                dve.tensor_tensor(by_e, oh1, oh2, ALU.add).then_inc(S("comb"), 1)
            dve.wait_ge(S("mixing"), MIXING * m + 1)
            dve.tensor_copy(comb_T[:, :], ps[:, 3, 0:P]).then_inc(S("comb_T"), 1)
            for c in range(NG):
                dve.wait_ge(S("mixing"), MIXING * m + c + 2)
                dve.tensor_copy(comb_b[:, 0, c * 512:(c + 1) * 512], ps[:, c, :]).then_inc(S("first_mix"), 1)
            with dve.Fori(0, E // 2) as jj:
                def low_part(i):
                    dve.wait_ge(S("h_hi"), jj * per + (base + i + 1))
                    dve.tensor_tensor(h_parts[:, 1, i % RING, :], act_h[:, i % RING, :], h_parts[:, 0, i % RING, :],
                                      ALU.subtract).then_inc(S("h_lo"), 1)

                for i, s, c, k in items:
                    at = jj * per + (base + i)
                    if (s, k) == (0, 0):
                        dve.wait_ge(S("first_mix"), NG * m + c + 1)
                    if (c, k) == (0, 0):
                        dve.wait_ge(S(f"comb_b{s}"), jj * 16 + 16 * ((3 + s) * m + 1))
                    dve.wait_ge(S("act_h"), at + 1 + RING)
                    dve.tensor_tensor(act_h[:, i % RING, :], act_h[:, i % RING, :],
                                      comb_b[:, s, c * 512:(c + 1) * 512], ALU.mult).then_inc(S("prod"), 1)
                    if i:
                        low_part(i - 1)
                low_part(per - 1)
            for c in range(NG):
                dve.wait_ge(S("out_turned"), NG * m + c + 1)
                dve.tensor_tensor(x[:, 4 * c:4 * c + 4, :], x[:, 4 * c:4 * c + 4, :],
                                  ps[:, 4 + c, :].rearrange("p (i d) -> p i d", d=D), ALU.add)\
                    .then_inc(S("x_updates"), 1)

        def moe_pool(pool, L, before_x):
            m, base, H = MOE[L], BASE[L], HC[L] * P
            pool.wait_ge(S("x_updates"), before_x)

            def split(jj, s):
                pool.wait_ge(S(f"expert_w{s}"), jj * 32 + 32 + 32 * 4 * m)
                pool.sem_inc(S("seen"), 1)
                for w, raw in enumerate((w1_e[:, s, 0:H], w2_e[:, s, :, :].rearrange("p k d -> p (k d)")[:, 0:H])):
                    pool.tensor_copy(w_parts[:, s, w, 0, 0:H], raw).then_inc(S("w_hi"), 1)
                    pool.wait_ge(S("w_hi"), jj * 4 + (2 * (E * m + s) + w + 1))
                    pool.tensor_tensor(w_parts[:, s, w, 1, 0:H], raw, w_parts[:, s, w, 0, 0:H], ALU.subtract)\
                        .then_inc(S("w_lo"), 1)

            for s in range(2):
                split(0, s)
            with pool.Fori(1, E // 2) as jj:
                for s in range(2):
                    pool.wait_ge(S("down"), (jj * 2 + s) * ITEMS[L] + (base - ITEMS[L] + RING))
                    split(jj, s)

        def moe_sync(sp, L, n):
            m, base = MOE[L], BASE[L]
            H = HC[L] * P
            w1, w2 = t[f"{L}_ffn_W1"], t[f"{L}_ffn_W2"]

            def weights(e, s):
                sp.dma_start(w1_e[:, s, 0:H], w1[bass.ds(e, 1), :, :].rearrange("e d h -> d (e h)"))\
                    .then_inc(S(f"expert_w{s}"), 16)
                sp.dma_start(w2_e[:, s, 0:HC[L], :],
                             w2[bass.ds(e, 1), :, :].rearrange("e (k p) d -> p (e k) d", p=P))\
                    .then_inc(S(f"expert_w{s}"), 16)

            def mix(e, s):
                sp.dma_start(comb_b[:, s, :],
                             comb_dram[L][bass.ds(e, 1), :].to_broadcast([P, N])).then_inc(S(f"comb_b{s}"), 16)

            for s in range(2):
                if m:
                    sp.wait_ge(S("w_lo"), 2 * E)
                    sp.wait_ge(S("x_updates"), need["sage"])
                weights(s, s)
            sp.wait_ge(S("comb_T"), m + 1)
            sp.dma_start(comb_dram[L].rearrange("e (i n) -> (e i) n", n=P), comb_T[:, :]).then_inc(S("comb_out"), 16)
            sp.wait_ge(S("comb_out"), 16 * (m + 1))
            mix(1, 1)
            sp.dma_start(comb8, comb_dram[L][:, :]).then_inc(S("comb8"), 16)
            with sp.Fori(1, E // 2) as jj:
                for s in range(2):
                    e = jj * 2 + s
                    sp.wait_ge(S("prod"), e * ITEMS[L] + (base - ITEMS[L]))
                    mix(e, s)
                    sp.wait_ge(S("w_lo"), e * 2 + 2 * (E * m - 1))
                    weights(e, s)

        PARTS = [(0, 0, P), (1, P, P), (2, 2 * P, NS), (3, 2 * P + NS, NS)]
        HALO = 3

        def on_chunk(eng, g, name, k):
            eng.wait_ge(S(name), g * 4 + (k + 1 + 2))

        CHUNKS = ["m_turned", "m_rows", "m_tri_dA", "m_segsum", "m_decay", "m_mix", "m_x_dt", "m_x_decayed",
                  "m_x_skip", "m_y_parts", "m_state_new", "m_state", "m_y_sum", "m_y_skip", "m_y_gated",
                  "m_yT_turned", "m_yT", "m_out", "m_y_rows", "m_square"]

        FIRST = -1

        def conv_bank(g, q):
            return q if g is FIRST else 5

        def mamba_groups(eng, body):
            with eng.Fori(0, NG - 1) as g:
                body(g, False)
            body(NG - 1, True)

        def mamba_tensor(pe, n):
            pe.wait_ge(S("mamba_loaded"), 16 * 10)
            hT_ready(pe, n)
            for k in range(2):
                mm = pe.matmul(ps[:, 5, k * P:(k + 1) * P], wout_T[:, k, :], w_lin[:, :], start=True, stop=True)
            mm.then_inc(S("m_proj"), 1)
            pe.wait_ge(S("m_halved"), 3)
            for i in range(NT):
                if i >= 4:
                    pe.wait_ge(S("m_z_gate"), i - 3)
                    pe.wait_ge(S("m_dt_raw"), i - 3)
                pe.matmul(ps[:, i % 4, 0:DI + NH], hT[:, i * P:(i + 1) * P], win_zd[:, :], start=True, stop=True)\
                    .then_inc(S("m_zd"), 1)

            def conv_in(g, q):
                if g is not FIRST:
                    on_chunk(pe, g, "m_rows", 3)
                    pe.wait_ge(S("m_conv_seed"), g * 4 + (4 + q))
                    pe.sem_inc(S("seen"), 1)
                _, c0, w = PARTS[q]
                pe.matmul(ps[0:w, conv_bank(g, q), :], win_x[:, c0:c0 + w], hT[:, bass.ts(g + 1, 512)],
                          start=True, stop=True).then_inc(S("m_conv_in"), 1)

            def turn(g, i):
                pe.wait_ge(S("m_conv"), g * 4 + (4 + 3))
                on_chunk(pe, g, "m_rows", i + 2)
                for q in range(2):
                    pe.transpose(ps[:, 4 + i % 2, q * P:(q + 1) * P], conv_out[:, q, i * P:(i + 1) * P], ident[:, :])
                pe.transpose(ps[:, 4 + i % 2, DI:DI + NS], conv_out[0:NS, 2, i * P:(i + 1) * P], ident[0:NS, 0:NS])\
                    .then_inc(S("m_turned"), 1)

            def segsum(g, i):
                on_chunk(pe, g, "m_tri_dA", i)
                on_chunk(pe, g, "m_decay", i - 1)
                pe.matmul(ps[:, 7, :], after[:, :], tri_dA[:, i % 2, :], start=True, stop=True)\
                    .then_inc(S("m_segsum"), 1)

            def front(g):
                turn(g, 0)
                turn(g, 1)
                pe.wait_ge(S("m_conv"), g * 4 + (4 + 4))
                if g is not FIRST:
                    pe.wait_ge(S("m_cb_masked"), g + 1)
                for i in range(4):
                    mm = pe.matmul(ps[:, 6, i * P:(i + 1) * P], conv_out[0:NS, 2, i * P:(i + 1) * P],
                                   conv_out[0:NS, 3, i * P:(i + 1) * P], start=True, stop=True)
                mm.then_inc(S("m_cb"), 1)
                turn(g, 2)
                turn(g, 3)

            pe.wait_ge(S("m_clear"), 5)
            pe.wait_ge(S("m_z_gate"), NT)
            pe.wait_ge(S("m_dt_raw"), NT)
            for q in range(4):
                conv_in(FIRST, q)
            pe.wait_ge(S("m_dA"), 1)
            pe.matmul(ps[:, 4, 0:64], tri[:, :], dts[:, 4, :], start=True, stop=True)
            pe.matmul(ps[:, 4, 64:128], ones[:, :], dts[:, 4, :], start=True, stop=True).then_inc(S("m_cum"), 1)
            segsum(0, 0)
            pe.wait_ge(S("m_carry"), 1)
            segsum(0, 1)
            front(FIRST)

            def body(g, last):
                def turn_y(i):
                    on_chunk(pe, g, "m_y_gated", i)
                    on_chunk(pe, g, "m_y_rows", i - 1)
                    for k in range(2):
                        mm = pe.transpose(ps[:, 3, k * P:(k + 1) * P], y_gated[:, i % 2, k * P:(k + 1) * P],
                                          ident[:, :])
                    mm.then_inc(S("m_yT_turned"), 1)

                def project(i):
                    on_chunk(pe, g, "m_yT", i)
                    for k in range(2):
                        mm = pe.matmul(ps[:, 3, DI:DI + D], y_T[:, i % 2, k * P:(k + 1) * P], w_proj[:, k, :],
                                       start=(k == 0), stop=(k == 1))
                    mm.then_inc(S("m_out"), 1)

                for i in range(4):
                    on_chunk(pe, g, "m_state", i - 1)
                    on_chunk(pe, g, "m_y_sum", i - 2)
                    pe.matmul(ps[:, i % 2, DI:2 * DI], conv_out[0:NS, 3, i * P:(i + 1) * P], state[:, i % 2, :],
                              start=True, stop=True)
                    on_chunk(pe, g, "m_mix", i)
                    on_chunk(pe, g, "m_x_dt", i)
                    for h in range(NH):
                        mm = pe.matmul(ps[:, i % 2, h * HD:(h + 1) * HD], mixm[:, i % 2, h * P:(h + 1) * P],
                                       x_dt[:, i % 2, h * HD:(h + 1) * HD], start=True, stop=True)
                    mm.then_inc(S("m_y_parts"), 1)
                    on_chunk(pe, g, "m_x_decayed", i)
                    pe.matmul(ps[0:NS, 2, 0:DI], xb_rows[:, i, DI:DI + NS], x_decayed[:, i % 2, :],
                              start=True, stop=True).then_inc(S("m_state_new"), 1)
                    if i >= 1:
                        turn_y(i - 1)
                    if not last:
                        conv_in(g, i)
                    if not (last and i >= 2):
                        segsum(g, i + 2)
                    if i >= 1:
                        project(i - 1)
                if not last:
                    front(g)
                turn_y(3)
                project(3)

            mamba_groups(pe, body)

        def mamba_scalar(act, n):
            act.wait_ge(S("mamba_loaded"), 16 * 10)
            act.activation(exp_A[:, :], small_in[:, 1, :], ACT.Exp).then_inc(S("m_expA"), 1)
            for i in range(NT):
                act.wait_ge(S("m_zd"), i + 1)
                if i >= 2:
                    act.wait_ge(S("m_z_gate"), i - 1)
                act.activation(z_tanh[:, i % 2, :], ps[:, i % 4, 0:DI], ACT.Tanh).then_inc(S("m_z_tanh"), 1)
            act.wait_ge(S("m_dt_abs"), 1)
            act.activation(dts[:, 2, :], dts[:, 1, :], ACT.Exp, scale=-1.0).then_inc(S("m_dt_exp"), 1)
            act.wait_ge(S("m_dt_exp"), 1)
            act.activation(dts[:, 5, :], dts[:, 2, :], ACT.Ln, bias=1.0).then_inc(S("m_dt_ln"), 1)

            def seed(g, q):
                _, c0, w = PARTS[q]
                if g is not FIRST:
                    act.wait_ge(S("m_conv_tap"), g * 12 + 3 * (q + 1))
                    act.copy(conv_raw[:, q, 0:HALO], conv_raw[:, q, 512:512 + HALO]).then_inc(S("m_halo"), 1)
                    act.wait_ge(S("m_halo"), g * 4 + (q + 1))
                    act.wait_ge(S("m_conv"), g * 4 + (q + 1))
                act.wait_ge(S("m_conv_in"), g * 4 + (4 + q + 1))
                bank = conv_bank(g, q)
                act.copy(conv_raw[0:w, q, HALO:HALO + 512], ps[0:w, bank, :]).then_inc(S("m_conv_raw"), 1)
                act.activation(conv[0:w, q, :], ps[0:w, bank, :], ACT.Identity, bias=conv_b[0:w, q:q + 1],
                               scale=conv_w[0:w, q, HALO:HALO + 1]).then_inc(S("m_conv_seed"), 1)

            def tanh(g, q):
                w = PARTS[q][2]
                act.wait_ge(S("m_conv_tap"), g * 12 + (12 + 3 * (q + 1)))
                act.activation(conv_tanh[0:w, q, :], conv[0:w, q, :], ACT.Tanh).then_inc(S("m_conv_tanh"), 1)

            def decays(g, i):
                on_chunk(act, g, "m_segsum", i)
                on_chunk(act, g, "m_mix", i - 2)
                on_chunk(act, g, "m_x_decayed", i - 2)
                act.activation(decay[:, i % 2, :], ps[:, 7, :], ACT.Exp).then_inc(S("m_decay"), 1)

            def rows(g):
                for i in range(4):
                    on_chunk(act, g, "m_turned", i + 4)
                    if g is not FIRST:
                        on_chunk(act, g, "m_state_new", i)
                        on_chunk(act, g, "m_x_skip", i)
                    act.copy(xb_rows[:, i, :], ps[:, 4 + i % 2, 0:DI + NS]).then_inc(S("m_rows"), 1)

            for q in range(4):
                seed(FIRST, q)
            act.wait_ge(S("m_cum"), 1)
            act.activation(carry[:, :, :], ps[:, 4, 0:128].rearrange("p (s n) -> p s n", s=2), ACT.Exp)\
                .then_inc(S("m_carry"), 1)
            decays(0, 0)
            for q in range(4):
                tanh(FIRST, q)
            rows(FIRST)

            def body(g, last):
                def copy_turned(i):
                    on_chunk(act, g, "m_yT_turned", i)
                    on_chunk(act, g, "m_out", i - 2)
                    act.copy(y_T[:, i % 2, :], ps[:, 3, 0:DI]).then_inc(S("m_yT"), 1)

                def tail(i):
                    on_chunk(act, g, "m_square", i - 1)
                    act.activation(y_square[:, :], y_gated[:, i % 2, :], ACT.Square,
                                   accum_out=sumsq[:, bass.ds(g * 4 + i, 1)]).then_inc(S("m_square"), 1)
                    on_chunk(act, g, "m_out", i)
                    act.copy(y_rows[:, bass.ds(g * 4 + i, 1), :], ps[:, 3, DI:DI + D]).then_inc(S("m_y_rows"), 1)

                for i in range(4):
                    if not (last and i == 3):
                        decays(g, i + 1)
                    if i >= 1:
                        copy_turned(i - 1)
                    if not last:
                        seed(g, i)
                    if not last and i >= 1:
                        tanh(g, i - 1)
                    if i >= 1:
                        tail(i - 1)
                if not last:
                    tanh(g, 3)
                    rows(g)
                copy_turned(3)
                tail(3)

            mamba_groups(act, body)
            act.wait_ge(S("m_square"), NT + 2)
            act.activation(sumsq[:, :], sumsq[:, :], ACT.Sqrt, scale=1.0 / DI, bias=EPS).then_inc(S("m_rms"), 1)

        def mamba_pool(pool):
            pool.wait_ge(S("m_dA"), 1)

            def heads(g, ap, c, w):
                return ap[:, bass.ds(g * 16 + c * NH, NH)].unsqueeze(2).to_broadcast([P, NH, w])

            def tri_times(g, i):
                on_chunk(pool, g, "m_segsum", i - 2)
                pool.tensor_tensor(tri_dA[:, i % 2, :].rearrange("p (h l) -> p h l", h=NH),
                                   tri[:, :].unsqueeze(1).to_broadcast([P, NH, P]), heads(g, dts[:, 4, :], i, P),
                                   ALU.mult).then_inc(S("m_tri_dA"), 1)

            def body(g, last):
                for i in range(4):
                    on_chunk(pool, g, "m_rows", i)
                    on_chunk(pool, g, "m_y_parts", i - 2)
                    on_chunk(pool, g, "m_x_decayed", i - 2)
                    x3 = xb_rows[:, i, 0:DI].rearrange("p (h d) -> p h d", h=NH)
                    pool.tensor_tensor(x_dt[:, i % 2, :].rearrange("p (h d) -> p h d", h=NH), x3,
                                       heads(g, dts[:, 3, :], i, HD), ALU.mult).then_inc(S("m_x_dt"), 1)
                    on_chunk(pool, g, "m_y_skip", i - 2)
                    pool.tensor_tensor(x_skip[:, i % 2, :].rearrange("p (h d) -> p h d", h=NH), x3,
                                       small_in[:, 2, :].unsqueeze(2).to_broadcast([P, NH, HD]), ALU.mult)\
                        .then_inc(S("m_x_skip"), 1)
                    on_chunk(pool, g, "m_x_dt", i)
                    on_chunk(pool, g, "m_decay", i)
                    on_chunk(pool, g, "m_state_new", i - 2)
                    last_row = decay[:, i % 2, :].rearrange("p (h l) -> p h l", h=NH)[:, :, P - 1]
                    pool.tensor_tensor(x_decayed[:, i % 2, :].rearrange("p (h d) -> p h d", h=NH),
                                       x_dt[:, i % 2, :].rearrange("p (h d) -> p h d", h=NH),
                                       last_row.unsqueeze(2).to_broadcast([P, NH, HD]), ALU.mult)\
                        .then_inc(S("m_x_decayed"), 1)
                    if not (last and i >= 2):
                        tri_times(g, i + 2)

            tri_times(0, 0)
            tri_times(0, 1)
            mamba_groups(pool, body)

        def mamba_vector(dve, n):
            dve.wait_ge(S("mamba_loaded"), 16 * 10)
            dve.tensor_scalar(win_zd[:, 0:DI], win_zd[:, 0:DI], 0.5, None, ALU.mult).then_inc(S("m_halved"), 1)
            dve.tensor_scalar(conv_w[:, :, :], conv_w[:, :, :], 0.5, None, ALU.mult).then_inc(S("m_halved"), 1)
            dve.tensor_scalar(conv_b[:, :], conv_b[:, :], 0.5, None, ALU.mult).then_inc(S("m_halved"), 1)
            dve.wait_ge(S("m_proj"), 1)
            dve.memset(ones[:, :], 1.0).then_inc(S("m_clear"), 1)
            dve.memset(conv_raw[:, :, :], 0.0).then_inc(S("m_clear"), 1)
            dve.memset(state[:, :], 0.0).then_inc(S("m_clear"), 1)
            for k in range(2):
                dve.tensor_scalar(w_proj[:, k, :], ps[:, 5, k * P:(k + 1) * P], norm_w[:, k:k + 1], None, ALU.mult)\
                    .then_inc(S("m_clear"), 1)
            dve.wait_ge(S("m_clear"), 5)
            for i in range(NT):
                dve.wait_ge(S("m_z_tanh"), i + 1)
                dve.tensor_copy(dts[:, 0, i * NH:(i + 1) * NH], ps[:, i % 4, DI:DI + NH]).then_inc(S("m_dt_raw"), 1)
                dve.scalar_tensor_tensor(z_gate[:, i, :], z_tanh[:, i % 2, :], 1.0, ps[:, i % 4, 0:DI],
                                         ALU.add, ALU.mult).then_inc(S("m_z_gate"), 1)
            dt3 = [dts[:, q, :].rearrange("p (c h) -> p c h", h=NH) for q in range(6)]
            dve.wait_ge(S("m_dt_raw"), NT)
            dve.tensor_tensor(dt3[0], dt3[0], small_in[:, 0, :].unsqueeze(1).to_broadcast([P, NT, NH]), ALU.add)\
                .then_inc(S("m_dt_bias"), 1)
            dve.wait_ge(S("m_dt_bias"), 1)
            dve.scalar_tensor_tensor(dts[:, 1, :], dts[:, 0, :], -1.0, dts[:, 0, :], ALU.mult, ALU.max)\
                .then_inc(S("m_dt_abs"), 1)
            dve.wait_ge(S("m_dt_ln"), 1)
            dve.scalar_tensor_tensor(dts[:, 3, :], dts[:, 0, :], 0.0, dts[:, 5, :], ALU.max, ALU.add)\
                .then_inc(S("m_dt_bias"), 1)
            dve.wait_ge(S("m_dt_bias"), 2)
            dve.wait_ge(S("m_expA"), 1)
            dve.scalar_tensor_tensor(dt3[4], dt3[3], -1.0, exp_A[:, :].unsqueeze(1).to_broadcast([P, NT, NH]),
                                     ALU.mult, ALU.mult).then_inc(S("m_dA"), 1)

            def tap(g, q, k):
                w = PARTS[q][2]
                if k == 0:
                    dve.wait_ge(S("m_conv_seed"), g * 4 + (4 + q + 1))
                else:
                    dve.wait_ge(S("m_conv_tap"), g * 12 + (12 + 3 * q + k))
                dve.scalar_tensor_tensor(conv[0:w, q, :], conv_raw[0:w, q, k:k + 512], conv_w[0:w, q, k:k + 1],
                                         conv[0:w, q, :], ALU.mult, ALU.add).then_inc(S("m_conv_tap"), 1)

            def silu(g, q):
                w = PARTS[q][2]
                dve.wait_ge(S("m_conv_tanh"), g * 4 + (4 + q + 1))
                if g is not FIRST:
                    if q == 0:
                        on_chunk(dve, g, "m_turned", 3)
                    if q == 2:
                        dve.wait_ge(S("m_cb"), g + 1)
                    if q == 3:
                        on_chunk(dve, g, "m_y_parts", 3)
                dve.scalar_tensor_tensor(conv_out[0:w, q, :], conv_tanh[0:w, q, :], 1.0, conv[0:w, q, :],
                                         ALU.add, ALU.mult).then_inc(S("m_conv"), 1)

            def masked(g):
                dve.wait_ge(S("m_cb"), g + 2)
                dve.tensor_tensor(cb_masked[:, :, :], ps[:, 6, :].rearrange("p (i l) -> p i l", i=4),
                                  tri[:, :].unsqueeze(1).to_broadcast([P, 4, P]), ALU.mult)\
                    .then_inc(S("m_cb_masked"), 1)
                dve.wait_ge(S("m_cb_masked"), g + 2)

            def mix(g, i):
                on_chunk(dve, g, "m_decay", i)
                on_chunk(dve, g, "m_y_parts", i - 2)
                dve.tensor_tensor(mixm[:, i % 2, :].rearrange("p (h l) -> p h l", h=NH),
                                  decay[:, i % 2, :].rearrange("p (h l) -> p h l", h=NH),
                                  cb_masked[:, i % 4, :].unsqueeze(1).to_broadcast([P, NH, P]), ALU.mult)\
                    .then_inc(S("m_mix"), 1)

            for q in range(4):
                for k in range(HALO):
                    tap(FIRST, q, k)
            for q in range(4):
                silu(FIRST, q)
            masked(FIRST)
            mix(0, 0)
            dve.wait_ge(S("m_carry"), 1)

            def body(g, last):
                def heads(ap, rows, c, w):
                    return ap[0:rows, bass.ds(g * 16 + c * NH, NH)].unsqueeze(2).to_broadcast([rows, NH, w])

                for i in range(4):
                    b = i % 2
                    if i < 3:
                        mix(g, i + 1)
                    on_chunk(dve, g, "m_state", i - 1)
                    on_chunk(dve, g, "m_y_parts", i - 1)
                    dve.tensor_tensor(state[:, 1 - b, :].rearrange("p (h d) -> p h d", h=NH),
                                      state[:, b, :].rearrange("p (h d) -> p h d", h=NH),
                                      heads(carry[:, 1, :], NS, i, HD), ALU.mult).then_inc(S("m_state_aged"), 1)
                    on_chunk(dve, g, "m_y_parts", i)
                    on_chunk(dve, g, "m_y_sum", i - 1)
                    dve.tensor_tensor(y_a[:, :].rearrange("p (h d) -> p h d", h=NH),
                                      ps[:, b, DI:2 * DI].rearrange("p (h d) -> p h d", h=NH),
                                      heads(carry[:, 0, :], P, i, HD), ALU.mult).then_inc(S("m_y_a"), 1)
                    on_chunk(dve, g, "m_state_new", i)
                    dve.wait_ge(S("m_state_aged"), g * 4 + (i + 1))
                    dve.tensor_tensor(state[:, 1 - b, :], state[:, 1 - b, :], ps[0:NS, 2, 0:DI], ALU.add)\
                        .then_inc(S("m_state"), 1)
                    dve.wait_ge(S("m_y_a"), g * 4 + (i + 1))
                    on_chunk(dve, g, "m_y_skip", i - 1)
                    dve.tensor_tensor(y_b[:, :], y_a[:, :], ps[:, b, 0:DI], ALU.add).then_inc(S("m_y_sum"), 1)
                    if not last:
                        tap(g, i, 0)
                    on_chunk(dve, g, "m_y_sum", i)
                    on_chunk(dve, g, "m_x_skip", i)
                    on_chunk(dve, g, "m_yT_turned", i - 2)
                    on_chunk(dve, g, "m_square", i - 2)
                    dve.tensor_tensor(y_b[:, :], y_b[:, :], x_skip[:, b, :], ALU.add).then_inc(S("m_y_skip"), 1)
                    if not last:
                        tap(g, i, 1)
                    on_chunk(dve, g, "m_y_skip", i)
                    dve.tensor_tensor(y_gated[:, b, :], y_b[:, :], z_gate[:, bass.ds(g * 4 + i, 1), :], ALU.mult)\
                        .then_inc(S("m_y_gated"), 1)
                    if not last:
                        tap(g, i, 2)
                        if i:
                            silu(g, i - 1)
                if not last:
                    silu(g, 3)
                    masked(g)
                    mix(g, 4)

            mamba_groups(dve, body)
            dve.wait_ge(S("m_rms"), 1)
            dve.reciprocal(sumsq[:, :], sumsq[:, :]).then_inc(S("m_rms_inv"), 1)
            dve.wait_ge(S("m_y_rows"), NT + 2)
            dve.wait_ge(S("m_x_bias"), 1)
            dve.wait_ge(S("m_rms_inv"), 1)
            for i in range(NT):
                dve.scalar_tensor_tensor(x[:, i, :], y_rows[:, i, :], sumsq[:, i:i + 1], x[:, i, :],
                                         ALU.mult, ALU.add).then_inc(S("x_updates"), 1)

        def add_to_rows(pool, n, bias, name, loaded, count):
            hT_ready(pool, n)
            pool.wait_ge(S(loaded), 16 * count)
            pool.tensor_tensor(x[:, :, :], x[:, :, :], bias[:, :].unsqueeze(1).to_broadcast([P, NT, D]), ALU.add)\
                .then_inc(S(name), 1)

        PW = 3 * D + 1

        def sage_tensor(pe, n):
            pe.wait_ge(S("sage_loaded"), 16 * 2)
            hT_ready(pe, n)
            for i in range(NT):
                pe.matmul(ps[:, i // 2, (i % 2) * 2 * D:(i % 2 + 1) * 2 * D], hT[:, i * P:(i + 1) * P], sage_w[:, :],
                          start=True, stop=True).then_inc(S("g_in"), 1)
            pe.wait_ge(S("g_y"), 2 * NG + 1)
            pe.wait_ge(S("g_own"), 1)
            with pe.Fori(0, NT // 2) as ii:
                for b in range(2):
                    pe.wait_ge(S("g_x"), ii * 2 + (b + 1))
                    for j in range(NT):
                        mm = pe.matmul(ps[:, b, 0:PW], adjT[:, j, bass.ds(ii * 2 * P + b * P, P)],
                                       sage_y[:, j, 0:PW], start=(j == 0), stop=(j == NT - 1))
                    mm.then_inc(S("g_sums"), 1)

        def group_of(c):
            return ps[:, 2 * c:2 * c + 2, :].rearrange("p b (k d) -> p b k d", k=2)

        def four(ap):
            return ap.rearrange("p (b k) d -> p b k d", k=2)

        def sage_scalar(act):
            for c in range(NG):
                act.wait_ge(S("g_in"), 4 * c + 4)
                act.copy(four(sage_y[:, 4 * c:4 * c + 4, 0:D]), group_of(c)[:, :, :, 0:D]).then_inc(S("g_y1"), 1)

        def sage_vector(dve, n):
            dve.wait_ge(S("g_in"), 4)
            dve.memset(sage_y[:, :, 3 * D:PW], 1.0).then_inc(S("g_y"), 1)
            for step in range(NG + 2):
                for part in range(3):
                    c = step - part
                    if not 0 <= c < NG:
                        continue
                    a = slice(4 * c, 4 * c + 4)
                    if part == 0:
                        dve.wait_ge(S("g_y1"), c + 1)
                        dve.tensor_tensor(four(sage_r[:, a, :]), group_of(c)[:, :, :, 0:D], four(sage_y[:, a, 0:D]),
                                          ALU.subtract).then_inc(S("g_r"), 1)
                    if part == 1:
                        dve.wait_ge(S("g_r"), c + 1)
                        dve.tensor_copy(sage_y[:, a, D:2 * D], sage_r[:, a, :]).then_inc(S("g_y"), 1)
                    if part == 2:
                        dve.wait_ge(S("g_y"), [2, 3, 5, 7][c])
                        dve.tensor_tensor(sage_y[:, a, 2 * D:3 * D], sage_r[:, a, :], sage_y[:, a, D:2 * D],
                                          ALU.subtract).then_inc(S("g_y"), 1)
            dve.wait_ge(S("g_x_bias"), 1)
            for c in range(NG):
                x4 = four(x[:, 4 * c:4 * c + 4, :])
                dve.tensor_tensor(x4, x4, group_of(c)[:, :, :, D:2 * D], ALU.add).then_inc(S("g_own"), 1)
            dve.wait_ge(S("g_own"), NG)
            with dve.Fori(0, NT // 2) as ii:
                for b in range(2):
                    at = ii * 2 + b
                    dve.wait_ge(S("g_sums"), at + 1)
                    dve.reciprocal(sage_rec[:, b:b + 1], ps[:, b, 3 * D:PW]).then_inc(S("g_rec"), 1)
                    dve.tensor_reduce(sage_sum[:, b, :], ps[:, b, 0:3 * D].rearrange("p (s d) -> p d s", s=3), AX.X,
                                      ALU.add).then_inc(S("g_x"), 1)
                    dve.wait_ge(S("g_rec"), at + 1)
                    dve.wait_ge(S("g_x"), at + (2 + 1))
                    dve.scalar_tensor_tensor(x[:, bass.ds(at, 1), :], sage_sum[:, b, :], sage_rec[:, b:b + 1],
                                             x[:, bass.ds(at, 1), :], ALU.mult, ALU.add)\
                        .then_inc(S("x_updates"), 1)

        def on_tile(eng, g, name, k):
            eng.wait_ge(S(name), g * 4 + (k + 1 + 2))

        last = {name: NT + 2 for name in CHUNKS} | {
            "m_conv_in": 4 * NG, "m_conv_raw": 4 * NG, "m_conv_seed": 4 * NG, "m_conv_tap": 12 * NG,
            "m_conv_tanh": 4 * NG, "m_conv": 4 * NG, "m_cb": NG, "m_cb_masked": NG, "m_halo": 4 * (NG - 1),
            "m_zd": NT, "m_z_tanh": NT, "m_z_gate": NT, "m_dt_raw": NT, "m_dt_bias": 2, "m_dt_abs": 1,
            "m_dt_exp": 1, "m_dt_ln": 1, "m_dA": 1, "m_cum": 1, "m_carry": 1, "m_y_a": NT, "m_state_aged": NT}
        signals = """
            y_A_min y_block y_cb y_cbm y_clear y_conv y_conv_in y_dec y_dec_cb y_dt y_dt_abs y_dt_in y_exp
            y_fD y_gT y_gT_w y_gated y_halved y_ln y_mix y_normed y_o y_q y_raw y_rms y_rows y_slice_w
            y_spans y_ss y_t y_tanh y_tap y_tdA y_turned y_y y_z y_z_in y_z_tanh""".split()
        reused.update({y: (m, last[m]) for y, m in zip(signals, sorted(last), strict=False)})

        def after_mamba(name, count):
            return reused[name][1] + count

        TILES = ["s_logits", "s_add", "s_maxed", "s_sub", "s_exped", "s_summed", "s_rec", "s_sw", "s_acc", "s_A",
                 "s_turned", "s_swT", "s_stagedT", "s_staged"]
        S_LOADED = 16 * 15
        HPARTS = [(0, P), (1, P), (2, P), (3, P), (4, NS), (5, NS)]

        def heads8(ap, rows, w):
            return ap.unsqueeze(2).to_broadcast([rows, SH, w])

        def by_head(ap):
            return ap.rearrange("p (h g) -> p h g", h=SH)

        def slice_weights_tensor(pe, before_x):
            pe.wait_ge(S("logits_loaded"), 16 * 5)
            pe.wait_ge(S("zeros"), 1)
            pe.wait_ge(S("x_updates"), before_x)
            for h in range(SH):
                pe.matmul(ps[:, 0, h * SG:(h + 1) * SG], wx_h[:, h, :], ws_T, start=True, stop=True)
            for h in range(SH):
                mm = pe.matmul(ps[:, 1, h * SG:(h + 1) * SG], bx_T[:, h:h + 1].to_broadcast([NS, P]), ws_T,
                               start=True, stop=True)
            mm.then_inc(S("s_weights"), 1)
            for w in range(0, SI, 256):
                mm = pe.matmul(ps[:, 2, w:w + 256], zeros[:, 0:P], zeros[:, 0:256], start=(w == 0), stop=False,
                               skip_group_check=True)
            mm.then_inc(S("s_cleared"), 1)

        def slice_groups(eng, body):
            with eng.Fori(0, NG - 1) as g:
                body(g, False)
            body(NG - 1, True)

        def slice_tensor(pe, n):
            pe.wait_ge(S("s_logit_w"), 2)
            pe.wait_ge(S("s_cleared"), 1)

            def logits(g, i):
                on_tile(pe, g, "s_stagedT", i)
                on_tile(pe, g, "s_add", i - 2)
                pe.matmul(ps[:, i % 2, :], s_hT[:, i % 4, :], logit_w, start=True, stop=True)\
                    .then_inc(S("s_logits"), 1)

            def body(g, last):
                for i in range(4):
                    if not (last and i >= 2):
                        logits(g, i + 2)
                    on_tile(pe, g, "s_sw", i)
                    on_tile(pe, g, "s_staged", i)
                    pe.matmul(ps[:, 2, :], s_h[:, i, :], s_sw[:, i % 2, :], start=False, stop=False,
                              skip_group_check=True).then_inc(S("s_A"), 1)
                    on_tile(pe, g, "s_swT", i - 2)
                    for k in range(4):
                        mm = pe.transpose(ps[:, 3 + i % 2, k * P:(k + 1) * P], s_sw[:, i % 2, k * P:(k + 1) * P],
                                          ident[:, :])
                    mm.then_inc(S("s_turned"), 1)

            logits(0, 0)
            logits(0, 1)
            slice_groups(pe, body)
            pe.wait_ge(S("s_acc"), NT + 2)
            pe.matmul(ps[:, 5, :], ones[:, :], s_acc, start=True, stop=True).then_inc(S("s_norm"), 1)
            pe.wait_ge(S("s_AT"), 1)
            for k in range(4):
                mm = pe.matmul(ps[:, 6, k * P:(k + 1) * P], wfx_T[:, k * P:(k + 1) * P], A_T[:, k * P:(k + 1) * P],
                               start=True, stop=True)
            mm.then_inc(S("s_st"), 1)
            pe.wait_ge(S("s_stT"), 8)
            pe.wait_ge(S("s_swT"), NT + 2)
            for k in range(4):
                mm = pe.matmul(ps[0:SG, 1, 0:2 * SH], st_T[:, k, :], hy_in[:, k, SI * 2 + 2 * NS:HYP],
                               start=(k == 0), stop=(k == 3))
            mm.then_inc(S("y_dt_in"), 1)
            for q, w in HPARTS:
                c0 = SI + q * P if q < 4 else 2 * SI + (q - 4) * NS
                for k in range(4):
                    mm = pe.matmul(ps[0:w, 3, q * SG:(q + 1) * SG], hy_in[:, k, c0:c0 + w], st_T[:, k, :],
                                   start=(k == 0), stop=(k == 3))
            mm.then_inc(S("y_conv_in"), 1)
            for k in range(4):
                mm = pe.matmul(ps[0:SG, 0, :], st_T[:, k, :], hy_in[:, k, 0:SI], start=(k == 0), stop=(k == 3))
            mm.then_inc(S("y_z_in"), 1)
            pe.wait_ge(S("y_tdA"), after_mamba("y_tdA", 2))
            pe.wait_ge(S("s_loaded"), S_LOADED)
            pe.matmul(ps[0:SG, 4, :], after[0:SG, 0:SG], hy_tdA[:, 0, :], start=True, stop=True)\
                .then_inc(S("y_spans"), 1)
            pe.matmul(ps[0:SG, 5, :], before[:, :], hy_tdA[:, 1, :], start=True, stop=True).then_inc(S("y_spans"), 1)
            pe.wait_ge(S("y_conv"), after_mamba("y_conv", 2))
            pe.matmul(ps[0:SG, 2, 0:SG], hc[0:NS, 4, :], hc[0:NS, 5, :], start=True, stop=True)
            for k in range(4):
                mm = pe.matmul(ps[0:SG, 2, SG:SG + SH], hc[:, k, :], hy_fcD[:, k, :], start=(k == 0), stop=(k == 3))
            mm.then_inc(S("y_cb"), 1)
            for k in range(4):
                mm = pe.transpose(ps[0:SG, 6, k * P:(k + 1) * P], hc[:, k, :], ident[:, :])
            mm.then_inc(S("y_turned"), 1)
            pe.wait_ge(S("y_mix"), after_mamba("y_mix", 2))
            pe.wait_ge(S("y_rows"), after_mamba("y_rows", 1))
            for h in range(SH):
                mm = pe.matmul(ps[0:SG, 7, h * SG:(h + 1) * SG], hy_mix[:, h * SG:(h + 1) * SG],
                               hx_rows[:, h * SG:(h + 1) * SG], start=True, stop=True)
            mm.then_inc(S("y_y"), 1)
            pe.wait_ge(S("y_normed"), after_mamba("y_normed", 1))
            for k in range(4):
                mm = pe.transpose(ps[:, 1, k * SG:(k + 1) * SG], hy_a[:, k * P:(k + 1) * P], ident[0:SG, 0:SG])
            mm.then_inc(S("y_gT"), 1)
            pe.wait_ge(S("y_gT_w"), after_mamba("y_gT_w", 4))
            for c in range(4):
                for k in range(4):
                    mm = pe.matmul(ps[:, 3, c * SG:(c + 1) * SG], hy_out[:, k, c * P:(c + 1) * P], yg_T[:, k, :],
                                   start=(k == 0), stop=(k == 3))
            mm.then_inc(S("y_o"), 1)
            pe.wait_ge(S("y_block"), after_mamba("y_block", 3))
            for c in range(4):
                mm = pe.matmul(ps[:, 2, c * P:(c + 1) * P], block_o[:, c, :], wo_T[:, c, :], start=True, stop=True)
            mm.then_inc(S("y_q"), 1)
            pe.wait_ge(S("y_slice_w"), after_mamba("y_slice_w", 1))
            for c in range(NG):
                for i in range(4):
                    at = (4 * c + i) * P
                    for k in range(4):
                        mm = pe.matmul(ps[:, 4 + c, i * P:(i + 1) * P], sw_T[:, k, at:at + P], slice_w[:, k, :],
                                       start=(k == 0), stop=(k == 3))
                mm.then_inc(S("s_mixed"), 1)

        def slice_scalar(act, n):
            def exps(g, i):
                on_tile(act, g, "s_sub", i)
                on_tile(act, g, "s_sw", i - 2)
                act.activation(s_exp[:, i % 2, :], s_logit[:, i % 2, :], ACT.Exp).then_inc(S("s_exped"), 1)

            def stage(g, i, first):
                if not first:
                    on_tile(act, g, "s_logits", i - 4)
                    on_tile(act, g, "s_A", i - 4)
                    act.sem_inc(S("seen"), 1)
                act.copy(s_hT[:, i % 4, :], hT[:, bass.ds(g * 512 + i * P, P)]).then_inc(S("s_stagedT"), 1)
                act.copy(s_h[:, i % 4, :], h_all[:, bass.ds(g * 4 + i, 1), :]).then_inc(S("s_staged"), 1)

            hT_ready(act, n)
            act.wait_ge(S("h_rows"), NT * (n + 1))
            for i in range(4):
                stage(0, i, True)

            def body(g, last):
                for i in range(4):
                    if not (last and i == 3):
                        exps(g, i + 1)
                    on_tile(act, g, "s_turned", i)
                    act.copy(sw_T[:, :, bass.ds(g * 512 + i * P, P)],
                             ps[:, 3 + i % 2, :].rearrange("p (k n) -> p k n", k=4)).then_inc(S("s_swT"), 1)
                    if not last:
                        stage(g, i + 4, False)

            exps(0, 0)
            slice_groups(act, body)
            act.wait_ge(S("y_dt_abs"), after_mamba("y_dt_abs", 1))
            act.activation(hy_dt[:, 2, :], hy_dt[:, 1, :], ACT.Exp, scale=-1.0).then_inc(S("y_exp"), 1)
            act.wait_ge(S("y_A_min"), after_mamba("y_A_min", 1))
            act.activation(hy_small[0:SG, 1, :], hy_small[0:SG, 1, :], ACT.Exp).then_inc(S("y_exp"), 1)
            act.wait_ge(S("y_exp"), after_mamba("y_exp", 2))
            act.activation(hy_dt[:, 3, :], hy_dt[:, 2, :], ACT.Ln, bias=1.0).then_inc(S("y_ln"), 1)
            act.wait_ge(S("y_conv_in"), after_mamba("y_conv_in", 1))
            act.wait_ge(S("y_clear"), after_mamba("y_clear", 2))
            act.copy(hc_raw[:, 0:4, 2:66], ps[:, 3, 0:256].rearrange("p (q l) -> p q l", q=4)).then_inc(S("y_raw"), 1)
            act.copy(hc_raw[0:NS, 4:6, 2:66], ps[0:NS, 3, 256:384].rearrange("p (q l) -> p q l", q=2))\
                .then_inc(S("y_raw"), 1)
            act.wait_ge(S("y_tap"), after_mamba("y_tap", 18))
            act.activation(hc_tanh[:, 0:4, :], hc[:, 0:4, :], ACT.Tanh).then_inc(S("y_tanh"), 1)
            act.activation(hc_tanh[0:NS, 4:6, :], hc[0:NS, 4:6, :], ACT.Tanh).then_inc(S("y_tanh"), 1)
            act.wait_ge(S("y_z_in"), after_mamba("y_z_in", 1))
            act.activation(hz, ps[0:SG, 0, :], ACT.Tanh, scale=0.5).then_inc(S("y_z_tanh"), 1)
            for s in range(2):
                act.wait_ge(S("y_spans"), after_mamba("y_spans", s + 1))
                act.activation(hy_dec[:, s, :], ps[0:SG, 4 + s, :], ACT.Exp).then_inc(S("y_dec"), 1)
            act.wait_ge(S("y_turned"), after_mamba("y_turned", 1))
            act.copy(hx_rows, ps[0:SG, 6, :]).then_inc(S("y_rows"), 1)
            act.wait_ge(S("y_gated"), after_mamba("y_gated", 1))
            act.activation(hy_b, hy_a, ACT.Square, scale=0.5, accum_out=hy_ss[:, 0:1]).then_inc(S("y_ss"), 1)
            act.wait_ge(S("y_ss"), after_mamba("y_ss", 1))
            act.activation(hy_ss[:, 0:1], hy_ss[:, 0:1], ACT.Sqrt, scale=1.0 / SI, bias=EPS).then_inc(S("y_rms"), 1)
            act.wait_ge(S("y_q"), after_mamba("y_q", 1))
            act.copy(slice_w.rearrange("p k d -> p (k d)"), ps[:, 2, :]).then_inc(S("y_slice_w"), 1)

        def gat_pool(pool):
            pool.wait_ge(S("KF"), 2 * (VAL["L3"][1] + 1))
            pool.wait_ge(S("values_kept"), 4)
            pool.wait_ge(S("s2_rel"), 2 * (VAL["L3"][0] + 1) + 1)
            pool.tensor_copy(G[:, 1, :, D], F[:, 1, :]).then_inc(S("G_neg"), 1)
            pool.tensor_tensor(G[:, 1, :, 0:D], G[:, 1, :, 0:D], F[:, 1, :].unsqueeze(2).to_broadcast([P, NT, D]),
                               ALU.mult).then_inc(S("G_neg"), 1)

        def slice_pool(pool, n):
            with pool.Fori(0, NG) as g:
                for i in range(4):
                    b = i % 2
                    on_tile(pool, g, "s_rec", i)
                    on_tile(pool, g, "s_turned", i - 2)
                    on_tile(pool, g, "s_acc", i - 2)
                    pool.tensor_tensor(by_head(s_sw[:, b, :]), by_head(s_exp[:, b, :]), heads8(s_rec[:, b, :], P, SG),
                                       ALU.mult).then_inc(S("s_sw"), 1)
                    on_tile(pool, g, "s_sw", i)
                    on_tile(pool, g, "s_acc", i - 1)
                    pool.tensor_tensor(s_acc, s_acc, s_sw[:, b, :], ALU.add).then_inc(S("s_acc"), 1)
            pool.wait_ge(S("s_loaded"), S_LOADED)
            pool.tensor_tensor(x[:, :, :], x[:, :, :], ob_b.unsqueeze(1).to_broadcast([P, NT, D]), ALU.add)\
                .then_inc(S("s_x_bias"), 1)

        def slice_vector(dve, n):
            dve.wait_ge(S("logits_loaded"), 16 * 5)
            dve.tensor_scalar(temp_b, temp_b, 1e-6, None, ALU.max).then_inc(S("s_temp"), 1)
            dve.wait_ge(S("s_temp"), 1)
            dve.reciprocal(temp_b, temp_b).then_inc(S("s_temp"), 1)
            dve.wait_ge(S("s_weights"), 1)
            dve.wait_ge(S("s_temp"), 2)
            dve.tensor_tensor(by_head(logit_w), by_head(ps[:, 0, :]), heads8(temp_b, P, SG), ALU.mult)\
                .then_inc(S("s_logit_w"), 1)
            dve.tensor_tensor(by_head(logit_c), by_head(ps[:, 1, :]), bs_b.unsqueeze(1).to_broadcast([P, SH, SG]),
                              ALU.add).then_inc(S("s_bias_sum"), 1)
            dve.wait_ge(S("s_bias_sum"), 1)
            dve.tensor_tensor(by_head(logit_c), by_head(logit_c), heads8(temp_b, P, SG), ALU.mult)\
                .then_inc(S("s_logit_w"), 1)
            dve.memset(s_acc, 0.0).then_inc(S("s_zeroed"), 1)
            dve.memset(ones[:, :], 1.0).then_inc(S("s_zeroed"), 1)
            dve.memset(block_o[:, :, :], 0.0).then_inc(S("y_block"), 1)
            dve.memset(hc_raw[:, :, :], 0.0).then_inc(S("y_clear"), 1)
            dve.memset(hy_mix, 0.0).then_inc(S("y_clear"), 1)
            dve.wait_ge(S("s_zeroed"), 2)
            dve.wait_ge(S("s_logit_w"), 2)

            def centred(g, i):
                b = i % 2
                on_tile(dve, g, "s_logits", i)
                on_tile(dve, g, "s_exped", i - 2)
                dve.tensor_tensor(s_logit[:, b, :], ps[:, b, :], logit_c, ALU.add).then_inc(S("s_add"), 1)
                on_tile(dve, g, "s_add", i)
                on_tile(dve, g, "s_sub", i - 2)
                dve.tensor_reduce(s_max[:, b, :], by_head(s_logit[:, b, :]), AX.X, ALU.max)\
                    .then_inc(S("s_maxed"), 1)
                on_tile(dve, g, "s_maxed", i)
                dve.tensor_tensor(by_head(s_logit[:, b, :]), by_head(s_logit[:, b, :]),
                                  heads8(s_max[:, b, :], P, SG), ALU.subtract).then_inc(S("s_sub"), 1)

            def body(g, last):
                for i in range(4):
                    b = i % 2
                    if not (last and i == 3):
                        centred(g, i + 1)
                    on_tile(dve, g, "s_exped", i)
                    on_tile(dve, g, "s_rec", i - 2)
                    dve.tensor_reduce(s_sum[:, b, :], by_head(s_exp[:, b, :]), AX.X, ALU.add)\
                        .then_inc(S("s_summed"), 1)
                    on_tile(dve, g, "s_summed", i)
                    on_tile(dve, g, "s_sw", i - 2)
                    dve.reciprocal(s_rec[:, b, :], s_sum[:, b, :]).then_inc(S("s_rec"), 1)

            centred(0, 0)
            slice_groups(dve, body)
            dve.wait_ge(S("s_loaded"), S_LOADED)
            dve.tensor_scalar(hy_cw, hy_cw, 0.5, None, ALU.mult).then_inc(S("y_halved"), 1)
            dve.tensor_scalar(hy_cb, hy_cb, 0.5, None, ALU.mult).then_inc(S("y_halved"), 1)
            dve.tensor_scalar(hy_small[:, 1, :], hy_small[:, 1, :], 88.0, None, ALU.min).then_inc(S("y_A_min"), 1)
            dve.wait_ge(S("s_norm"), 1)
            dve.tensor_scalar(sn_rec, ps[:, 5, :], 1e-5, None, ALU.add).then_inc(S("s_q"), 1)
            dve.wait_ge(S("s_q"), 1)
            dve.reciprocal(sn_rec, sn_rec).then_inc(S("s_q"), 1)
            dve.wait_ge(S("s_q"), 2)
            dve.tensor_tensor(A_T, ps[:, 2, :], sn_rec, ALU.mult).then_inc(S("s_AT"), 1)
            dve.tensor_tensor(q_rows, ps[:, 5, :], sn_rec, ALU.mult).then_inc(S("s_q"), 1)
            dve.wait_ge(S("s_st"), 1)
            dve.wait_ge(S("s_q"), 3)
            for k in range(4):
                for s in range(2):
                    r = slice(s * 64, s * 64 + 64)
                    c0 = k * P + s * SG
                    dve.scalar_tensor_tensor(st_T[r, k, :], q_rows[r, c0:c0 + SG], bfx_T[r, k:k + 1],
                                             ps[r, 6, c0:c0 + SG], ALU.mult, ALU.add).then_inc(S("s_stT"), 1)
            def two(ap):
                return ap.rearrange("p (s h) -> p s h", s=2)

            dve.wait_ge(S("y_dt_in"), after_mamba("y_dt_in", 1))
            dve.tensor_tensor(two(hy_dt[:, 0, :]), two(ps[0:SG, 1, 0:2 * SH]),
                              hy_small[0:SG, 0, :].unsqueeze(1).to_broadcast([SG, 2, SH]), ALU.add)\
                .then_inc(S("y_dt"), 1)
            dve.wait_ge(S("y_dt"), after_mamba("y_dt", 1))
            dve.scalar_tensor_tensor(hy_dt[:, 1, :], hy_dt[:, 0, :], -1.0, hy_dt[:, 0, :], ALU.mult, ALU.max)\
                .then_inc(S("y_dt_abs"), 1)
            dve.wait_ge(S("y_ln"), after_mamba("y_ln", 1))
            dve.scalar_tensor_tensor(hy_dt[:, 4, :], hy_dt[:, 0, :], 0.0, hy_dt[:, 3, :], ALU.max, ALU.add)\
                .then_inc(S("y_dt"), 1)
            dve.wait_ge(S("y_dt"), after_mamba("y_dt", 2))
            dve.wait_ge(S("y_exp"), after_mamba("y_exp", 2))
            dve.scalar_tensor_tensor(two(hy_dt[:, 5, :]), two(hy_dt[:, 4, :]), -1.0,
                                     hy_small[0:SG, 1, :].unsqueeze(1).to_broadcast([SG, 2, SH]),
                                     ALU.mult, ALU.mult).then_inc(S("y_dt"), 1)
            dve.wait_ge(S("y_dt"), after_mamba("y_dt", 3))
            dve.tensor_scalar(hy_dt[:, 5, :], hy_dt[:, 5, :], -1.0e4, None, ALU.max).then_inc(S("y_dt"), 1)
            dve.wait_ge(S("y_dt"), after_mamba("y_dt", 4))
            for s, m in enumerate((tri[0:SG, 0:SG], low[:, :])):
                dve.tensor_tensor(by_head(hy_tdA[:, s, :]), m.unsqueeze(1).to_broadcast([SG, SH, SG]),
                                  heads8(hy_dt[:, 5, s * SH:(s + 1) * SH], SG, SG), ALU.mult).then_inc(S("y_tdA"), 1)
            dve.wait_ge(S("y_clear"), after_mamba("y_clear", 2))
            dve.wait_ge(S("y_halved"), after_mamba("y_halved", 2))
            for k in (2, 0, 1):
                at = {2: 0, 0: 6, 1: 12}[k]
                for q, w in HPARTS:
                    if k == 2:
                        dve.wait_ge(S("y_raw"), after_mamba("y_raw", 1 if q < 4 else 2))
                        dve.tensor_scalar(hc[0:w, q, :], hc_raw[0:w, q, 2:66], hy_cw[0:w, q, 2:3], hy_cb[0:w, q:q + 1],
                                          ALU.mult, ALU.add).then_inc(S("y_tap"), 1)
                    else:
                        dve.wait_ge(S("y_tap"), after_mamba("y_tap", at + q - 5))
                        dve.scalar_tensor_tensor(hc[0:w, q, :], hc_raw[0:w, q, k:k + 64], hy_cw[0:w, q, k:k + 1],
                                                 hc[0:w, q, :], ALU.mult, ALU.add).then_inc(S("y_tap"), 1)
            dve.wait_ge(S("y_tanh"), after_mamba("y_tanh", 1))
            dve.scalar_tensor_tensor(hc[:, 0:4, :], hc_tanh[:, 0:4, :], 1.0, hc[:, 0:4, :], ALU.add, ALU.mult)\
                .then_inc(S("y_conv"), 1)
            dve.wait_ge(S("y_tanh"), after_mamba("y_tanh", 2))
            dve.scalar_tensor_tensor(hc[0:NS, 4:6, :], hc_tanh[0:NS, 4:6, :], 1.0, hc[0:NS, 4:6, :],
                                     ALU.add, ALU.mult).then_inc(S("y_conv"), 1)
            dve.wait_ge(S("y_z_tanh"), after_mamba("y_z_tanh", 1))
            dve.scalar_tensor_tensor(hz, hz, 1.0, ps[0:SG, 0, :], ALU.add, ALU.mult).then_inc(S("y_z"), 1)
            dve.wait_ge(S("y_cb"), after_mamba("y_cb", 1))
            for s, m in enumerate((tri[0:SG, 0:SG], low[:, :])):
                dve.tensor_tensor(hy_cbm[:, s, :], ps[0:SG, 2, 0:SG], m, ALU.mult).then_inc(S("y_cbm"), 1)
            dve.tensor_tensor(hy_fD, ps[0:SG, 2, SG:SG + SH], hy_small[0:SG, 2, :], ALU.add).then_inc(S("y_fD"), 1)
            dve.wait_ge(S("y_cbm"), after_mamba("y_cbm", 2))
            for s in range(2):
                d3 = by_head(hy_dec[:, s, :])
                dve.wait_ge(S("y_dec"), after_mamba("y_dec", s + 1))
                dve.tensor_tensor(d3, d3, hy_cbm[:, s, :].unsqueeze(1).to_broadcast([SG, SH, SG]), ALU.mult)\
                    .then_inc(S("y_dec_cb"), 1)
            m3 = by_head(hy_mix)
            dve.wait_ge(S("y_dec_cb"), after_mamba("y_dec_cb", 1))
            dve.tensor_tensor(m3[:, :, 1:SG], by_head(hy_dec[:, 0, :])[:, :, 0:SG - 1],
                              heads8(hy_dt[:, 4, 0:SH], SG, SG - 1), ALU.mult).then_inc(S("y_mix"), 1)
            dve.wait_ge(S("y_dec_cb"), after_mamba("y_dec_cb", 2))
            d1 = by_head(hy_dec[:, 1, :])
            dve.tensor_tensor(d1, d1, heads8(hy_dt[:, 4, SH:2 * SH], SG, SG), ALU.mult).then_inc(S("y_dec_cb"), 1)
            dve.wait_ge(S("y_dec_cb"), after_mamba("y_dec_cb", 3))
            dve.wait_ge(S("y_mix"), after_mamba("y_mix", 1))
            dve.tensor_tensor(m3[:, :, 0:SG - 1], m3[:, :, 0:SG - 1], d1[:, :, 1:SG], ALU.add)\
                .then_inc(S("y_mix"), 1)
            dve.wait_ge(S("y_rows"), after_mamba("y_rows", 1))
            dve.wait_ge(S("y_fD"), after_mamba("y_fD", 1))
            dve.tensor_tensor(by_head(hy_b), by_head(hx_rows), heads8(hy_fD, SG, SG), ALU.mult).then_inc(S("y_t"), 1)
            dve.wait_ge(S("y_y"), after_mamba("y_y", 1))
            dve.wait_ge(S("y_t"), after_mamba("y_t", 1))
            dve.tensor_tensor(hy_b, hy_b, ps[0:SG, 7, :], ALU.add).then_inc(S("y_t"), 1)
            dve.wait_ge(S("y_t"), after_mamba("y_t", 2))
            dve.wait_ge(S("y_z"), after_mamba("y_z", 1))
            dve.tensor_tensor(hy_a, hy_b, hz, ALU.mult).then_inc(S("y_gated"), 1)
            dve.wait_ge(S("y_rms"), after_mamba("y_rms", 1))
            dve.reciprocal(hy_ss[:, 1:2], hy_ss[:, 0:1]).then_inc(S("y_t"), 1)
            dve.wait_ge(S("y_t"), after_mamba("y_t", 3))
            dve.wait_ge(S("y_gated"), after_mamba("y_gated", 1))
            dve.tensor_scalar(hy_a, hy_a, hy_ss[:, 1:2], 0.5, ALU.mult, ALU.mult).then_inc(S("y_normed"), 1)
            dve.wait_ge(S("y_gT"), after_mamba("y_gT", 1))
            for k in range(4):
                dve.tensor_scalar(yg_T[:, k, :], ps[:, 1, k * SG:(k + 1) * SG], hy_nw[:, k:k + 1], None, ALU.mult)\
                    .then_inc(S("y_gT_w"), 1)
            dve.wait_ge(S("y_o"), after_mamba("y_o", 1))
            dve.wait_ge(S("y_block"), after_mamba("y_block", 1))
            for s in range(2):
                r = slice(s * 64, s * 64 + 64)
                dve.tensor_copy(block_o[r, :, s * SG:(s + 1) * SG],
                                ps[r, 3, 0:256].rearrange("p (k g) -> p k g", k=4)).then_inc(S("y_block"), 1)
            dve.wait_ge(S("s_x_bias"), 1)
            for c in range(NG):
                dve.wait_ge(S("s_mixed"), c + 1)
                dve.tensor_tensor(x[:, 4 * c:4 * c + 4, :], x[:, 4 * c:4 * c + 4, :],
                                  ps[:, 4 + c, :].rearrange("p (i d) -> p i d", d=D), ALU.add)\
                    .then_inc(S("x_updates"), 1)

        def slice_sync(sp, before_x):
            sp.wait_ge(S("w_lo"), 4 * E)
            for dst, name in ((wx_h, "L3_wx"), (ws_T, "L3_wsT"), (bx_T, "L3_bxT")):
                sp.dma_start(dst, t[name]).then_inc(S("logits_loaded"), 16)
            for dst, name in ((bs_b, "L3_ffn_b_slice"), (temp_b, "L3_temp")):
                sp.dma_start(dst, t[name].partition_broadcast(P)).then_inc(S("logits_loaded"), 16)
            sp.wait_ge(S("x_updates"), before_x)
            for dst, name in ((wfx_T, "L3_wfxT"), (bfx_T, "L3_bfxT"), (hy_cw, "L3_cw"), (hy_cb, "L3_cb"),
                              (hy_fcD, "L3_fcDT"), (hy_nw, "L3_nwT"), (before[:, :], "before"), (low[:, :], "low"),
                              (wo_T, "L3_woT"), (hy_out, "L3_hyoutT"), (hy_in, "L3_hyinT")):
                sp.dma_start(dst, t[name]).then_inc(S("s_loaded"), 16)
            for dst, name in ((hy_small[:, 0, :], "L3_ffn_hy_dt_bias"), (hy_small[:, 1, :], "L3_ffn_hy_A_log"),
                              (hy_small[:, 2, :], "L3_ffn_hy_D"), (ob_b, "L3_ffn_out_b")):
                sp.dma_start(dst, t[name].partition_broadcast(P)).then_inc(S("s_loaded"), 16)

        NORMS = {"gnn0": 0, "moe0": 1, "gnn1": 2, "mamba": 3, "sage": 4, "moe2": 5, "gnn3": 6, "slice": 7}
        UPDATES = {"gnn0": 3, "moe0": 4, "gnn1": 3, "mamba": NT, "sage": NT, "moe2": 4, "gnn3": 6, "slice": 4}
        need = {}
        total = 16
        for s in STAGES:
            need[s] = total
            if s == "gnn3":
                pass_end["L3"] = total + 3
            total += UPDATES[s]
        x_total = total

        CREDITS = {"weights": 2, "weights_used": 2, "act_h": RING, "h_lo": RING,
                   "down": RING, "comb_b0": 16}
        CREDITS |= {name: 2 for name in CHUNKS}
        CREDITS |= {"g_x": 2}
        CREDITS |= {name: 2 for name in TILES}

        @block.gpsimd
        def _(pool):
            for name, n in CREDITS.items():
                pool.sem_inc(S(name), n)
            for s in STAGES:
                if s == "gnn3":
                    gat_pool(pool)
                if s[:3] == "moe":
                    moe_pool(pool, "L" + s[3], need[s])
                if s == "mamba":
                    add_to_rows(pool, NORMS[s], b_lin, "m_x_bias", "bias_loaded", 1)
                    mamba_pool(pool)
                if s == "slice":
                    slice_pool(pool, NORMS[s])
                if s == "sage":
                    add_to_rows(pool, NORMS[s], sage_b, "g_x_bias", "sage_loaded", 2)

        @block.sync
        def _(sp):
            sp.dma_start(x[:, :, :], t["x"].rearrange("(i p) d -> p i d", p=P)).then_inc(S("x_updates"), 16)
            sp.dma_start(ident[:, :], t["ident"]).then_inc(S("gat_loaded"), 16)
            for l, L in enumerate(("L0", "L1", "L3")):
                sp.dma_start(gat_wT[:, l, :], t[f"{L}_gnn_WT"]).then_inc(S("gat_loaded"), 16)
                sp.dma_start(gat_a[:, l, :], t[f"{L}_gnn_a"]).then_inc(S("gat_loaded"), 16)
            sp.dma_start(value_w[:, 0, 0:D], t["L0_gnn_W"]).then_inc(S("gat_loaded"), 16)
            sp.dma_start(value_w[:, 1, 0:D], t["L1_gnn_W"]).then_inc(S("gat_loaded"), 16)
            sp.dma_start(value_w[:, 2:4, 0:D], t["L3_gnn_wtrans"].rearrange("(s d) o -> d s o", d=D))\
                .then_inc(S("gat_loaded"), 16)
            adj_rows = t["adjT"].rearrange("(j p) n -> j p n", p=P)
            for b in range(2):
                sp.dma_start(adj_in[:, b, :], adj_rows[b]).then_inc(S(f"adj_landed{b}"), 16)
            sp.dma_start(first[:, :], t["first"].partition_broadcast(P)).then_inc(S("moe_loaded"), 16)
            for m, L in enumerate(("L0", "L2")):
                sp.dma_start(gate_w[:, m, :], t[f"{L}_ffn_Wg"]).then_inc(S("moe_loaded"), 16)
                sp.dma_start(gate_b[:, m, :], t[f"{L}_ffn_bg"].partition_broadcast(P)).then_inc(S("moe_loaded"), 16)
                sp.dma_start(b1_T[L][:, :], t[f"{L}_ffn_b1"]).then_inc(S("moe_loaded"), 16)
                sp.dma_start(b2[:, m, :], t[f"{L}_ffn_b2"]).then_inc(S("moe_loaded"), 16)
            with sp.Fori(1, NT // 2) as jj:
                for b in range(2):
                    sp.wait_ge(S("adjT"), jj * 2 + (b - 1))
                    sp.dma_start(adj_in[:, b, :], adj_rows[bass.ds(jj * 2 + b, 1)].rearrange("j p n -> p (j n)"))\
                        .then_inc(S(f"adj_landed{b}"), 16)
            for dst, name in ((tri, "tri"), (after, "after"), (win_x, "L1_win_x"), (win_zd, "L1_win_zd"),
                              (conv_w, "L1_conv_w"), (conv_b, "L1_conv_b"), (wout_T, "L1_wout_T"),
                              (w_lin, "L1_W_lin"), (norm_w, "L1_norm_w")):
                sp.dma_start(dst[tuple([slice(None)] * len(dst.shape))], t[name]).then_inc(S("mamba_loaded"), 16)
            sp.dma_start(small_in[:, :, :], t["L1_small"].partition_broadcast(P)).then_inc(S("mamba_loaded"), 16)
            sp.dma_start(b_lin[:, :], t["L1_b_lin"].partition_broadcast(P)).then_inc(S("bias_loaded"), 16)
            sp.dma_start(sage_w[:, :], t["L2_gnn_w"]).then_inc(S("sage_loaded"), 16)
            sp.dma_start(sage_b[:, :], t["L2_gnn_bias"].partition_broadcast(P)).then_inc(S("sage_loaded"), 16)
            for s in STAGES:
                if s == "moe0":
                    moe_sync(sp, "L0", 1)
                if s == "moe2":
                    moe_sync(sp, "L2", 5)
                if s == "slice":
                    slice_sync(sp, need[s])
            sp.wait_ge(S("moe_loaded"), 16 * 9)
            parts = NG if STAGES[-1] == "slice" else 1
            for c in range(parts):
                sp.wait_ge(S("x_updates"), x_total - parts + c + 1)
                tiles = slice(c * NT // parts, (c + 1) * NT // parts)
                sp.dma_start(outs[0].rearrange("(i p) d -> p i d", p=P)[:, tiles, :], x[:, tiles, :])\
                    .then_inc(S("stored"), 16)
            sp.wait_ge(S("stored"), 16 * parts)

        @block.vector
        def _(dve):
            for s in STAGES:
                norm_vector(dve, NORMS[s], need[s])
                if s[:3] == "gnn":
                    gat_vector(dve, "L" + s[3], NORMS[s])
                if s[:3] == "moe":
                    moe_vector(dve, "L" + s[3], NORMS[s])
                if s == "mamba":
                    mamba_vector(dve, NORMS[s])
                if s == "slice":
                    slice_vector(dve, NORMS[s])
                if s == "sage":
                    sage_vector(dve, NORMS[s])

        @block.scalar
        def _(act):
            for s in STAGES:
                norm_scalar(act, NORMS[s])
                if s[:3] == "gnn":
                    gat_scalar(act, "L" + s[3], NORMS[s])
                if s[:3] == "moe":
                    moe_scalar(act, "L" + s[3], NORMS[s])
                if s == "mamba":
                    mamba_scalar(act, NORMS[s])
                if s == "sage":
                    sage_scalar(act)
                if s == "slice":
                    slice_scalar(act, NORMS[s])

        @block.tensor
        def _(pe):
            gat_setup_tensor(pe)
            for s in STAGES:
                if s == "slice":
                    slice_weights_tensor(pe, need[s])
                norm_tensor(pe, NORMS[s])
                if s[:3] == "gnn":
                    gat_tensor(pe, "L" + s[3], NORMS[s])
                if s[:3] == "moe":
                    moe_tensor(pe, "L" + s[3], NORMS[s])
                if s == "mamba":
                    mamba_tensor(pe, NORMS[s])
                if s == "slice":
                    slice_tensor(pe, NORMS[s])
                if s == "sage":
                    sage_tensor(pe, NORMS[s])


def kernel(**inputs):
    import numpy as _np
    import concourse.bacc as _bacc
    from concourse import mybir as _mybir
    from concourse.bass_utils import run_bass_kernel_spmd as _run

    a = {k: _np.asarray(v) for k, v in inputs.items()}
    c = _np.ascontiguousarray
    arrays = {
        "x": a["x"], "adjT": c(a["adj"].T),
        "ident": _np.eye(P, dtype=_np.float32), "first": _np.arange(E, 0, -1).astype(_np.float32),
    }
    for L in ("L0", "L1", "L3"):
        arrays[f"{L}_gnn_WT"] = c(a[f"{L}_gnn_W"].T)
        arrays[f"{L}_gnn_a"] = c(a[f"{L}_gnn_a"].reshape(2, D).T)
    arrays["L0_gnn_W"], arrays["L1_gnn_W"] = a["L0_gnn_W"], a["L1_gnn_W"]
    arrays["L3_gnn_wtrans"] = a["L3_gnn_wtrans"]
    arrays["L0_ffn_Wg"], arrays["L2_ffn_Wg"] = a["L0_ffn_Wg"], c(a["L2_ffn_Wg"].T)
    arrays["L0_ffn_W1"], arrays["L2_ffn_W1"] = a["L0_ffn_W1"], c(a["L2_ffn_W1"].transpose(0, 2, 1))
    arrays["L0_ffn_W2"], arrays["L2_ffn_W2"] = a["L0_ffn_W2"], c(a["L2_ffn_W2"].transpose(0, 2, 1))
    for L in ("L0", "L2"):
        arrays[f"{L}_ffn_bg"], arrays[f"{L}_ffn_b2"] = a[f"{L}_ffn_bg"], a[f"{L}_ffn_b2"]
        arrays[f"{L}_ffn_b1"] = c(a[f"{L}_ffn_b1"].reshape(E * HC[L], P).T)
    tri = _np.triu(_np.ones((P, P), _np.float32))
    arrays["tri"], arrays["after"] = tri, _np.tril(_np.ones((P, P), _np.float32), -1)
    win = a["L1_ffn_W_in"]
    arrays["L1_win_x"] = c(win[:, DI:DI + 384])
    arrays["L1_win_zd"] = c(_np.concatenate([win[:, :DI], win[:, DI + 384:]], axis=1))
    cw, cb = _np.zeros((P, 4, 4), _np.float32), _np.zeros((P, 4), _np.float32)
    for q, c0, w in ((0, 0, P), (1, P, P), (2, 2 * P, NS), (3, 2 * P + NS, NS)):
        cw[:w, q], cb[:w, q] = a["L1_ffn_conv_w"][c0:c0 + w], a["L1_ffn_conv_b"][c0:c0 + w]
    arrays["L1_conv_w"], arrays["L1_conv_b"] = cw, cb
    arrays["L1_wout_T"] = c(a["L1_ffn_W_out"].T.reshape(P, 2, P))
    arrays["L1_W_lin"], arrays["L1_b_lin"] = a["L1_ffn_W_lin"], a["L1_ffn_b_lin"]
    arrays["L1_norm_w"] = c(a["L1_ffn_norm_w"].reshape(2, P).T)
    arrays["L1_small"] = _np.stack([a["L1_ffn_dt_bias"], a["L1_ffn_A_log"], a["L1_ffn_D"]])
    arrays["L2_gnn_w"] = c(a["L2_gnn_weight"].reshape(2, D, D).transpose(1, 0, 2).reshape(D, 2 * D))
    arrays["L2_gnn_bias"] = a["L2_gnn_bias"]
    arrays["before"] = c(_np.triu(_np.ones((SG, SG), _np.float32), 1))
    arrays["low"] = c(_np.tril(_np.ones((SG, SG), _np.float32)))
    arrays["L3_wx"] = c(a["L3_ffn_W_x"].reshape(SH, NS, D).transpose(1, 0, 2))
    arrays["L3_wsT"] = c(a["L3_ffn_W_slice"].T)
    arrays["L3_bxT"] = c(a["L3_ffn_b_x"].reshape(SH, NS).T)
    arrays["L3_wfxT"] = c(a["L3_ffn_W_fx"].T)
    arrays["L3_bfxT"] = c(a["L3_ffn_b_fx"].reshape(4, P).T)
    hw, hb = _np.zeros((P, 6, 3), _np.float32), _np.zeros((P, 6), _np.float32)
    for q in range(6):
        c0, w = (q * P, P) if q < 4 else (SI + (q - 4) * NS, NS)
        hw[:w, q], hb[:w, q] = a["L3_ffn_hy_conv_w"][c0:c0 + w], a["L3_ffn_hy_conv_b"][c0:c0 + w]
    arrays["L3_cw"], arrays["L3_cb"] = hw, hb

    def chunks(m):
        return c(m.reshape(4, P, -1).transpose(1, 0, 2))

    arrays["L3_fcDT"] = chunks(a["L3_ffn_hy_fcD_w"].T)
    arrays["L3_nwT"] = c(a["L3_ffn_hy_norm_w"].reshape(4, P).T)
    arrays["L3_hyinT"] = chunks(a["L3_ffn_hy_in_w"].T)
    arrays["L3_hyoutT"] = chunks(a["L3_ffn_hy_out_w"].T)
    arrays["L3_woT"] = chunks(a["L3_ffn_out_w"].T)
    arrays["L3_temp"] = a["L3_ffn_temperature"].reshape(SH)
    for name in ("b_slice", "hy_dt_bias", "hy_A_log", "hy_D", "out_b"):
        arrays[f"L3_ffn_{name}"] = a[f"L3_ffn_{name}"]
    nc = _bacc.Bacc("TRN2", target_bir_lowering=False, num_devices=1)
    t, ins = {}, {}
    for name, arr in arrays.items():
        ins[f"in_{name}"] = arr
        t[name] = nc.dram_tensor(f"in_{name}", arr.shape, _mybir.dt.from_np(arr.dtype), kind="ExternalInput").ap()
    outs = [nc.dram_tensor("out", (N, D), F32, kind="ExternalOutput").ap()]
    program(nc, t, outs)
    r = _run(nc, [ins], core_ids=[0])
    return r.results[0]["out"]
```
